# Optimizing a Trainium2 kernel written in Bass

```python
import numpy as np
import jax
import jax.numpy as jnp

def _softmax(x, axis=-1):
    return jax.nn.softmax(x, axis=axis)

def _gelu(x):
    return jax.nn.gelu(x, approximate=True)

def _silu(x):
    return jax.nn.silu(x)

def _sigmoid(x):
    return jax.nn.sigmoid(x)

def _layernorm(x, axis=-1, eps=1e-05):
    m = jnp.mean(x, axis=axis, keepdims=True)
    v = jnp.var(x, axis=axis, keepdims=True)
    return (x - m) / jnp.sqrt(v + eps)

def _scatter_add(tgt, idx, src, axis=0):
    return tgt.at[idx].add(src)

def _segment_sum(src, seg, n):
    return jax.ops.segment_sum(src, seg, n)
kernel_name = 'mk_seq_preln_d2_jaxref_r8_31337a'

def setup_inputs(seed: int=0):
    np.random.seed(seed)
    _w = jnp.asarray

    def _L0_attn_setup():
        import jax, jax.numpy as jnp
        import numpy as np
        EMBED_DIM = 128
        NUM_HEADS = 16
        HEAD_DIM = EMBED_DIM // NUM_HEADS

        def _kernel_exp(x):
            return jnp.exp(x - jnp.max(x, axis=-1, keepdims=True))
        key = jax.random.key(seed)
        ks = jax.random.split(key, 9)
        s = 1.0 / np.sqrt(EMBED_DIM)
        inp = {'x': jax.random.normal(ks[0], (4, 1024, EMBED_DIM), dtype=jnp.float32)}
        for i, name in enumerate(['q', 'k', 'v', 'o']):
            inp[f'W{name}'] = jax.random.uniform(ks[1 + 2 * i], (EMBED_DIM, EMBED_DIM), jnp.float32, -s, s)
            inp[f'b{name}'] = jax.random.uniform(ks[2 + 2 * i], (EMBED_DIM,), jnp.float32, -s, s)
        return inp
    _L0_attn_in = _L0_attn_setup()

    def _L0_ffn_setup():
        import jax, jax.numpy as jnp
        import numpy as np
        TOP_K = 2
        EPS = 1e-09
        key = jax.random.key(seed)
        ks = jax.random.split(key, 6)
        B, T, D, H, E = (4, 256, 128, 256, 8)
        x = jax.random.normal(ks[0], (B, T, D), dtype=jnp.float32)
        Wg = jax.random.normal(ks[1], (E, D), dtype=jnp.float32) * 0.02
        W1 = jax.random.normal(ks[2], (E, 2 * H, D), dtype=jnp.float32) * 0.02
        b1 = jax.random.normal(ks[3], (E, 2 * H), dtype=jnp.float32) * 0.02
        Wo = jax.random.normal(ks[4], (D, H), dtype=jnp.float32) * 0.02
        bo = jax.random.normal(ks[5], (D,), dtype=jnp.float32) * 0.02
        return {'x': x, 'Wg': Wg, 'W1': W1, 'b1': b1, 'Wo': Wo, 'bo': bo}
    _L0_ffn_in = _L0_ffn_setup()

    def _L1_attn_setup():
        import jax, jax.numpy as jnp
        import numpy as np
        D_MODEL = 128
        N_HEAD = 16
        D_HEAD = D_MODEL // N_HEAD
        N_CTX = 256
        ROPE_BASE = 10000.0
        SCALE = 1

        def _rope_cache(seq_len, d_head, dtype=jnp.float32):
            inv_freq = 1.0 / ROPE_BASE ** (jnp.arange(0, d_head, 2, dtype=jnp.float32) / d_head)
            t = jnp.arange(seq_len, dtype=jnp.float32)
            freqs = jnp.outer(t, inv_freq)
            emb = jnp.concatenate([freqs, freqs], -1)
            cos = jnp.cos(emb)[None, :, None, :].astype(dtype)
            sin = jnp.sin(emb)[None, :, None, :].astype(dtype)
            return (cos, sin)

        def _apply_rope(x, cos, sin):
            x_even = x[..., 0::2]
            x_odd = x[..., 1::2]
            x_rot = jnp.stack([-x_odd, x_even], axis=-1).reshape(x.shape)
            return x * cos + x_rot * sin

        def _rmsnorm(x, w):
            eps = jnp.finfo(x.dtype).eps
            var = jnp.mean(jnp.square(x), axis=-1, keepdims=True)
            return x * jax.lax.rsqrt(var + eps) * w
        key = jax.random.key(seed)
        ks = jax.random.split(key, 9)
        B, S = (2, N_CTX)
        x = jax.random.normal(ks[0], (B, S, D_MODEL), jnp.float32)
        s = 0.02
        Wq = jax.random.normal(ks[1], (D_MODEL, D_MODEL), jnp.float32) * s
        bq = jax.random.normal(ks[2], (D_MODEL,), jnp.float32) * s
        Wk = jax.random.normal(ks[3], (D_MODEL, D_MODEL), jnp.float32) * s
        bk = jax.random.normal(ks[4], (D_MODEL,), jnp.float32) * s
        Wv = jax.random.normal(ks[5], (D_MODEL, D_MODEL), jnp.float32) * s
        bv = jax.random.normal(ks[6], (D_MODEL,), jnp.float32) * s
        Wo = jax.random.normal(ks[7], (D_MODEL, D_MODEL), jnp.float32) * s
        norm_w = jnp.ones((D_HEAD,), jnp.float32)
        return {'x': x, 'Wq': Wq, 'bq': bq, 'Wk': Wk, 'bk': bk, 'Wv': Wv, 'bv': bv, 'Wo': Wo, 'norm_w': norm_w}
    _L1_attn_in = _L1_attn_setup()

    def _L1_ffn_setup():
        import jax, jax.numpy as jnp
        import numpy as np
        D_MODEL = 128
        D_FF = 512
        N_EXPERTS = 8
        TOP_K = 2

        def _ffn(x, w1, b1, w2, b2):
            h = jax.nn.gelu(x @ w1.T + b1)
            return h @ w2.T + b2
        key = jax.random.key(seed)
        ks = jax.random.split(key, 12)
        s = 0.02
        x = jax.random.normal(ks[0], (4, 256, D_MODEL), dtype=jnp.float32)
        shared_w1 = jax.random.normal(ks[1], (D_FF, D_MODEL), dtype=jnp.float32) * s
        shared_b1 = jnp.zeros((D_FF,), dtype=jnp.float32)
        shared_w2 = jax.random.normal(ks[2], (D_MODEL, D_FF), dtype=jnp.float32) * s
        shared_b2 = jnp.zeros((D_MODEL,), dtype=jnp.float32)
        router_w = jax.random.normal(ks[3], (N_EXPERTS, D_MODEL), dtype=jnp.float32) * s
        router_b = jnp.zeros((N_EXPERTS,), dtype=jnp.float32)
        spec_w1 = jax.random.normal(ks[4], (N_EXPERTS, D_FF, D_MODEL), dtype=jnp.float32) * s
        spec_b1 = jnp.zeros((N_EXPERTS, D_FF), dtype=jnp.float32)
        spec_w2 = jax.random.normal(ks[5], (N_EXPERTS, D_MODEL, D_FF), dtype=jnp.float32) * s
        spec_b2 = jnp.zeros((N_EXPERTS, D_MODEL), dtype=jnp.float32)
        return dict(x=x, shared_w1=shared_w1, shared_b1=shared_b1, shared_w2=shared_w2, shared_b2=shared_b2, router_w=router_w, router_b=router_b, spec_w1=spec_w1, spec_b1=spec_b1, spec_w2=spec_w2, spec_b2=spec_b2)
    _L1_ffn_in = _L1_ffn_setup()
    _d = {'L0_attn_x': _L0_attn_in['x'], 'L0_attn_Wq': _L0_attn_in['Wq'], 'L0_attn_bq': _L0_attn_in['bq'], 'L0_attn_Wk': _L0_attn_in['Wk'], 'L0_attn_bk': _L0_attn_in['bk'], 'L0_attn_Wv': _L0_attn_in['Wv'], 'L0_attn_bv': _L0_attn_in['bv'], 'L0_attn_Wo': _L0_attn_in['Wo'], 'L0_attn_bo': _L0_attn_in['bo'], 'L0_ffn_Wg': _L0_ffn_in['Wg'], 'L0_ffn_W1': _L0_ffn_in['W1'], 'L0_ffn_b1': _L0_ffn_in['b1'], 'L0_ffn_Wo': _L0_ffn_in['Wo'], 'L0_ffn_bo': _L0_ffn_in['bo'], 'L1_attn_Wq': _L1_attn_in['Wq'], 'L1_attn_bq': _L1_attn_in['bq'], 'L1_attn_Wk': _L1_attn_in['Wk'], 'L1_attn_bk': _L1_attn_in['bk'], 'L1_attn_Wv': _L1_attn_in['Wv'], 'L1_attn_bv': _L1_attn_in['bv'], 'L1_attn_Wo': _L1_attn_in['Wo'], 'L1_attn_norm_w': _L1_attn_in['norm_w'], 'L1_ffn_shared_w1': _L1_ffn_in['shared_w1'], 'L1_ffn_shared_b1': _L1_ffn_in['shared_b1'], 'L1_ffn_shared_w2': _L1_ffn_in['shared_w2'], 'L1_ffn_shared_b2': _L1_ffn_in['shared_b2'], 'L1_ffn_router_w': _L1_ffn_in['router_w'], 'L1_ffn_router_b': _L1_ffn_in['router_b'], 'L1_ffn_spec_w1': _L1_ffn_in['spec_w1'], 'L1_ffn_spec_b1': _L1_ffn_in['spec_b1'], 'L1_ffn_spec_w2': _L1_ffn_in['spec_w2'], 'L1_ffn_spec_b2': _L1_ffn_in['spec_b2']}
    _x0 = _d['L0_attn_x']
    _d['L0_attn_x'] = jax.random.normal(jax.random.fold_in(jax.random.key(seed), 1), (8, 1024, 128), dtype=_x0.dtype)
    del _x0
    return _d

def reference(L0_attn_x, L0_attn_Wq, L0_attn_bq, L0_attn_Wk, L0_attn_bk, L0_attn_Wv, L0_attn_bv, L0_attn_Wo, L0_attn_bo, L0_ffn_Wg, L0_ffn_W1, L0_ffn_b1, L0_ffn_Wo, L0_ffn_bo, L1_attn_Wq, L1_attn_bq, L1_attn_Wk, L1_attn_bk, L1_attn_Wv, L1_attn_bv, L1_attn_Wo, L1_attn_norm_w, L1_ffn_shared_w1, L1_ffn_shared_b1, L1_ffn_shared_w2, L1_ffn_shared_b2, L1_ffn_router_w, L1_ffn_router_b, L1_ffn_spec_w1, L1_ffn_spec_b1, L1_ffn_spec_w2, L1_ffn_spec_b2):

    def _L0_attn_ref(x, Wq, bq, Wk, bk, Wv, bv, Wo, bo):
        import jax, jax.numpy as jnp
        import numpy as np
        EMBED_DIM = 128
        NUM_HEADS = 16
        HEAD_DIM = EMBED_DIM // NUM_HEADS

        def _kernel_exp(x):
            return jnp.exp(x - jnp.max(x, axis=-1, keepdims=True))
        b, s, e = x.shape

        def proj(W, bias):
            return (x @ W.T + bias).reshape(b, s, NUM_HEADS, HEAD_DIM).transpose(0, 2, 1, 3)
        q = proj(Wq, bq)
        k = proj(Wk, bk)
        v = proj(Wv, bv)
        q_kern = _kernel_exp(q)
        k_kern = _kernel_exp(k)
        kv = jnp.einsum('bhsd,bhse->bhde', k_kern, v)
        k_sum = jnp.sum(k_kern, axis=2)
        denom = jnp.einsum('bhqd,bhd->bhq', q_kern, k_sum) + 1e-06
        y = jnp.einsum('bhqd,bhde->bhqe', q_kern, kv) / denom[..., None]
        y = y.transpose(0, 2, 1, 3).reshape(b, s, e)
        return y @ Wo.T + bo

    def _L0_ffn_ref(x, Wg, W1, b1, Wo, bo):
        import jax, jax.numpy as jnp
        import numpy as np
        TOP_K = 2
        EPS = 1e-09
        E = Wg.shape[0]
        gate_logits = jnp.einsum('btd,ed->bte', x, Wg)
        gate_scores = jax.nn.softmax(gate_logits, axis=-1)
        topk_val, topk_idx = jax.lax.top_k(gate_scores, TOP_K)
        topk_val = topk_val / (topk_val.sum(axis=-1, keepdims=True) + EPS)
        comb = (jax.nn.one_hot(topk_idx, E, dtype=x.dtype) * topk_val[..., None]).sum(axis=-2)
        out = jnp.zeros_like(x)
        for e in range(E):
            h = jnp.einsum('btd,hd->bth', x, W1[e]) + b1[e]
            a, b = jnp.split(h, 2, axis=-1)
            g = a * jax.nn.sigmoid(b)
            eo = jnp.einsum('bth,dh->btd', g, Wo) + bo
            out = out + eo * comb[..., e:e + 1]
        return out

    def _L1_attn_ref(x, Wq, bq, Wk, bk, Wv, bv, Wo, norm_w):
        import jax, jax.numpy as jnp
        import numpy as np
        D_MODEL = 128
        N_HEAD = 16
        D_HEAD = D_MODEL // N_HEAD
        N_CTX = 256
        ROPE_BASE = 10000.0
        SCALE = 1

        def _rope_cache(seq_len, d_head, dtype=jnp.float32):
            inv_freq = 1.0 / ROPE_BASE ** (jnp.arange(0, d_head, 2, dtype=jnp.float32) / d_head)
            t = jnp.arange(seq_len, dtype=jnp.float32)
            freqs = jnp.outer(t, inv_freq)
            emb = jnp.concatenate([freqs, freqs], -1)
            cos = jnp.cos(emb)[None, :, None, :].astype(dtype)
            sin = jnp.sin(emb)[None, :, None, :].astype(dtype)
            return (cos, sin)

        def _apply_rope(x, cos, sin):
            x_even = x[..., 0::2]
            x_odd = x[..., 1::2]
            x_rot = jnp.stack([-x_odd, x_even], axis=-1).reshape(x.shape)
            return x * cos + x_rot * sin

        def _rmsnorm(x, w):
            eps = jnp.finfo(x.dtype).eps
            var = jnp.mean(jnp.square(x), axis=-1, keepdims=True)
            return x * jax.lax.rsqrt(var + eps) * w
        B, S, _ = x.shape
        split = lambda t: t.reshape(B, S, N_HEAD, D_HEAD)
        q = split(x @ Wq.T + bq)
        k = split(x @ Wk.T + bk)
        v = split(x @ Wv.T + bv)
        cos, sin = _rope_cache(S, D_HEAD, x.dtype)
        q = _apply_rope(_rmsnorm(q, norm_w), cos, sin)
        k = _apply_rope(_rmsnorm(k, norm_w), cos, sin)
        scores = jnp.einsum('bqhd,bkhd->bhqk', q, k)
        causal = jnp.tril(jnp.ones((S, S), x.dtype))
        pattern = jnp.square(scores / D_HEAD) * causal
        z = jnp.einsum('bhqk,bkhd->bqhd', pattern, v).reshape(B, S, D_MODEL)
        return x + z @ Wo.T * SCALE

    def _L1_ffn_ref(x, shared_w1, shared_b1, shared_w2, shared_b2, router_w, router_b, spec_w1, spec_b1, spec_w2, spec_b2):
        import jax, jax.numpy as jnp
        import numpy as np
        D_MODEL = 128
        D_FF = 512
        N_EXPERTS = 8
        TOP_K = 2

        def _ffn(x, w1, b1, w2, b2):
            h = jax.nn.gelu(x @ w1.T + b1)
            return h @ w2.T + b2
        B, T, D = x.shape
        xf = x.reshape(-1, D)
        U = xf.shape[0]
        logits = xf @ router_w.T + router_b
        routing = jax.nn.softmax(logits, axis=-1)
        sel_w, sel_idx = jax.lax.top_k(routing, TOP_K)
        sel_w = sel_w / sel_w.sum(axis=-1, keepdims=True)
        comb = jnp.zeros_like(routing).at[jnp.arange(U)[:, None], sel_idx].set(sel_w)
        shared_out = _ffn(xf, shared_w1, shared_b1, shared_w2, shared_b2)

        def body(acc, params):
            w1, b1, w2, b2, we = params
            return (acc + we[:, None] * _ffn(xf, w1, b1, w2, b2), None)
        acc0 = jnp.zeros_like(shared_out)
        acc, _ = jax.lax.scan(body, acc0, (spec_w1, spec_b1, spec_w2, spec_b2, comb.T))
        return (shared_out + acc).reshape(B, T, D)
    x = L0_attn_x
    x = x + _L0_attn_ref(_layernorm(x, axis=-1), L0_attn_Wq, L0_attn_bq, L0_attn_Wk, L0_attn_bk, L0_attn_Wv, L0_attn_bv, L0_attn_Wo, L0_attn_bo)
    x = x + _L0_ffn_ref(_layernorm(x, axis=-1), L0_ffn_Wg, L0_ffn_W1, L0_ffn_b1, L0_ffn_Wo, L0_ffn_bo)
    x = x + _L1_attn_ref(_layernorm(x, axis=-1), L1_attn_Wq, L1_attn_bq, L1_attn_Wk, L1_attn_bk, L1_attn_Wv, L1_attn_bv, L1_attn_Wo, L1_attn_norm_w)
    x = x + _L1_ffn_ref(_layernorm(x, axis=-1), L1_ffn_shared_w1, L1_ffn_shared_b1, L1_ffn_shared_w2, L1_ffn_shared_b2, L1_ffn_router_w, L1_ffn_router_b, L1_ffn_spec_w1, L1_ffn_spec_b1, L1_ffn_spec_w2, L1_ffn_spec_b2)
    return x

_drawn_inputs = setup_inputs


def setup_inputs(seed=0):
    import zlib

    import numpy as np

    out = dict(_drawn_inputs(seed))
    spreads = {'L1_attn_norm_w': (1.0, 0.2),
     'L1_ffn_shared_b1': (0.0, 0.719),
     'L1_ffn_shared_b2': (0.0, 0.1),
     'L1_ffn_router_b': (0.0, 0.293),
     'L1_ffn_spec_b1': (0.0, 0.8),
     'L1_ffn_spec_b2': (0.0, 0.1)}
    factors = {'L0_attn_Wq': 8.0,
     'L0_attn_bq': 29.663,
     'L0_attn_Wk': 7.189,
     'L0_attn_bk': 30.372,
     'L0_ffn_b1': 8.0,
     'L1_ffn_spec_w1': 3.227,
     'L1_ffn_spec_w2': 2.913}
    for name, (base, spread) in spreads.items():
        noise = np.random.default_rng([zlib.crc32(name.encode()), seed]).standard_normal(out[name].shape)
        drawn = base * np.exp(spread * noise) if base else spread * noise
        out[name] = jnp.asarray(drawn.astype(out[name].dtype))
    for name, factor in factors.items():
        out[name] = (out[name] * factor).astype(out[name].dtype)
    return out
```

```python
from contextlib import ExitStack

import concourse.bass as bass
from concourse import mybir
from concourse.alu_op_type import AluOpType as ALU

P = 128
D = 128
SEQS, SEQ = 8, 1024
TOKENS = SEQS * SEQ
T = SEQ // P
H, DH = 16, 8
E = 8
FF = 512
ROWS = 256
UNROLL = 4
REGION = TOKENS + ROWS
ROUTED = 2 * TOKENS // ROWS + E
SHARED = TOKENS // ROWS
DUMMY = E * REGION
X1_SHARED = DUMMY + ROWS
Y_SHARED = ROUTED * ROWS
NDIFF = 5

C_IDENT, C_BLOCK, C_PREFIX, C_STATE = 0, 128, 256, 384
C_SHIFT = C_STATE + NDIFF * 128
C_HEAD = C_SHIFT + 4 * 128
C_RANK = C_HEAD + H
C_BASE = C_RANK + E
C_COS = C_BASE + E
C_SIN = C_COS + T * DH
C_JOB = C_SIN + T * DH
JOBS = (ROUTED, ROUTED + SHARED)
NC_COLS = C_JOB + ROUTED

R_QKV0, R_O0, R_QKV1, R_GATE = 0, 384, 512, 896
NR_COLS = R_GATE + E
EPS = 1e-5


def program(nc, x_in, consts, bias_row, w_attn0, w_attn1, w_gate, w_out0, w_exp0, w_exp1, b_out0, b_out1,
            norm_w, out, xs, ys):
    fp32, bf16, i32 = mybir.dt.float32, mybir.dt.bfloat16, mybir.dt.int32
    f32r = mybir.dt.float32r
    ACT, AX = mybir.ActivationFunctionType, mybir.AxisListType

    def at(i, n):
        return slice(i, i + n) if isinstance(i, int) else bass.DynSlice(i, n)

    with ExitStack() as ctx:
        def sb(name, shape, dt=fp32):
            return ctx.enter_context(nc.sbuf_tensor(name, shape, dt))

        def sem(name):
            return ctx.enter_context(nc.semaphore(name))

        X = sb("X", [P, SEQS * T, D])
        K = sb("K", [P, NC_COLS])
        WA = [sb(f"WA{n}", [P, 4 * D]) for n in range(2)]
        WG = [sb(f"WG{n}", [P, E]) for n in range(2)]
        brow = sb("brow", [3, NR_COLS], bf16)
        ones3 = sb("ones3", [3, P], bf16)
        prefix16 = sb("prefix16", [P, P], bf16)
        ones16 = sb("ones16", [P, P], bf16)
        gains = sb("gains", [P, T * SEQS, 2])
        places = sb("places", [P, T * SEQS, 2])
        carry = [sb(f"carry{n}", [P, E]) for n in range(2)]
        table = [sb(f"table{n}", [1, 2, JOBS[n]], i32) for n in range(2)]
        padrow = [sb(f"padrow{n}", [1, E], i32) for n in range(2)]
        zeros = sb("zeros", [P, ROWS // P, D])
        ropeC = sb("ropeC", [P, T, DH])
        ropeS = sb("ropeS", [P, T, DH])
        wn = sb("wn", [P, DH])
        ident = K[:, C_IDENT:C_IDENT + P]
        block = K[:, C_BLOCK:C_BLOCK + P]

        xn = sb("xn", [P, T, D])
        xnT = sb("xnT", [P, T * P])
        qk = sb("qk", [P, T, 2 * D])
        val = sb("val", [P, T, D + 1])
        qT = sb("qT", [P, T * P])
        y = sb("y", [P, T, D])
        xn2 = sb("xn2", [P, T, D])
        kvm = sb("kvm", [P, D + H])
        stats = sb("stats", [P, T, 6])
        mv = sb("mv", [P, T, 2])
        rs = sb("rs", [P, 3, T])
        rsh = sb("rsh", [P, 3, T * 2 * H])
        mx = sb("mx", [P, 2 * H])
        den = sb("den", [P, 2, H])
        lg = sb("lg", [P, 6, T, E])
        lr = sb("lr", [P, 8, T])
        mask16 = sb("mask16", [P, T, E], bf16)
        idx = sb("idx", [P, T, 2], i32)
        got = sb("got", [P, T, 2, D])
        t2 = sb("t2", [P, T, 2 * D])
        prods = sb("prods", [P, NDIFF, T, D])
        ksum = sb("ksum", [P, T * H])
        split = sb("split", [P, 2, 4, 4, 4, DH], f32r)
        splitT = sb("splitT", [P, 8, P], f32r)
        feats = sb("feats", [P, NDIFF, P])
        state = sb("state", [P, NDIFF, P])
        score = sb("score", [P, 4, 4, P])
        vpad = sb("vpad", [P, H, 32])
        zT = sb("zT", [P, P])
        WT = [sb(f"WT{m}", [P, 2 * FF + 4]) for m in range(UNROLL)]
        BT = [sb(f"BT{m}", [P, D]) for m in range(UNROLL)]
        XT = [sb(f"XT{u}", [P, ROWS // P, D]) for u in range(2)]
        XTT = [sb(f"XTT{u}", [P, ROWS]) for u in range(2)]
        HT = [sb(f"HT{u}", [P, 4, ROWS]) for u in range(2)]
        SG = [sb(f"SG{u}", [P, 2, ROWS]) for u in range(2)]
        YT = [sb(f"YT{u}", [P, ROWS // P, D]) for u in range(2)]

        banks = [ctx.enter_context(nc.psum_tensor(f"bank{n}", [P, 512], fp32)) for n in range(8)]

        S = {}

        def s(name):
            if name not in S:
                S[name] = sem(name)
            return S[name]

        for name in ("const_in rope_in w_in bias_in bias_split bias_rows setup_done zeroed "
                     "a0_x a0_ln1 a0_t1 a0_xT a0_qkv a0_qsub a0_v a0_exp a0_t2 a0_qT a0_kv a0_kvm "
                     "a0_num a0_y a0_t3 a0_yT a0_o a0_x1 a0_ln2 a0_t4 a0_x2T a0_gate a0_gcopy a0_dmax "
                     "a0_p a0_mask a0_pre a0_idx a0_scat "
                     "a1_idx a1_got a1_comb a1_ln1 a1_t1 a1_xT a1_qkv a1_qv a1_sq a1_t2 a1_rope a1_prod "
                     "a1_split a1_splitT_ps a1_splitTa a1_splitTb a1_plain a1_qT a1_ph a1_feat a1_f0 a1_qk a1_sqr a1_mask "
                     "a1_vpad a1_z a1_zT a1_st a1_state a1_o a1_x1 a1_ln2 a1_t4 a1_x2T a1_gate a1_gcopy a1_dmax "
                     "a1_p a1_mask2 a1_pre a1_idx2 a1_scat a1_nat "
                     "c_idx c_got c_sh c_out c_store").split():
            s(name)
        for n in range(2):
            for name in "table pads".split():
                s(f"{name}{n}")
            for name in "x xt xT h sig act y ysb st".split():
                for u in range(2):
                    s(f"b{n}_{name}{u}")
            for m in range(UNROLL):
                s(f"b{n}_w{m}")
        words = [sb(f"word{n}", [1, 2]) for n in range(2)]
        block_ = ctx.enter_context(nc.Block())

        def rsqrt(v, work, n):
            r, a, t = work[:, 0, 0:n], work[:, 1, 0:n], work[:, 2, 0:n]
            v.tensor_scalar(r.bitcast(i32), a.bitcast(i32), 1, None, ALU.logical_shift_right)
            v.drain()
            v.tensor_scalar(r.bitcast(i32), r.bitcast(i32), -1.0, float(0x5F3759DF), ALU.mult, ALU.add)
            for _ in range(3):
                v.drain()
                v.scalar_tensor_tensor(t, r, -0.5, r, ALU.mult, ALU.mult)
                v.drain()
                v.tensor_tensor(t, t, a, ALU.mult)
                v.drain()
                v.scalar_tensor_tensor(r, t, 1.5, r, ALU.add, ALU.mult)
            v.drain()

        def wait_apart(eng, signal, value):
            eng.drain()
            eng.wait_ge(signal, value)
            word = words[eng is not nc.vector]
            eng.tensor_tensor(word[:, 1:2], word[:, 0:1], word[:, 0:1], ALU.add)

        def every_group(eng, jobs, run):
            run(0, True, False)
            with eng.Fori(1, jobs // UNROLL - 1) as i:
                run(i, False, False)
            run(jobs // UNROLL - 1, False, True)

        def each_sequence(eng, run):
            run(0)
            with eng.Fori(1, SEQS) as i:
                run(i)

        def use(i, m):
            return 2 * i + m // 2

        def after(i, m):
            return (i, m + 1) if m + 1 < UNROLL else (i + 1, 0)

        def before(i, m):
            return (i, m - 1) if m > 0 else (i - 1, UNROLL - 1)

        def wait_earlier(eng, signal, value):
            if not isinstance(value, int) or value > 0:
                eng.wait_ge(signal, value)

        def layernorm(v, first, dst, done):
            for t in range(T):
                v.bn_stats(stats[:, t, :], X[:, at(first + t, 1), :].rearrange("p a d -> p (a d)"))
            v.drain()
            for t in range(T):
                v.bn_aggr(mv[:, t, :], stats[:, t, :])
            v.drain()
            v.tensor_scalar(rs[:, 1, :], mv[:, :, 1], EPS, None, ALU.add)
            v.drain()
            rsqrt(v, rs, T)
            for t in range(T):
                last = v.tensor_scalar(dst[:, t, :], X[:, at(first + t, 1), :].rearrange("p a d -> p (a d)"),
                                       mv[:, t, 0:1], rs[:, 0, t:t + 1], ALU.subtract, ALU.mult)
            last.then_inc(done, 1)

        def spread(a):
            return a.unsqueeze(2).broadcast_to([P, T, E])

        rank = K[:, C_RANK:C_RANK + E].unsqueeze(1).broadcast_to([P, T, E])

        def first_of(v, flags, hot):
            v.tensor_reduce(lr[:, 3, :], flags, AX.X, ALU.max)
            v.drain()
            v.tensor_tensor(hot, rank, spread(lr[:, 3, :]), ALU.is_equal)
            v.drain()

        def routing(v, n, i, gates, names):
            gcopy, dmax, p_ready, mask, pre, idx_ready = (s(f"a{n}_{k}") for k in names)
            prob, hot1, hot2, pos, tmp = (lg[:, k] for k in range(5))
            v.wait_ge(s(f"a{n}_gate"), i + 1)
            v.tensor_reduce(lr[:, 0, :], gates, AX.X, ALU.max)
            v.drain()
            v.tensor_tensor(tmp, gates, spread(lr[:, 0, :]), ALU.subtract).then_inc(dmax, 1)
            v.wait_ge(p_ready, i + 1)
            v.tensor_reduce(lr[:, 1, :], prob, AX.X, ALU.add)
            v.scalar_tensor_tensor(tmp, prob, 1.0, rank, ALU.is_equal, ALU.mult)
            v.drain()
            first_of(v, tmp, hot1)
            v.scalar_tensor_tensor(pos, hot1, -2.0, prob, ALU.mult, ALU.add)
            v.drain()
            v.tensor_reduce(lr[:, 2, :], pos, AX.X, ALU.max)
            v.drain()
            v.tensor_tensor(tmp, pos, spread(lr[:, 2, :]), ALU.is_equal)
            v.drain()
            v.tensor_tensor(tmp, tmp, rank, ALU.mult)
            v.drain()
            first_of(v, tmp, hot2)
            v.tensor_tensor(mask16[:, :, :], hot1, hot2, ALU.add).then_inc(mask, 1)
            v.tensor_scalar(lr[:, 4, :], lr[:, 2, :], 1.0, None, ALU.add)
            v.drain()
            if n == 0:
                v.scalar_tensor_tensor(lr[:, 5, :], lr[:, 1, :], 1e-9, lr[:, 4, :], ALU.mult, ALU.add)
            else:
                v.tensor_copy(lr[:, 5, :], lr[:, 4, :])
            v.drain()
            v.reciprocal(lr[:, 6, :], lr[:, 5, :])
            v.drain()
            v.tensor_copy(gains[:, at(T * i, T), 0], lr[:, 6, :])
            v.tensor_tensor(gains[:, at(T * i, T), 1], lr[:, 6, :], lr[:, 2, :], ALU.mult)
            v.wait_ge(pre, i + 1)
            v.tensor_tensor(pos, banks[7][:, 256:256 + T * E].rearrange("p (t e) -> p t e", e=E),
                            carry[n][:, :].unsqueeze(1).broadcast_to([P, T, E]), ALU.add)
            v.drain()
            v.tensor_tensor(carry[n][:, :], carry[n][:, :], banks[7][:, 320:320 + E], ALU.add)
            v.tensor_tensor(hot1, hot1, pos, ALU.mult)
            v.tensor_tensor(hot2, hot2, pos, ALU.mult)
            v.drain()
            v.tensor_reduce(lr[:, 4, :], hot1, AX.X, ALU.add)
            v.tensor_reduce(lr[:, 5, :], hot2, AX.X, ALU.add)
            v.drain()
            if not (isinstance(i, int) and i == 0):
                v.wait_ge(s(f"a{n}_scat"), 16 * 2 * T * i)
            v.tensor_copy(idx[:, :, 0], lr[:, 4, :])
            v.tensor_copy(idx[:, :, 1], lr[:, 5, :])
            v.drain()
            v.tensor_copy(places[:, at(T * i, T), :], idx[:, :, :]).then_inc(idx_ready, 1)

        def make_table(v, n):
            cnt, til, cum, gap = (lr[:, k, :] for k in range(4))
            whole = lr[:, 4, :].bitcast(i32)
            jobs = K[0:1, C_JOB:C_JOB + ROUTED]
            v.drain()
            v.tensor_tensor(cnt, carry[n][:, :], K[:, C_BASE:C_BASE + E], ALU.subtract)
            v.drain()
            v.tensor_scalar(whole, cnt, ROWS - 1.0, None, ALU.add)
            v.drain()
            v.tensor_scalar(whole, whole, ROWS.bit_length() - 1, None, ALU.logical_shift_right)
            v.drain()
            v.tensor_copy(til, whole)
            v.drain()
            v.tensor_tensor_scan(cum, ones8[:, :], til, 0.0, ALU.mult, ALU.add)
            v.tensor_scalar(gap, til, -float(ROWS), float(REGION), ALU.mult, ALU.add)
            v.tensor_copy(padrow[n][:, :], carry[n][0:1, :])
            v.drain()
            v.tensor_tensor(lg2[:, :, :], jobs.unsqueeze(2).broadcast_to([1, ROUTED, E]),
                            cum[0:1, :].unsqueeze(1).broadcast_to([1, ROUTED, E]), ALU.is_ge)
            v.drain()
            v.tensor_reduce(jw[:, 0, :], lg2[:, :, :], AX.X, ALU.add)
            v.drain()
            v.tensor_tensor(lg2[:, :, :], lg2[:, :, :], gap[0:1, :].unsqueeze(1).broadcast_to([1, ROUTED, E]),
                            ALU.mult)
            v.drain()
            v.tensor_reduce(jw[:, 1, :], lg2[:, :, :], AX.X, ALU.add)
            v.drain()
            v.scalar_tensor_tensor(jw[:, 2, :], jobs, float(ROWS), jw[:, 1, :], ALU.mult, ALU.add)
            v.drain()
            v.tensor_scalar(table[n][:, 0, 0:ROUTED], jw[:, 2, :], float(DUMMY), None, ALU.min)
            last = v.tensor_scalar(table[n][:, 1, 0:ROUTED], jw[:, 0, :], float(E - 1), None, ALU.min)
            if n == 1:
                sh = K[0:1, C_JOB:C_JOB + SHARED]
                v.tensor_scalar(table[1][:, 0, ROUTED:], sh, float(ROWS), float(X1_SHARED), ALU.mult, ALU.add)
                last = v.tensor_scalar(table[1][:, 1, ROUTED:], sh, 0.0, float(E), ALU.mult, ALU.add)
            last.then_inc(s(f"table{n}"), 1)
            flat_places = places[:, :, :].rearrange("p t c -> p (t c)")
            shifts = got[:, 0:E, 0, :]
            for e in range(1, E):
                v.tensor_scalar(shifts[:, e, :], flat_places, float(e * REGION), gap[:, e - 1:e], ALU.is_ge,
                                ALU.mult)
            for e in range(1, E):
                v.drain()
                v.tensor_tensor(flat_places, flat_places, shifts[:, e, :], ALU.subtract)
            v.drain()

        gcur = sb("gcur", [P, T, 2])
        WA2 = sb("WA2", [P, 2, D])

        lg2 = sb("lg2", [1, ROUTED, E])
        jw = sb("jw", [1, 3, ROUTED])
        ones8 = sb("ones8", [P, E])
        tiles = range(T)

        def flat(a):
            return a.rearrange("p a d -> p (a d)")

        @block_.sync
        def _(sp):
            sp.dma_start(K[:, :], consts).then_inc(s("const_in"), 16)
            sp.dma_start(WA[0][:, :], w_attn0).then_inc(s("w_in"), 16)
            sp.dma_start(WA[1][:, :], w_attn1).then_inc(s("w_in"), 16)
            for n in range(2):
                sp.dma_start(WG[n][:, :], w_gate[n]).then_inc(s("w_in"), 16)
            sp.dma_start(WA2[:, :, :], w_out0.rearrange("(c p) d -> p c d", p=P)).then_inc(s("w_in"), 16)
            sp.dma_start(BT[0][:, :], b_out0.partition_broadcast(P)).then_inc(s("w_in"), 16)
            sp.dma_start(wn[:, :], norm_w.partition_broadcast(P)).then_inc(s("rope_in"), 16)
            sp.dma_start(qk[0:1, 0:4, :].rearrange("p a d -> p (a d)")[:, 0:NR_COLS], bias_row)\
                .then_inc(s("bias_in"), 16)
            sp.wait_ge(s("bias_split"), 1)
            parts = got[0:1, :, :, :].rearrange("p a c d -> p (a c d)").bitcast(bf16)
            for r in range(3):
                sp.dma_start(brow[r:r + 1, :], parts[:, r * NR_COLS:(r + 1) * NR_COLS])\
                    .then_inc(s("bias_rows"), 16)
            for b in range(SEQS):
                sp.dma_start(X[:, T * b:T * (b + 1), :], x_in[b * SEQ:(b + 1) * SEQ, :]
                             .rearrange("(t p) d -> p t d", p=P)).then_inc(s("a0_x"), 16)
                sp.wait_ge(s("a0_x"), 16 * (b + 1))
            for n in range(2):
                if n == 1:
                    def sequence(i):
                        sp.wait_ge(s("a1_ln2"), i + 1)
                        sp.dma_start(xs[1][at(X1_SHARED + SEQ * i, SEQ), :].rearrange("(t p) d -> p t d", p=P),
                                     xn2[:, :, :]).then_inc(s("a1_nat"), 16)
                    each_sequence(sp, sequence)
                sp.wait_ge(s(f"table{n}"), 1)
                sp.wait_ge(s("zeroed"), 1)
                for e in range(E):
                    row = sp.value_load(padrow[n][0:1, e:e + 1], min_val=0, max_val=DUMMY - ROWS)
                    sp.dma_start(xs[n][at(row, ROWS), :].rearrange("(a p) d -> p a d", p=P), zeros[:, :, :])\
                        .then_inc(s(f"pads{n}"), 16)
                sp.dma_start(xs[n][DUMMY:DUMMY + ROWS, :].rearrange("(a p) d -> p a d", p=P), zeros[:, :, :])\
                    .then_inc(s(f"pads{n}"), 16)
                sp.wait_ge(s(f"pads{n}"), 16 * (E + 1))
                sp.wait_ge(s(f"a{n}_scat"), 16 * 2 * T * SEQS)
                if n == 1:
                    sp.wait_ge(s("a1_nat"), 16 * SEQS)
                width = (FF + 4, 2 * FF + 4)[n]

                def load(i, m):
                    k, u = use(i, m), m % 2
                    e = sp.value_load(table[n][0:1, 1, at(UNROLL * i + m, 1)], min_val=0, max_val=E - 1 + n)
                    row = sp.value_load(table[n][0:1, 0, at(UNROLL * i + m, 1)], min_val=0,
                                        max_val=(DUMMY, X1_SHARED + TOKENS - ROWS)[n])
                    wait_earlier(sp, s(f"b{n}_xt{u}"), k)
                    sp.dma_start(XT[u][:, :, :], xs[n][at(row, ROWS), :].rearrange("(a p) d -> p a d", p=P))\
                        .then_inc(s(f"b{n}_x{u}"), 16)
                    wait_earlier(sp, s(f"b{n}_ysb{u}"), k - 1)
                    sp.dma_start(WT[m][:, 0:width], (w_exp0, w_exp1)[n][at(e, 1), :, :].rearrange("a p f -> p (a f)"))\
                        .then_inc(s(f"b{n}_w{m}"), 16)
                    if n == 1:
                        sp.dma_start(BT[m][:, :], b_out1[at(e, 1), :].rearrange("a d -> (a d)").partition_broadcast(P))\
                            .then_inc(s(f"b{n}_w{m}"), 16)

                def load_group(i, first, last):
                    for m in range(UNROLL):
                        load(i, m)

                every_group(sp, JOBS[n], load_group)
            for u in range(2):
                sp.wait_ge(s(f"b1_st{u}"), 16 * (JOBS[1] // 2))
            def sequence(i):
                wait_earlier(sp, s("c_out"), i)
                sp.dma_start(y[:, :, :], ys[1][at(Y_SHARED + SEQ * i, SEQ), :].rearrange("(t p) d -> p t d", p=P))\
                    .then_inc(s("c_sh"), 16)
                sp.wait_ge(s("c_out"), i + 1)
                sp.dma_start(out[at(SEQ * i, SEQ), :].rearrange("(t p) d -> p t d", p=P), X[:, at(T * i, T), :])\
                    .then_inc(s("c_store"), 16)
            each_sequence(sp, sequence)
            sp.wait_ge(s("c_store"), 16 * SEQS)

        @block_.gpsimd
        def _(g):
            g.memset(vpad[:, :, :], 0.0)
            g.memset(words[1][:, :], 0.0)
            g.memset(zeros[:, :, :], 0.0).then_inc(s("zeroed"), 1)

            def scatter(n, i, ready):
                wait_apart(g, ready, i + 1)
                for t in tiles:
                    for c in range(2):
                        g.indirect_dma_start(xs[n], bass.IndirectOffsetOnAxis(idx[:, t, c:c + 1], 0),
                                             xn2[:, t, :], None).then_inc(s(f"a{n}_scat"), 16)

            def gather(n, i, ready, done):
                wait_apart(g, ready, i + 1)
                for t in tiles:
                    for c in range(2):
                        g.indirect_dma_start(got[:, t, c, :], None, ys[n],
                                             bass.IndirectOffsetOnAxis(idx[:, t, c:c + 1], 0)).then_inc(done, 16)

            def store_all(n):
                def store_group(i, first, last):
                    for m in range(UNROLL):
                        k, u = use(i, m), m % 2
                        g.wait_ge(s(f"b{n}_ysb{u}"), k + 1)
                        g.dma_start(ys[n][at(ROWS * (UNROLL * i + m), ROWS), :].rearrange("(a p) d -> p a d", p=P), YT[u][:, :, :])\
                            .then_inc(s(f"b{n}_st{u}"), 16)

                every_group(g, JOBS[n], store_group)
                for u in range(2):
                    g.wait_ge(s(f"b{n}_st{u}"), 16 * (JOBS[n] // 2))

            def sequence(i):
                scatter(0, i, s("a0_idx"))
            each_sequence(g, sequence)
            store_all(0)
            def sequence(i):
                gather(0, i, s("a1_idx"), s("a1_got"))
                for t in tiles:
                    wait_apart(g, s("a1_sqr"), T * i + t + 1)
                    g.affine_select(out=score[:, :, :, :].rearrange("p a b c -> p (a b) c"),
                                    in_=score[:, :, :, :].rearrange("p a b c -> p (a b) c"),
                                    compare_op=ALU.is_ge, fill=0.0, base=0, pattern=[[0, H], [1, P]],
                                    channel_multiplier=-1).then_inc(s("a1_mask"), 1)
                scatter(1, i, s("a1_idx2"))
            each_sequence(g, sequence)
            store_all(1)
            def sequence(i):
                gather(1, i, s("c_idx"), s("c_got"))

            each_sequence(g, sequence)
        @block_.scalar
        def _(a):
            def experts(n):
                def xt(i, m):
                    k, u = use(i, m), m % 2
                    a.wait_ge(s(f"b{n}_xt{u}"), k + 1)
                    a.activation(XTT[u][:, :], banks[u][:, 0:ROWS], ACT.Copy).then_inc(s(f"b{n}_xT{u}"), 1)

                def act_group(i, first, last):
                    if first:
                        xt(0, 0)
                    for m in range(UNROLL):
                        k, u = use(i, m), m % 2
                        if not (last and m == UNROLL - 1):
                            xt(*after(i, m))
                        for half in range(2):
                            hp = banks[2 + 2 * u + half][:, :].rearrange("p (c r) -> p c r", r=ROWS)
                            if n == 0 and half == 0:
                                continue
                            a.wait_ge(s(f"b{n}_h{u}"), 2 * k + half + 1)
                            if n == 0:
                                wait_earlier(a, s(f"b{n}_act{u}"), k)
                            elif half == 0:
                                wait_earlier(a, s(f"b{n}_y{u}"), k)
                            for c in range(2):
                                cc = 2 * half + c
                                bias = WT[m][:, FF + cc:FF + cc + 1]
                                if n == 0:
                                    last_ = a.activation(SG[u][:, c, :], hp[:, c, :], ACT.Sigmoid, bias=bias)
                                else:
                                    last_ = a.activation(HT[u][:, cc, :], hp[:, c, :], ACT.Gelu_apprx_tanh, bias=bias)
                            last_.then_inc(s(f"b{n}_{'sig' if n == 0 else 'act'}{u}"), 1)

                every_group(a, JOBS[n], act_group)

            def evac_pair(src, dst, wait, i, done, per=2):
                for half in range(2):
                    a.wait_ge(wait, per * i + half + 1)
                    a.activation(dst[:, 512 * half:512 * (half + 1)], banks[src + half][:, :], ACT.Copy)\
                        .then_inc(done, 1)

            def sequence(i):
                evac_pair(0, xnT, s("a0_t1"), i, s("a0_xT"))
                for t in tiles:
                    a.wait_ge(s("a0_qsub"), T * i + t + 1)
                    a.activation(val[:, t, 0:D], banks[2 + t % 2][:, 2 * D:3 * D], ACT.Copy).then_inc(s("a0_v"), 1)
                for half in range(2):
                    a.wait_ge(s("a0_qsub"), T * i + 4 * half + 4)
                    a.activation(qk[:, 4 * half:4 * half + 4, :], qk[:, 4 * half:4 * half + 4, :], ACT.Exp)\
                        .then_inc(s("a0_exp"), 1)
                evac_pair(0, qT, s("a0_t2"), i, s("a0_qT"))
                evac_pair(0, qT, s("a0_t3"), i, s("a0_yT"))
                evac_pair(0, xnT, s("a0_t4"), i, s("a0_x2T"))
                a.wait_ge(s("a0_dmax"), i + 1)
                a.activation(lg[:, 0], lg[:, 4], ACT.Exp).then_inc(s("a0_p"), 1)
            each_sequence(a, sequence)
            experts(0)
            def sequence(i):
                evac_pair(4, xnT, s("a1_t1"), i, s("a1_xT"))
                for t in tiles:
                    a.wait_ge(s("a1_qkv"), T * i + t + 1)
                    a.activation(qk[:, t, :], banks[4 + t % 2][:, 0:2 * D], ACT.Copy)
                    a.activation(val[:, t, 0:D], banks[4 + t % 2][:, 2 * D:3 * D], ACT.Copy).then_inc(s("a1_qv"), 1)
                a.drain()
                a.activation(t2[:, :, :], qk[:, :, :], ACT.Square).then_inc(s("a1_sq"), 1)
                for t in tiles:
                    k = T * i + t
                    a.wait_ge(s("a1_plain"), k + 1)
                    a.activation(qT[:, 0:P], banks[5][:, 0:P], ACT.Copy)
                    a.activation(feats[:, 0, :], banks[5][:, 0:P], ACT.Square).then_inc(s("a1_qT"), 1)
                    a.wait_ge(s("a1_splitT_ps"), 2 * k + 1)
                    a.activation(splitT[:, 0:4, :].rearrange("p a b -> p (a b)"), banks[4][:, :], ACT.Copy)\
                        .then_inc(s("a1_splitTa"), 1)
                    a.wait_ge(s("a1_ph"), k + 1)
                    a.activation(feats[:, 1:NDIFF, :].rearrange("p a b -> p (a b)"), banks[4][:, :], ACT.Square)\
                        .then_inc(s("a1_feat"), 1)
                    a.wait_ge(s("a1_qk"), k + 1)
                    for hh in range(4):
                        last = a.activation(score[:, hh, :, :].rearrange("p g c -> p (g c)"), banks[hh][:, :],
                                            ACT.Square, scale=1.0 / DH)
                    last.then_inc(s("a1_sqr"), 1)
                    a.wait_ge(s("a1_z"), k + 1)
                    a.activation(zT[:, :], banks[6][:, 0:P], ACT.Copy).then_inc(s("a1_zT"), 1)
                evac_pair(4, xnT, s("a1_t4"), i, s("a1_x2T"))
                a.wait_ge(s("a1_dmax"), i + 1)
                a.activation(lg[:, 0], lg[:, 4], ACT.Exp).then_inc(s("a1_p"), 1)
            each_sequence(a, sequence)
            experts(1)

        @block_.vector
        def _(v):
            v.wait_ge(s("bias_in"), 16)
            raw = qk[0:1, 0:4, :].rearrange("p a d -> p (a d)")[:, 0:NR_COLS]
            parts = got[0:1, :, :, :].rearrange("p a c d -> p (a c d)").bitcast(bf16)
            rest = qk[0:1, 4:8, :].rearrange("p a d -> p (a d)")[:, 0:NR_COLS]
            for r in range(3):
                part = parts[:, r * NR_COLS:(r + 1) * NR_COLS]
                last = v.tensor_copy(part, raw if r == 0 else rest)
                if r < 2:
                    v.drain()
                    v.tensor_tensor(rest, raw if r == 0 else rest, part, ALU.subtract)
                    v.drain()
            last.then_inc(s("bias_split"), 1)
            v.memset(ones3[:, :], 1.0)
            v.memset(words[0][:, :], 0.0)
            v.memset(ones16[:, :], 1.0)
            v.memset(val[:, :, D:D + 1], 1.0)
            v.memset(ones8[:, :], 1.0)
            v.wait_ge(s("const_in"), 16)
            for n in range(2):
                v.tensor_copy(carry[n][:, :], K[:, C_BASE:C_BASE + E])
            v.tensor_copy(prefix16[:, :], K[:, C_PREFIX:C_PREFIX + P]).then_inc(s("setup_done"), 1)
            v.wait_ge(s("rope_in"), 16)
            v.wait_ge(s("w_in"), 16 * 6)
            v.tensor_tensor(ropeC[:, :, :], K[:, C_COS:C_COS + T * DH].rearrange("p (t d) -> p t d", d=DH),
                            wn[:, :].unsqueeze(1).broadcast_to([P, T, DH]), ALU.mult)
            sin = K[:, C_SIN:C_SIN + T * DH].rearrange("p (t j c) -> p t j c", j=4, c=2)
            ws = wn[:, :].rearrange("p (j c) -> p j c", c=2)
            rS = ropeS[:, :, :].rearrange("p t (j c) -> p t j c", c=2)
            for c in range(2):
                v.tensor_tensor(rS[:, :, :, c], sin[:, :, :, c],
                                ws[:, :, 1 - c].unsqueeze(1).broadcast_to([P, T, 4]), ALU.mult)
            v.wait_ge(s("bias_rows"), 48)
            v.wait_ge(s("zeroed"), 1)
            heads = "p (h d) -> p h d"
            def sequence(i):
                wait_apart(v, s("a0_x"), 16 * i + 16)
                layernorm(v, T * i, xn, s("a0_ln1"))
                for t in tiles:
                    v.wait_ge(s("a0_qkv"), T * i + t + 1)
                    src = banks[2 + t % 2][:, 0:2 * D].rearrange(heads, d=DH)
                    v.tensor_reduce(mx[:, :], src, AX.X, ALU.max)
                    v.drain()
                    v.tensor_tensor(qk[:, t, :].rearrange(heads, d=DH), src,
                                    mx[:, :].unsqueeze(2).broadcast_to([P, 2 * H, DH]), ALU.subtract)\
                        .then_inc(s("a0_qsub"), 1)
                    v.drain()
                v.wait_ge(s("a0_kv"), i + 1)
                v.tensor_tensor(kvm[:, 0:D], banks[4][:, 0:D], block, ALU.mult)
                v.tensor_scalar(kvm[:, D:D + H], K[:, C_HEAD:C_HEAD + H], banks[4][:, D:D + 1], None, ALU.mult)\
                    .then_inc(s("a0_kvm"), 1)
                for t2_ in range(T // 2):
                    v.wait_ge(s("a0_num"), (T // 2) * i + t2_ + 1)
                    yb = banks[5 + t2_ % 2][:, :].rearrange("p (a c) -> p a c", a=2)
                    v.tensor_scalar(den[:, :, :], yb[:, :, D:D + H], 1e-6, None, ALU.add)
                    v.drain()
                    v.reciprocal(den[:, :, :], den[:, :, :])
                    v.drain()
                    v.tensor_tensor(y[:, 2 * t2_:2 * t2_ + 2, :].rearrange("p a (h d) -> p a h d", d=DH),
                                    yb[:, :, 0:D].rearrange("p a (h d) -> p a h d", d=DH),
                                    den[:, :, :].unsqueeze(3).broadcast_to([P, 2, H, DH]), ALU.mult)\
                        .then_inc(s("a0_y"), 1)
                    v.drain()
                for half in range(2):
                    v.wait_ge(s("a0_o"), 2 * i + half + 1)
                    rows = X[:, at(T * i + 4 * half, 4), :]
                    last = v.tensor_tensor(rows, rows, banks[2 + half][:, :].rearrange("p (a d) -> p a d", a=4),
                                           ALU.add)
                last.then_inc(s("a0_x1"), 1)
                v.drain()
                if not isinstance(i, int) or i > 0:
                    wait_apart(v, s("a0_scat"), 16 * 2 * T * i)
                layernorm(v, T * i, xn2, s("a0_ln2"))
                routing(v, 0, i, banks[7][:, 0:T * E].rearrange("p (t e) -> p t e", e=E),
                        ("gcopy", "dmax", "p", "mask", "pre", "idx"))
                v.drain()
            each_sequence(v, sequence)

            def combine(i, ready, done=None):
                v.wait_ge(ready, 16 * 2 * T * (i + 1))
                for c in range(2):
                    for t in tiles:
                        row = X[:, at(T * i + t, 1), :].rearrange("p a d -> p (a d)")
                        last = v.scalar_tensor_tensor(row, got[:, t, c, :], gcur[:, t, c:c + 1], row,
                                                      ALU.mult, ALU.add)
                    if c == 0:
                        v.drain()
                if done is not None:
                    last.then_inc(done, 1)
                v.drain()

            def fetch_places(i, ready):
                v.tensor_copy(idx[:, :, :], places[:, at(T * i, T), :]).then_inc(ready, 1)
                v.tensor_copy(gcur[:, :, :], gains[:, at(T * i, T), :])
                v.drain()

            def experts(n):
                def finish(i, m):
                    k, u = use(i, m), m % 2
                    v.wait_ge(s(f"b{n}_y{u}"), k + 1)
                    wait_earlier(v, s(f"b{n}_st{u}"), 16 * k)
                    bt = BT[0] if n == 0 else BT[m]
                    v.tensor_tensor(YT[u][:, :, :], banks[6 + u][:, 0:ROWS].rearrange("p (a d) -> p a d", d=D),
                                    bt[:, :].unsqueeze(1).broadcast_to([P, ROWS // P, D]), ALU.add)\
                        .then_inc(s(f"b{n}_ysb{u}"), 1)

                def gate(i, m):
                    k, u = use(i, m), m % 2
                    v.wait_ge(s(f"b{n}_sig{u}"), k + 1)
                    wait_earlier(v, s(f"b{n}_y{u}"), k)
                    hp = banks[2 + 2 * u][:, :].rearrange("p (c r) -> p c r", r=ROWS)
                    for c in range(2):
                        last = v.scalar_tensor_tensor(HT[u][:, c, :], hp[:, c, :], WT[m][:, FF + c:FF + c + 1],
                                                      SG[u][:, c, :], ALU.add, ALU.mult)
                    last.then_inc(s(f"b{n}_act{u}"), 1)

                def dve_group(i, first, last):
                    for m in range(UNROLL):
                        if n == 0:
                            gate(i, m)
                        if not (first and m == 0):
                            finish(*before(i, m))
                    if last:
                        finish(i, UNROLL - 1)

                every_group(v, JOBS[n], dve_group)

            v.wait_ge(s("a0_scat"), 16 * 2 * T * SEQS)
            make_table(v, 0)
            experts(0)
            v.drain()
            def sequence(i):
                wait_earlier(v, s("a1_scat"), 16 * 2 * T * i)
                fetch_places(i, s("a1_idx"))
                combine(i, s("a1_got"))
                layernorm(v, T * i, xn, s("a1_ln1"))
                v.drain()
                xseq = X[:, at(T * i, T), :]
                v.tensor_tensor(xseq, xseq, xn[:, :, :], ALU.add)
                v.wait_ge(s("a1_sq"), i + 1)
                v.tensor_reduce(rsh[:, 2, :], t2[:, :, :].rearrange("p t (h d) -> p (t h) d", d=DH), AX.X, ALU.add)
                v.drain()
                v.tensor_scalar(rsh[:, 1, :], rsh[:, 2, :], 1.0 / DH, 2.0 ** -23, ALU.mult, ALU.add)
                v.drain()
                rsqrt(v, rsh, T * 2 * H)
                qk3 = qk[:, :, :].rearrange("p t (h d) -> p (t h) d", d=DH)
                v.tensor_tensor(qk3, qk3, rsh[:, 0, :].unsqueeze(2).broadcast_to([P, T * 2 * H, DH]), ALU.mult)
                v.drain()
                for t in tiles:
                    qh = qk[:, t, :].rearrange("p (h j c) -> p h j c", j=4, c=2)
                    th = t2[:, t, :].rearrange("p (h j c) -> p h j c", j=4, c=2)
                    for c in range(2):
                        v.tensor_tensor(th[:, :, :, c], qh[:, :, :, 1 - c],
                                        ropeS[:, t, :].rearrange("p (j c) -> p j c", c=2)[:, :, c]
                                        .unsqueeze(1).broadcast_to([P, 2 * H, 4]), ALU.mult)
                v.drain()
                for t in tiles:
                    q_ = qk[:, t, :].rearrange(heads, d=DH)
                    v.tensor_tensor(q_, q_, ropeC[:, t, :].unsqueeze(1).broadcast_to([P, 2 * H, DH]), ALU.mult)
                v.drain()
                v.tensor_tensor(qk[:, :, :], qk[:, :, :], t2[:, :, :], ALU.add).then_inc(s("a1_rope"), 1)
                v.drain()
                k_ = qk[:, :, D:2 * D].rearrange("p t (h d) -> p t h d", d=DH)
                v.tensor_reduce(ksum[:, :].rearrange("p (t h) -> p t h", h=H), k_, AX.X, ALU.add)
                v.drain()
                for t in tiles:
                    kt = qk[:, t, D:2 * D].rearrange(heads, d=DH)
                    v.scalar_tensor_tensor(prods[:, 0, t, :].rearrange(heads, d=DH), kt, 2.0,
                                           ksum[:, t * H:(t + 1) * H].unsqueeze(2).broadcast_to([P, H, DH]),
                                           ALU.mult, ALU.subtract)
                v.drain()
                v.tensor_tensor(prods[:, 0, :, :], prods[:, 0, :, :], qk[:, :, D:2 * D], ALU.mult)
                for d in range(1, NDIFF):
                    pd = prods[:, d, :, :].rearrange("p t (h d) -> p t h d", d=DH)
                    v.tensor_tensor(pd[:, :, :, 0:DH - d], k_[:, :, :, 0:DH - d], k_[:, :, :, d:DH], ALU.mult)
                    last = v.tensor_tensor(pd[:, :, :, DH - d:DH], k_[:, :, :, DH - d:DH], k_[:, :, :, 0:d], ALU.mult)
                last.then_inc(s("a1_prod"), 1)
                for t in tiles:
                    k = T * i + t
                    if t > 0:
                        v.wait_ge(s("a1_splitT_ps"), 2 * k)
                    q1 = qk[:, t, 0:D].rearrange("p (g h d) -> p g h d", g=4, d=DH)
                    k1 = qk[:, t, D:2 * D].rearrange("p (g h d) -> p g h d", g=4, d=DH)
                    for c in range(2):
                        v.tensor_copy(split[:, 0, :, :, 2 * c, :], q1)
                        v.tensor_copy(split[:, 1, :, :, c, :], k1)
                    v.drain()
                    for c in range(2):
                        v.tensor_tensor(split[:, 0, :, :, 2 * c + 1, :], q1, split[:, 0, :, :, 0, :], ALU.subtract)
                        last = v.tensor_tensor(split[:, 1, :, :, 2 + c, :], k1, split[:, 1, :, :, 0, :], ALU.subtract)
                    last.then_inc(s("a1_split"), 1)
                    if t > 0:
                        v.wait_ge(s("a1_z"), k)
                    for hh in range(4):
                        last = v.tensor_copy(vpad[:, :, :].rearrange("p (g h) e -> p g h e", h=4)
                                             [:, :, hh, DH * hh:DH * (hh + 1)],
                                             val[:, t, 0:D].rearrange("p (g h e) -> p g h e", g=4, h=4)[:, :, hh, :])
                    last.then_inc(s("a1_vpad"), 1)
                    v.wait_ge(s("a1_splitT_ps"), 2 * k + 2)
                    v.tensor_copy(splitT[:, 4:8, :].rearrange("p a b -> p (a b)"), banks[5][:, :])\
                        .then_inc(s("a1_splitTb"), 1)
                    if t < T - 1:
                        v.wait_ge(s("a1_st"), (T - 1) * i + t + 1)
                        v.wait_ge(s("a1_z"), k + 1)
                        v.tensor_tensor(state[:, :, :].rearrange("p d (g c) -> p d g c", c=32),
                                        banks[7][:, 0:NDIFF * 32].rearrange("p (d c) -> p d c", c=32)
                                        .unsqueeze(2).broadcast_to([P, NDIFF, 4, 32]),
                                        K[:, C_STATE:C_STATE + NDIFF * P]
                                        .rearrange("p (d g c) -> p d g c", g=4, c=32), ALU.mult)\
                            .then_inc(s("a1_state"), 1)
                    v.wait_ge(s("a1_o"), k + 1)
                    row = flat(X[:, at(k, 1), :])
                    v.tensor_tensor(row, row, banks[6][:, P:2 * P], ALU.add)\
                        .then_inc(s("a1_x1"), 1)
                v.drain()
                if not isinstance(i, int) or i > 0:
                    wait_apart(v, s("a1_nat"), 16 * i)
                layernorm(v, T * i, xn2, s("a1_ln2"))
                routing(v, 1, i, banks[6][:, 384:384 + T * E].rearrange("p (t e) -> p t e", e=E),
                        ("gcopy", "dmax", "p", "mask2", "pre", "idx2"))
                v.drain()
            each_sequence(v, sequence)
            v.wait_ge(s("a1_scat"), 16 * 2 * T * SEQS)
            make_table(v, 1)
            experts(1)
            v.drain()
            def sequence(i):
                wait_earlier(v, s("c_got"), 16 * 2 * T * i)
                fetch_places(i, s("c_idx"))
                v.wait_ge(s("c_sh"), 16 * (i + 1))
                rows = X[:, at(T * i, T), :]
                v.tensor_tensor(rows, rows, y[:, :, :], ALU.add)
                v.drain()
                combine(i, s("c_got"), s("c_out"))

            each_sequence(v, sequence)
        @block_.tensor
        def _(pe):
            def transposes(src, bank0, i, ready, done):
                pe.wait_ge(ready, i + 1)
                for half in range(2):
                    for t in range(4):
                        last = pe.transpose(banks[bank0 + half][:, P * t:P * (t + 1)], src(4 * half + t), ident)
                    last.then_inc(done, 1)

            def biased(dst, lhsT, rhs, col, n):
                pe.matmul(dst, ones3[:, :], brow[:, col:col + n], start=True, stop=False)
                return pe.matmul(dst, lhsT, rhs, start=False, stop=True)

            def routing_sums(n, i, mask, pre, i0):
                pe.wait_ge(mask, i + 1)
                pos = banks[7][:, 256:256 + T * E].rearrange("p (t e) -> p t e", e=E)
                for t in tiles:
                    pe.matmul(pos[:, t, :], prefix16[:, :], mask16[:, t, :], start=(t == 0), stop=False,
                              skip_group_check=True)
                for t in range(T - 1):
                    pe.matmul(pos[:, t + 1:T, :], ones16[:, :],
                              mask16[:, t, :].unsqueeze(1).broadcast_to([P, T - 1 - t, E]),
                              start=False, stop=(t == T - 2), skip_group_check=True)
                for t in tiles:
                    last = pe.matmul(banks[7][:, 320:320 + E], ones16[:, :], mask16[:, t, :],
                                     start=(t == 0), stop=(t == T - 1), skip_group_check=True)
                last.then_inc(pre, 1)

            def experts(n):
                def flip(i, m):
                    k, u = use(i, m), m % 2
                    pe.wait_ge(s(f"b{n}_x{u}"), 16 * (k + 1))
                    wait_earlier(pe, s(f"b{n}_xT{u}"), k)
                    for a_ in range(ROWS // P):
                        last = pe.transpose(banks[u][:, P * a_:P * (a_ + 1)], XT[u][:, a_, :], ident)
                    last.then_inc(s(f"b{n}_xt{u}"), 1)

                def up(i, m):
                    k, u = use(i, m), m % 2
                    pe.wait_ge(s(f"b{n}_xT{u}"), k + 1)
                    pe.wait_ge(s(f"b{n}_w{m}"), 16 * (1 + n) * (i + 1))
                    wait_earlier(pe, s(f"b{n}_act{u}"), k * (1 + n))
                    for half in range(2):
                        hp = banks[2 + 2 * u + half][:, :].rearrange("p (c r) -> p c r", r=ROWS)
                        for c in range(2):
                            cc = 2 * half + c
                            last = pe.matmul(hp[:, c, :], WT[m][:, P * cc:P * (cc + 1)], XTT[u][:, :],
                                             start=True, stop=True)
                        last.then_inc(s(f"b{n}_h{u}"), 1)

                def down(i, m):
                    k, u = use(i, m), m % 2
                    pe.wait_ge(s(f"b{n}_act{u}"), (k + 1) * (1 + n))
                    wait_earlier(pe, s(f"b{n}_ysb{u}"), k)
                    chunks = (2, 4)[n]
                    for a_ in range(ROWS // P):
                        for c in range(chunks):
                            rhs = WA2[:, c, :] if n == 0 else WT[m][:, FF + 4 + P * c:FF + 4 + P * (c + 1)]
                            last = pe.matmul(banks[6 + u][:, D * a_:D * (a_ + 1)],
                                             HT[u][:, c, P * a_:P * (a_ + 1)], rhs,
                                             start=(c == 0), stop=(c == chunks - 1))
                    last.then_inc(s(f"b{n}_y{u}"), 1)

                def pe_group(i, first, last):
                    if first:
                        flip(0, 0)
                    for m in range(UNROLL):
                        if not (last and m == UNROLL - 1):
                            flip(*after(i, m))
                        up(i, m)
                        if not (first and m == 0):
                            down(*before(i, m))
                    if last:
                        down(i, UNROLL - 1)

                every_group(pe, JOBS[n], pe_group)

            pe.wait_ge(s("const_in"), 16)
            pe.wait_ge(s("w_in"), 16 * 6)
            pe.wait_ge(s("bias_rows"), 48)
            pe.wait_ge(s("setup_done"), 1)
            def sequence(i):
                wait_earlier(pe, s("a0_qT"), 2 * i)
                wait_earlier(pe, s("a0_x2T"), 2 * i)
                transposes(lambda t: xn[:, t, :], 0, i, s("a0_ln1"), s("a0_t1"))
                pe.wait_ge(s("a0_xT"), 2 * i + 2)
                wait_earlier(pe, s("a0_x1"), i)
                for t in tiles:
                    if t >= 2:
                        pe.wait_ge(s("a0_qsub"), T * i + t - 1)
                        pe.wait_ge(s("a0_v"), T * i + t - 1)
                    biased(banks[2 + t % 2][:, 0:3 * D], xnT[:, P * t:P * (t + 1)], WA[0][:, 0:3 * D],
                           R_QKV0, 3 * D).then_inc(s("a0_qkv"), 1)
                pe.wait_ge(s("a0_exp"), 2 * i + 2)
                pe.wait_ge(s("a0_v"), T * i + T)
                for t in tiles:
                    last = pe.matmul(banks[4][:, 0:D + 1], qk[:, t, D:2 * D], val[:, t, :],
                                     start=(t == 0), stop=(t == T - 1))
                last.then_inc(s("a0_kv"), 1)
                transposes(lambda t: qk[:, t, 0:D], 0, 2 * i + 1, s("a0_exp"), s("a0_t2"))
                pe.wait_ge(s("a0_kvm"), i + 1)
                pe.wait_ge(s("a0_qT"), 2 * i + 2)
                for c in range(T // 2):
                    if c >= 2:
                        pe.wait_ge(s("a0_y"), (T // 2) * i + c - 1)
                    for t in range(2):
                        last = pe.matmul(banks[5 + c % 2][:, 256 * t:256 * t + D + H],
                                         qT[:, P * (2 * c + t):P * (2 * c + t + 1)], kvm[:, :], start=True, stop=True)
                    last.then_inc(s("a0_num"), 1)
                transposes(lambda t: y[:, t, :], 0, (T // 2) * i + T // 2 - 1, s("a0_y"), s("a0_t3"))
                pe.wait_ge(s("a0_yT"), 2 * i + 2)
                for half in range(2):
                    for t in range(4):
                        k = 4 * half + t
                        last = biased(banks[2 + half][:, D * t:D * (t + 1)], qT[:, P * k:P * (k + 1)],
                                      WA[0][:, 3 * D:4 * D], R_O0, D)
                    last.then_inc(s("a0_o"), 1)
                transposes(lambda t: xn2[:, t, :], 0, i, s("a0_ln2"), s("a0_t4"))
                pe.wait_ge(s("a0_x2T"), 2 * i + 2)
                for t in tiles:
                    last = pe.matmul(banks[7][:, E * t:E * (t + 1)], xnT[:, P * t:P * (t + 1)], WG[0][:, :],
                                     start=True, stop=True)
                last.then_inc(s("a0_gate"), 1)
                routing_sums(0, i, s("a0_mask"), s("a0_pre"), 0)
            each_sequence(pe, sequence)
            experts(0)
            def sequence(i):
                transposes(lambda t: xn[:, t, :], 4, i, s("a1_ln1"), s("a1_t1"))
                pe.wait_ge(s("a1_xT"), 2 * i + 2)
                for t in tiles:
                    if t >= 2:
                        pe.wait_ge(s("a1_qv"), T * i + t - 1)
                    biased(banks[4 + t % 2][:, 0:3 * D], xnT[:, P * t:P * (t + 1)], WA[1][:, 0:3 * D],
                           R_QKV1, 3 * D).then_inc(s("a1_qkv"), 1)
                pe.wait_ge(s("a1_qv"), T * i + T)
                pe.wait_ge(s("a1_rope"), i + 1)
                for t in tiles:
                    k = T * i + t
                    pe.transpose(banks[5][:, 0:P], qk[:, t, 0:D], ident).then_inc(s("a1_plain"), 1)
                    pe.wait_ge(s("a1_split"), k + 1)
                    for side in range(2):
                        if side == 1:
                            pe.wait_ge(s("a1_qT"), k + 1)
                        for g in range(4):
                            last = pe.transpose(banks[4 + side][:, P * g:P * (g + 1)],
                                                split[:, side, g, :, :, :].rearrange("p h c d -> p (h c d)").bitcast(fp32),
                                                ident)
                        last.then_inc(s("a1_splitT_ps"), 1)
                    pe.wait_ge(s("a1_splitTa"), k + 1)
                    for d in range(1, NDIFF):
                        last = pe.matmul(banks[4][:, P * (d - 1):P * d],
                                         K[:, C_SHIFT + P * (d - 1):C_SHIFT + P * d], qT[:, 0:P], start=True, stop=True)
                    last.then_inc(s("a1_ph"), 1)
                    pe.wait_ge(s("a1_splitTb"), k + 1)
                    for g in range(4):
                        for hh in range(4):
                            last = pe.matmul(banks[hh][:, P * g:P * (g + 1)],
                                             splitT[32 * hh:32 * hh + 32, 4 + g, :],
                                             splitT[32 * hh:32 * hh + 32, g, :], start=True, stop=True)
                    last.then_inc(s("a1_qk"), 1)
                    if t < T - 1:
                        pe.wait_ge(s("a1_prod"), i + 1)
                        if t > 0:
                            pe.wait_ge(s("a1_state"), (T - 1) * i + t)
                        for d in range(NDIFF):
                            for g in range(4):
                                last = pe.matmul(banks[7][32 * g:32 * g + 32, 32 * d:32 * d + 32],
                                                 prods[:, d, t, 32 * g:32 * g + 32], val[:, t, 32 * g:32 * g + 32],
                                                 start=(t == 0 and d == 0), stop=True, skip_group_check=True)
                        last.then_inc(s("a1_st"), 1)
                    pe.wait_ge(s("a1_feat"), k + 1)
                    wait_earlier(pe, s("a1_x1"), k)
                    if t > 0:
                        pe.wait_ge(s("a1_state"), (T - 1) * i + t)
                        for d in range(NDIFF):
                            pe.matmul(banks[6][:, 0:P], state[:, d, :], feats[:, d, :], start=(d == 0), stop=False,
                                      skip_group_check=True)
                    pe.wait_ge(s("a1_mask"), k + 1)
                    pe.wait_ge(s("a1_vpad"), k + 1)
                    for hh in range(4):
                        for g in range(4):
                            last = pe.matmul(banks[6][32 * g:32 * g + 32, 0:P], vpad[:, 4 * g + hh, :],
                                             score[:, hh, g, :], start=(t == 0 and hh == 0), stop=(hh == 3),
                                             skip_group_check=True)
                    last.then_inc(s("a1_z"), 1)
                    pe.wait_ge(s("a1_zT"), k + 1)
                    pe.matmul(banks[6][:, P:2 * P], zT[:, :], WA[1][:, 3 * D:4 * D], start=True, stop=True)\
                        .then_inc(s("a1_o"), 1)
                transposes(lambda t: xn2[:, t, :], 4, i, s("a1_ln2"), s("a1_t4"))
                pe.wait_ge(s("a1_x2T"), 2 * i + 2)
                for t in tiles:
                    last = biased(banks[6][:, 384 + E * t:384 + E * (t + 1)], xnT[:, P * t:P * (t + 1)], WG[1][:, :],
                                  R_GATE, E)
                last.then_inc(s("a1_gate"), 1)
                routing_sums(1, i, s("a1_mask2"), s("a1_pre"), 0)
            each_sequence(pe, sequence)
            experts(1)


def constants():
    import numpy as np
    f = np.float32
    p = np.arange(P)
    same = (p[:, None] // DH == p[None, :] // DH).astype(f)
    eye = np.eye(P, dtype=f)
    state = [same / DH ** 2] * (NDIFF - 1) + [same / (2 * DH ** 2)]
    head = p // DH * DH
    shift = [eye + (p[:, None] == (head + (p + d) % DH)[None, :]) for d in range(1, NDIFF)]
    inv = f(1.0) / f(10000.0) ** (np.arange(0, DH, 2, dtype=f) / f(DH))
    angle = np.outer(np.arange(SEQ, dtype=f), inv).astype(f)
    angle = np.concatenate([angle, angle], -1).reshape(T, P, DH).transpose(1, 0, 2)
    sign = np.where(np.arange(DH) % 2 == 0, -1.0, 1.0).astype(f)

    def rows(a):
        return np.broadcast_to(np.asarray(a, f), (P, len(a)))

    parts = [eye, same, (p[:, None] < p[None, :]).astype(f), *state, *shift,
             (p[:, None] // DH == np.arange(H)[None, :]).astype(f),
             rows(E - np.arange(E)), rows(np.arange(E) * REGION),
             np.cos(angle).reshape(P, T * DH), (np.sin(angle) * sign).reshape(P, T * DH),
             rows(np.arange(ROUTED))]
    return np.ascontiguousarray(np.concatenate(parts, 1), dtype=f)


def kernel(**inputs):
    import numpy as np
    import concourse.bacc as bacc
    from concourse.bass_utils import run_bass_kernel_spmd

    w = {k: np.asarray(v) for k, v in inputs.items()}
    cat = np.concatenate

    def attn(layer):
        return cat([w[f"L{layer}_attn_W{m}"].T for m in "qkvo"], 1)

    def columns(b):
        return b.reshape(-1, FF // P, P).transpose(0, 2, 1)

    w1 = cat([w["L1_ffn_spec_w1"], w["L1_ffn_shared_w1"][None]])
    b1 = cat([w["L1_ffn_spec_b1"], w["L1_ffn_shared_b1"][None]])
    w2 = cat([w["L1_ffn_spec_w2"], w["L1_ffn_shared_w2"][None]])
    laid = {
        "x_in": w["L0_attn_x"].reshape(TOKENS, D),
        "consts": constants(),
        "bias_row": cat([w["L0_attn_bq"], w["L0_attn_bk"], w["L0_attn_bv"], w["L0_attn_bo"],
                         w["L1_attn_bq"], w["L1_attn_bk"], w["L1_attn_bv"], w["L1_ffn_router_b"]])[None],
        "w_attn0": attn(0),
        "w_attn1": attn(1),
        "w_gate": np.stack([w["L0_ffn_Wg"].T, w["L1_ffn_router_w"].T]),
        "w_out0": w["L0_ffn_Wo"].T,
        "w_exp0": cat([w["L0_ffn_W1"].transpose(0, 2, 1), columns(w["L0_ffn_b1"])], 2),
        "w_exp1": cat([w1.transpose(0, 2, 1), columns(b1),
                       w2.reshape(E + 1, D, FF // P, P).transpose(0, 3, 2, 1).reshape(E + 1, P, FF)], 2),
        "b_out0": w["L0_ffn_bo"],
        "b_out1": cat([w["L1_ffn_spec_b2"], w["L1_ffn_shared_b2"][None]]),
        "norm_w": w["L1_attn_norm_w"],
    }
    nc = bacc.Bacc("TRN2", target_bir_lowering=False, num_devices=1)
    arrays, args = {}, []
    for name, a in laid.items():
        arrays[name] = np.ascontiguousarray(a)
        args.append(nc.dram_tensor(name, a.shape, mybir.dt.from_np(a.dtype), kind="ExternalInput").ap())
    fp32 = mybir.dt.float32
    out = nc.dram_tensor("out", (TOKENS, D), fp32, kind="ExternalOutput").ap()
    xs = [nc.dram_tensor(f"xs{n}", (DUMMY + ROWS + n * TOKENS, D), fp32, kind="Internal").ap() for n in range(2)]
    ys = [nc.dram_tensor(f"ys{n}", (Y_SHARED + n * TOKENS, D), fp32, kind="Internal").ap() for n in range(2)]
    program(nc, *args, out, xs, ys)
    r = run_bass_kernel_spmd(nc, [arrays], core_ids=[0])
    return r.results[0]["out"].reshape(SEQS, SEQ, D)
```

```python
from contextlib import ExitStack

import concourse.bass as bass
from concourse import mybir
from concourse.alu_op_type import AluOpType as ALU

P = 128
D = 128
SEQS, SEQ = 8, 1024
TOKENS = SEQS * SEQ
T = SEQ // P
H, DH = 16, 8
E = 8
FF = 512
ROWS = 256
UNROLL = 4
REGION = TOKENS + ROWS
ROUTED = 2 * TOKENS // ROWS + E
SHARED = TOKENS // ROWS
DUMMY = E * REGION
X1_SHARED = DUMMY + ROWS
Y_SHARED = ROUTED * ROWS
NDIFF = 5

C_IDENT, C_BLOCK, C_PREFIX, C_STATE = 0, 128, 256, 384
C_SHIFT = C_STATE + NDIFF * 128
C_HEAD = C_SHIFT + 4 * 128
C_RANK = C_HEAD + H
C_BASE = C_RANK + E
C_COS = C_BASE + E
C_SIN = C_COS + T * DH
C_JOB = C_SIN + T * DH
JOBS = (ROUTED, ROUTED + SHARED)
NC_COLS = C_JOB + ROUTED

R_QKV0, R_O0, R_QKV1, R_GATE = 0, 384, 512, 896
NR_COLS = R_GATE + E
EPS = 1e-5


def program(nc, x_in, consts, bias_row, w_attn0, w_attn1, w_gate, w_out0, w_exp0, w_exp1, b_out0, b_out1,
            norm_w, out, xs, ys):
    fp32, bf16, i32 = mybir.dt.float32, mybir.dt.bfloat16, mybir.dt.int32
    f32r = mybir.dt.float32r
    ACT, AX = mybir.ActivationFunctionType, mybir.AxisListType

    def at(i, n):
        return slice(i, i + n) if isinstance(i, int) else bass.DynSlice(i, n)

    with ExitStack() as ctx:
        def sb(name, shape, dt=fp32):
            return ctx.enter_context(nc.sbuf_tensor(name, shape, dt))

        def sem(name):
            return ctx.enter_context(nc.semaphore(name))

        X = sb("X", [P, SEQS * T, D])
        K = sb("K", [P, NC_COLS])
        WA = [sb(f"WA{n}", [P, 4 * D]) for n in range(2)]
        WG = [sb(f"WG{n}", [P, E]) for n in range(2)]
        brow = sb("brow", [3, NR_COLS], bf16)
        ones3 = sb("ones3", [3, P], bf16)
        prefix16 = sb("prefix16", [P, P], bf16)
        ones16 = sb("ones16", [P, P], bf16)
        gains = sb("gains", [P, T * SEQS, 2])
        places = sb("places", [P, T * SEQS, 2])
        carry = [sb(f"carry{n}", [P, E]) for n in range(2)]
        table = [sb(f"table{n}", [1, 2, JOBS[n]], i32) for n in range(2)]
        padrow = [sb(f"padrow{n}", [1, E], i32) for n in range(2)]
        zeros = sb("zeros", [P, ROWS // P, D])
        ropeC = sb("ropeC", [P, T, DH])
        ropeS = sb("ropeS", [P, T, DH])
        wn = sb("wn", [P, DH])
        ident = K[:, C_IDENT:C_IDENT + P]
        block = K[:, C_BLOCK:C_BLOCK + P]

        xn = sb("xn", [P, T, D])
        xnT = sb("xnT", [P, T * P])
        qk = sb("qk", [P, T, 2 * D])
        val = sb("val", [P, T, D + 1])
        qT = sb("qT", [P, T * P])
        y = sb("y", [P, T, D])
        xn2 = sb("xn2", [P, T, D])
        kvm = sb("kvm", [P, D + H])
        stats = sb("stats", [P, T, 6])
        mv = sb("mv", [P, T, 2])
        rs = sb("rs", [P, 3, T])
        rsh = sb("rsh", [P, 3, T * 2 * H])
        mx = sb("mx", [P, 2 * H])
        den = sb("den", [P, 2, H])
        lg = sb("lg", [P, 6, T, E])
        lr = sb("lr", [P, 8, T])
        mask16 = sb("mask16", [P, T, E], bf16)
        idx = sb("idx", [P, T, 2], i32)
        place = sb("place", [P, 4, 2], i32)
        gcur = sb("gcur", [P, T, 2])
        got = sb("got", [P, T, 2, D])
        mv1 = sb("mv1", [P, 4, 2])
        mv2 = sb("mv2", [P, 2, 2])
        std1 = sb("std1", [P, 4])
        rstd1 = sb("rstd1", [P, 4])
        std2 = sb("std2", [P, 2])
        rstd2 = sb("rstd2", [P, 2])
        bn1 = sb("bn1", [P, 2, 6])
        bn2 = sb("bn2", [P, 2, 6])
        eps1 = sb("eps1", [P, 1])
        eps_head = sb("eps_head", [P, 1])
        x1T = sb("x1T", [P, 2, P])
        x2T = sb("x2T", [P, P])
        sq = sb("sq", [P, 2, 2 * D])
        hsum = sb("hsum", [P, 4, 2 * H])
        hstd = sb("hstd", [P, 4, 2 * H])
        hrec = sb("hrec", [P, 2, 2 * H])
        turned = sb("turned", [P, 2, 2 * D])
        scaled = sb("scaled", [P, 2, 2 * D])
        prods = sb("prods", [P, 4, NDIFF, D])
        ksum = sb("ksum", [P, 2, H])
        split = sb("split", [P, 2, H, 4, DH], f32r)
        splitT = sb("splitT", [P, 2, 8, P], f32r)
        qT1 = sb("qT1", [P, 2, P])
        feats = sb("feats", [P, 4, NDIFF, P])
        state = sb("state", [P, NDIFF, P])
        score = sb("score", [P, 2, 4, 4, P])
        vpad = sb("vpad", [P, 2, H, 32])
        zT = sb("zT", [P, P])
        WT = [sb(f"WT{m}", [P, 2 * FF + 4]) for m in range(UNROLL)]
        BT = [sb(f"BT{m}", [P, D]) for m in range(UNROLL)]
        XT = [sb(f"XT{u}", [P, ROWS // P, D]) for u in range(2)]
        XTT = [sb(f"XTT{u}", [P, ROWS]) for u in range(2)]
        HT = [sb(f"HT{u}", [P, 4, ROWS]) for u in range(2)]
        SG = [sb(f"SG{u}", [P, 2, ROWS]) for u in range(2)]
        YT = [sb(f"YT{u}", [P, ROWS // P, D]) for u in range(2)]

        banks = [ctx.enter_context(nc.psum_tensor(f"bank{n}", [P, 512], fp32)) for n in range(8)]

        S = {}

        def s(name):
            if name not in S:
                S[name] = sem(name)
            return S[name]

        for name in ("const_in rope_in w_in bias_in bias_split bias_rows setup_done zeroed "
                     "a0_x a0_ln1 a0_t1 a0_xT a0_qkv a0_qsub a0_v a0_exp a0_t2 a0_qT a0_kv a0_kvm "
                     "a0_num a0_y a0_t3 a0_yT a0_o a0_x1 a0_ln2 a0_t4 a0_x2T a0_gate a0_gcopy a0_dmax "
                     "a0_p a0_mask a0_pre a0_idx a0_scat "
                     "a1_place a1_got0 a1_got1 a1_mv a1_std a1_ln1 a1_t1 a1_xT a1_qkv a1_qv a1_hsum a1_hstd a1_rope a1_high a1_plain "
                     "a1_qT a1_ph a1_feat a1_split a1_splitT_ps a1_splitT a1_prod a1_vpad a1_qk a1_sqr a1_mask a1_z "
                     "a1_zT a1_st a1_state a1_o a1_x1 a1_var2 a1_std2 a1_ln2 a1_t4 a1_x2T a1_gate a1_gcopy a1_dmax "
                     "a1_p a1_mask2 a1_pre a1_idx2 "
                     "a1_scat0 a1_scat1 a1_scat2 a1_scat3 a1_nat0 a1_nat1 a1_nat2 a1_nat3 "
                     "c_idx c_got c_sh c_out c_store").split():
            s(name)
        for n in range(2):
            for name in "table pads".split():
                s(f"{name}{n}")
            for name in "x xt xT h sig act y ysb st".split():
                for u in range(2):
                    s(f"b{n}_{name}{u}")
            for m in range(UNROLL):
                s(f"b{n}_w{m}")
        words = [sb(f"word{n}", [1, 2]) for n in range(2)]
        block_ = ctx.enter_context(nc.Block())

        def rsqrt(v, work, n):
            r, a, t = work[:, 0, 0:n], work[:, 1, 0:n], work[:, 2, 0:n]
            v.tensor_scalar(r.bitcast(i32), a.bitcast(i32), 1, None, ALU.logical_shift_right)
            v.drain()
            v.tensor_scalar(r.bitcast(i32), r.bitcast(i32), -1.0, float(0x5F3759DF), ALU.mult, ALU.add)
            for _ in range(3):
                v.drain()
                v.scalar_tensor_tensor(t, r, -0.5, r, ALU.mult, ALU.mult)
                v.drain()
                v.tensor_tensor(t, t, a, ALU.mult)
                v.drain()
                v.scalar_tensor_tensor(r, t, 1.5, r, ALU.add, ALU.mult)
            v.drain()

        def wait_apart(eng, signal, value):
            eng.drain()
            eng.wait_ge(signal, value)
            word = words[eng is not nc.vector]
            eng.tensor_tensor(word[:, 1:2], word[:, 0:1], word[:, 0:1], ALU.add)

        def every_group(eng, jobs, run):
            run(0, True, False)
            with eng.Fori(1, jobs // UNROLL - 1) as i:
                run(i, False, False)
            run(jobs // UNROLL - 1, False, True)

        def each_sequence(eng, run):
            run(0)
            with eng.Fori(1, SEQS) as i:
                run(i)

        def use(i, m):
            return 2 * i + m // 2

        def after(i, m):
            return (i, m + 1) if m + 1 < UNROLL else (i + 1, 0)

        def before(i, m):
            return (i, m - 1) if m > 0 else (i - 1, UNROLL - 1)

        def wait_earlier(eng, signal, value):
            if not isinstance(value, int) or value > 0:
                eng.wait_ge(signal, value)

        def stream(i, run):
            for r in range(T):
                def stage(lead, work, r=r):
                    seq, t = i + (r + lead) // T, (r + lead) % T
                    if not isinstance(seq, int) or 0 <= seq < SEQS:
                        work(seq, t)
                run(r, stage)

        def each_body(eng, body):
            body(-1)
            body(0)
            with eng.Fori(1, SEQS - 1) as i:
                body(i)
            body(SEQS - 1)

        def need(eng, signal, i, n, each=1, more=0):
            value = each * (T * i + n) + more
            wait_earlier(eng, signal, min(value, each * TOKENS // P) if isinstance(value, int) else value)

        def need_apart(eng, signal, i, n, each=1):
            value = each * (T * i + n)
            if not isinstance(value, int):
                wait_apart(eng, signal, value)
            elif value > 0:
                eng.wait_ge(signal, value)

        def scattered(n):
            return [(s("a0_scat"), 32 * T)] if n == 0 else [(s(f"a1_scat{m}"), 32 * T // 4) for m in range(4)]

        def layernorm(v, first, dst, done):
            for t in range(T):
                v.bn_stats(stats[:, t, :], X[:, at(first + t, 1), :].rearrange("p a d -> p (a d)"))
            v.drain()
            for t in range(T):
                v.bn_aggr(mv[:, t, :], stats[:, t, :])
            v.drain()
            v.tensor_scalar(rs[:, 1, :], mv[:, :, 1], EPS, None, ALU.add)
            v.drain()
            rsqrt(v, rs, T)
            for t in range(T):
                last = v.tensor_scalar(dst[:, t, :], X[:, at(first + t, 1), :].rearrange("p a d -> p (a d)"),
                                       mv[:, t, 0:1], rs[:, 0, t:t + 1], ALU.subtract, ALU.mult)
            last.then_inc(done, 1)

        def spread(a):
            return a.unsqueeze(2).broadcast_to([P, T, E])

        rank = K[:, C_RANK:C_RANK + E].unsqueeze(1).broadcast_to([P, T, E])

        def first_of(v, flags, hot):
            v.tensor_reduce(lr[:, 3, :], flags, AX.X, ALU.max)
            v.drain()
            v.tensor_tensor(hot, rank, spread(lr[:, 3, :]), ALU.is_equal)
            v.drain()

        def routing(v, n, i, gates, names):
            gcopy, dmax, p_ready, mask, pre, idx_ready = (s(f"a{n}_{k}") for k in names)
            bank = (7, 5)[n]
            prob, hot1, hot2, pos, tmp = (lg[:, k] for k in range(5))
            if n == 0:
                v.wait_ge(s("a0_gate"), i + 1)
            else:
                v.wait_ge(s("a1_gcopy"), T * i + T)
            v.tensor_reduce(lr[:, 0, :], gates, AX.X, ALU.max)
            v.drain()
            v.tensor_tensor(tmp, gates, spread(lr[:, 0, :]), ALU.subtract).then_inc(dmax, 1)
            v.wait_ge(p_ready, i + 1)
            v.tensor_reduce(lr[:, 1, :], prob, AX.X, ALU.add)
            v.scalar_tensor_tensor(tmp, prob, 1.0, rank, ALU.is_equal, ALU.mult)
            v.drain()
            first_of(v, tmp, hot1)
            v.scalar_tensor_tensor(pos, hot1, -2.0, prob, ALU.mult, ALU.add)
            v.drain()
            v.tensor_reduce(lr[:, 2, :], pos, AX.X, ALU.max)
            v.drain()
            v.tensor_tensor(tmp, pos, spread(lr[:, 2, :]), ALU.is_equal)
            v.drain()
            v.tensor_tensor(tmp, tmp, rank, ALU.mult)
            v.drain()
            first_of(v, tmp, hot2)
            v.tensor_tensor(mask16[:, :, :], hot1, hot2, ALU.add).then_inc(mask, 1)
            v.tensor_scalar(lr[:, 4, :], lr[:, 2, :], 1.0, None, ALU.add)
            v.drain()
            if n == 0:
                v.scalar_tensor_tensor(lr[:, 5, :], lr[:, 1, :], 1e-9, lr[:, 4, :], ALU.mult, ALU.add)
            else:
                v.tensor_copy(lr[:, 5, :], lr[:, 4, :])
            v.drain()
            v.reciprocal(lr[:, 6, :], lr[:, 5, :])
            v.drain()
            v.tensor_copy(gains[:, at(T * i, T), 0], lr[:, 6, :])
            v.tensor_tensor(gains[:, at(T * i, T), 1], lr[:, 6, :], lr[:, 2, :], ALU.mult)
            v.wait_ge(pre, i + 1)
            v.tensor_tensor(pos, banks[bank][:, 256:256 + T * E].rearrange("p (t e) -> p t e", e=E),
                            carry[n][:, :].unsqueeze(1).broadcast_to([P, T, E]), ALU.add)
            v.drain()
            v.tensor_tensor(carry[n][:, :], carry[n][:, :], banks[bank][:, 320:320 + E], ALU.add)
            v.tensor_tensor(hot1, hot1, pos, ALU.mult)
            v.tensor_tensor(hot2, hot2, pos, ALU.mult)
            v.drain()
            v.tensor_reduce(lr[:, 4, :], hot1, AX.X, ALU.add)
            v.tensor_reduce(lr[:, 5, :], hot2, AX.X, ALU.add)
            v.drain()
            for signal, count in scattered(n):
                wait_earlier(v, signal, count * i)
            v.tensor_copy(idx[:, :, 0], lr[:, 4, :])
            v.tensor_copy(idx[:, :, 1], lr[:, 5, :])
            v.drain()
            v.tensor_copy(places[:, at(T * i, T), :], idx[:, :, :]).then_inc(idx_ready, 1)

        def make_table(v, n):
            cnt, til, cum, gap = (lr[:, k, :] for k in range(4))
            whole = lr[:, 4, :].bitcast(i32)
            jobs = K[0:1, C_JOB:C_JOB + ROUTED]
            v.drain()
            v.tensor_tensor(cnt, carry[n][:, :], K[:, C_BASE:C_BASE + E], ALU.subtract)
            v.drain()
            v.tensor_scalar(whole, cnt, ROWS - 1.0, None, ALU.add)
            v.drain()
            v.tensor_scalar(whole, whole, ROWS.bit_length() - 1, None, ALU.logical_shift_right)
            v.drain()
            v.tensor_copy(til, whole)
            v.drain()
            v.tensor_tensor_scan(cum, ones8[:, :], til, 0.0, ALU.mult, ALU.add)
            v.tensor_scalar(gap, til, -float(ROWS), float(REGION), ALU.mult, ALU.add)
            v.tensor_copy(padrow[n][:, :], carry[n][0:1, :])
            v.drain()
            v.tensor_tensor(lg2[:, :, :], jobs.unsqueeze(2).broadcast_to([1, ROUTED, E]),
                            cum[0:1, :].unsqueeze(1).broadcast_to([1, ROUTED, E]), ALU.is_ge)
            v.drain()
            v.tensor_reduce(jw[:, 0, :], lg2[:, :, :], AX.X, ALU.add)
            v.drain()
            v.tensor_tensor(lg2[:, :, :], lg2[:, :, :], gap[0:1, :].unsqueeze(1).broadcast_to([1, ROUTED, E]),
                            ALU.mult)
            v.drain()
            v.tensor_reduce(jw[:, 1, :], lg2[:, :, :], AX.X, ALU.add)
            v.drain()
            v.scalar_tensor_tensor(jw[:, 2, :], jobs, float(ROWS), jw[:, 1, :], ALU.mult, ALU.add)
            v.drain()
            v.tensor_scalar(table[n][:, 0, 0:ROUTED], jw[:, 2, :], float(DUMMY), None, ALU.min)
            last = v.tensor_scalar(table[n][:, 1, 0:ROUTED], jw[:, 0, :], float(E - 1), None, ALU.min)
            if n == 1:
                sh = K[0:1, C_JOB:C_JOB + SHARED]
                v.tensor_scalar(table[1][:, 0, ROUTED:], sh, float(ROWS), float(X1_SHARED), ALU.mult, ALU.add)
                last = v.tensor_scalar(table[1][:, 1, ROUTED:], sh, 0.0, float(E), ALU.mult, ALU.add)
            last.then_inc(s(f"table{n}"), 1)
            flat_places = places[:, :, :].rearrange("p t c -> p (t c)")
            shifts = got[:, 0:E, 0, :]
            for e in range(1, E):
                v.tensor_scalar(shifts[:, e, :], flat_places, float(e * REGION), gap[:, e - 1:e], ALU.is_ge,
                                ALU.mult)
            for e in range(1, E):
                v.drain()
                v.tensor_tensor(flat_places, flat_places, shifts[:, e, :], ALU.subtract)
            v.drain()

        WA2 = sb("WA2", [P, 2, D])

        lg2 = sb("lg2", [1, ROUTED, E])
        jw = sb("jw", [1, 3, ROUTED])
        ones8 = sb("ones8", [P, E])
        tiles = range(T)

        def flat(a):
            return a.rearrange("p a d -> p (a d)")

        @block_.sync
        def _(sp):
            sp.dma_start(K[:, :], consts).then_inc(s("const_in"), 16)
            sp.dma_start(WA[0][:, :], w_attn0).then_inc(s("w_in"), 16)
            sp.dma_start(WA[1][:, :], w_attn1).then_inc(s("w_in"), 16)
            for n in range(2):
                sp.dma_start(WG[n][:, :], w_gate[n]).then_inc(s("w_in"), 16)
            sp.dma_start(WA2[:, :, :], w_out0.rearrange("(c p) d -> p c d", p=P)).then_inc(s("w_in"), 16)
            sp.dma_start(BT[0][:, :], b_out0.partition_broadcast(P)).then_inc(s("w_in"), 16)
            sp.dma_start(wn[:, :], norm_w.partition_broadcast(P)).then_inc(s("rope_in"), 16)
            sp.dma_start(qk[0:1, 0:4, :].rearrange("p a d -> p (a d)")[:, 0:NR_COLS], bias_row)\
                .then_inc(s("bias_in"), 16)
            sp.wait_ge(s("bias_split"), 1)
            parts = got[0:1, :, :, :].rearrange("p a c d -> p (a c d)").bitcast(bf16)
            for r in range(3):
                sp.dma_start(brow[r:r + 1, :], parts[:, r * NR_COLS:(r + 1) * NR_COLS])\
                    .then_inc(s("bias_rows"), 16)
            for b in range(SEQS):
                sp.dma_start(X[:, T * b:T * (b + 1), :], x_in[b * SEQ:(b + 1) * SEQ, :]
                             .rearrange("(t p) d -> p t d", p=P)).then_inc(s("a0_x"), 16)
                sp.wait_ge(s("a0_x"), 16 * (b + 1))
            for n in range(2):
                if n == 1:
                    def body(i):
                        def step(r, stage):
                            def store(i, t):
                                need(sp, s("a1_ln2"), i, t + 1)
                                sp.dma_start(xs[1][at(X1_SHARED + SEQ * i + P * t, P), :], xn2[:, t, :])\
                                    .then_inc(s(f"a1_nat{t % 4}"), 16)
                            stage(0, store)
                        stream(i, step)
                    each_body(sp, body)
                sp.wait_ge(s(f"table{n}"), 1)
                sp.wait_ge(s("zeroed"), 1)
                for e in range(E):
                    row = sp.value_load(padrow[n][0:1, e:e + 1], min_val=0, max_val=DUMMY - ROWS)
                    sp.dma_start(xs[n][at(row, ROWS), :].rearrange("(a p) d -> p a d", p=P), zeros[:, :, :])\
                        .then_inc(s(f"pads{n}"), 16)
                sp.dma_start(xs[n][DUMMY:DUMMY + ROWS, :].rearrange("(a p) d -> p a d", p=P), zeros[:, :, :])\
                    .then_inc(s(f"pads{n}"), 16)
                sp.wait_ge(s(f"pads{n}"), 16 * (E + 1))
                for signal, count in scattered(n):
                    sp.wait_ge(signal, count * SEQS)
                if n == 1:
                    for m in range(4):
                        sp.wait_ge(s(f"a1_nat{m}"), 16 * SEQS * T // 4)
                width = (FF + 4, 2 * FF + 4)[n]

                def load(i, m):
                    k, u = use(i, m), m % 2
                    e = sp.value_load(table[n][0:1, 1, at(UNROLL * i + m, 1)], min_val=0, max_val=E - 1 + n)
                    row = sp.value_load(table[n][0:1, 0, at(UNROLL * i + m, 1)], min_val=0,
                                        max_val=(DUMMY, X1_SHARED + TOKENS - ROWS)[n])
                    wait_earlier(sp, s(f"b{n}_xt{u}"), k)
                    sp.dma_start(XT[u][:, :, :], xs[n][at(row, ROWS), :].rearrange("(a p) d -> p a d", p=P))\
                        .then_inc(s(f"b{n}_x{u}"), 16)
                    wait_earlier(sp, s(f"b{n}_ysb{u}"), k - 1)
                    sp.dma_start(WT[m][:, 0:width], (w_exp0, w_exp1)[n][at(e, 1), :, :].rearrange("a p f -> p (a f)"))\
                        .then_inc(s(f"b{n}_w{m}"), 16)
                    if n == 1:
                        sp.dma_start(BT[m][:, :], b_out1[at(e, 1), :].rearrange("a d -> (a d)").partition_broadcast(P))\
                            .then_inc(s(f"b{n}_w{m}"), 16)

                def load_group(i, first, last):
                    for m in range(UNROLL):
                        load(i, m)

                every_group(sp, JOBS[n], load_group)
            for u in range(2):
                sp.wait_ge(s(f"b1_st{u}"), 16 * (JOBS[1] // 2))
            def sequence(i):
                wait_earlier(sp, s("c_out"), i)
                sp.dma_start(y[:, :, :], ys[1][at(Y_SHARED + SEQ * i, SEQ), :].rearrange("(t p) d -> p t d", p=P))\
                    .then_inc(s("c_sh"), 16)
                sp.wait_ge(s("c_out"), i + 1)
                sp.dma_start(out[at(SEQ * i, SEQ), :].rearrange("(t p) d -> p t d", p=P), X[:, at(T * i, T), :])\
                    .then_inc(s("c_store"), 16)
            each_sequence(sp, sequence)
            sp.wait_ge(s("c_store"), 16 * SEQS)

        @block_.gpsimd
        def _(g):
            g.memset(vpad[:, :, :, :], 0.0)
            g.memset(words[1][:, :], 0.0)
            g.memset(zeros[:, :, :], 0.0).then_inc(s("zeroed"), 1)

            def scatter(n, i, ready):
                wait_apart(g, ready, i + 1)
                for t in tiles:
                    for c in range(2):
                        g.indirect_dma_start(xs[n], bass.IndirectOffsetOnAxis(idx[:, t, c:c + 1], 0),
                                             xn2[:, t, :], None).then_inc(s(f"a{n}_scat"), 16)

            def gather(n, i, ready, done):
                wait_apart(g, ready, i + 1)
                for t in tiles:
                    for c in range(2):
                        g.indirect_dma_start(got[:, t, c, :], None, ys[n],
                                             bass.IndirectOffsetOnAxis(idx[:, t, c:c + 1], 0)).then_inc(done, 16)

            def store_all(n):
                def store_group(i, first, last):
                    for m in range(UNROLL):
                        k, u = use(i, m), m % 2
                        g.wait_ge(s(f"b{n}_ysb{u}"), k + 1)
                        g.dma_start(ys[n][at(ROWS * (UNROLL * i + m), ROWS), :].rearrange("(a p) d -> p a d", p=P), YT[u][:, :, :])\
                            .then_inc(s(f"b{n}_st{u}"), 16)

                every_group(g, JOBS[n], store_group)
                for u in range(2):
                    g.wait_ge(s(f"b{n}_st{u}"), 16 * (JOBS[n] // 2))

            def sequence(i):
                scatter(0, i, s("a0_idx"))
            each_sequence(g, sequence)
            store_all(0)
            def scatter_tile(i, t):
                for c in range(2):
                    g.indirect_dma_start(xs[1], bass.IndirectOffsetOnAxis(idx[:, t, c:c + 1], 0),
                                         xn2[:, t, :], None).then_inc(s(f"a1_scat{t % 4}"), 16)

            def body(i):
                def step(r, stage):
                    def gather_tile(i, t):
                        need_apart(g, s("a1_place"), i, t + 1)
                        for c in range(2):
                            g.indirect_dma_start(got[:, t, c, :], None, ys[0],
                                                 bass.IndirectOffsetOnAxis(place[:, t % 4, c:c + 1], 0))\
                                .then_inc(s(f"a1_got{t % 2}"), 16)

                    def causal(i, t):
                        need_apart(g, s("a1_sqr"), i, t + 1)
                        all_scores = score[:, t % 2, :, :, :].rearrange("p a b c -> p (a b) c")
                        g.affine_select(out=all_scores, in_=all_scores, compare_op=ALU.is_ge, fill=0.0, base=0,
                                        pattern=[[0, H], [1, P]], channel_multiplier=-1)\
                            .then_inc(s("a1_mask"), 1)

                    def scatter_last(i, t):
                        if t == 0:
                            wait_apart(g, s("a1_idx2"), i + 1)
                        scatter_tile(i, t)

                    stage(8, gather_tile)
                    stage(2, causal)
                    stage(-T, scatter_last)
                stream(i, step)
            each_body(g, body)
            g.wait_ge(s("a1_idx2"), SEQS)
            for t in tiles:
                scatter_tile(SEQS - 1, t)
            store_all(1)
            def sequence(i):
                gather(1, i, s("c_idx"), s("c_got"))

            each_sequence(g, sequence)
        @block_.scalar
        def _(a):
            def experts(n):
                def xt(i, m):
                    k, u = use(i, m), m % 2
                    a.wait_ge(s(f"b{n}_xt{u}"), k + 1)
                    a.activation(XTT[u][:, :], banks[u][:, 0:ROWS], ACT.Copy).then_inc(s(f"b{n}_xT{u}"), 1)

                def act_group(i, first, last):
                    if first:
                        xt(0, 0)
                    for m in range(UNROLL):
                        k, u = use(i, m), m % 2
                        if not (last and m == UNROLL - 1):
                            xt(*after(i, m))
                        for half in range(2):
                            hp = banks[2 + 2 * u + half][:, :].rearrange("p (c r) -> p c r", r=ROWS)
                            if n == 0 and half == 0:
                                continue
                            a.wait_ge(s(f"b{n}_h{u}"), 2 * k + half + 1)
                            if n == 0:
                                wait_earlier(a, s(f"b{n}_act{u}"), k)
                            elif half == 0:
                                wait_earlier(a, s(f"b{n}_y{u}"), k)
                            for c in range(2):
                                cc = 2 * half + c
                                bias = WT[m][:, FF + cc:FF + cc + 1]
                                if n == 0:
                                    last_ = a.activation(SG[u][:, c, :], hp[:, c, :], ACT.Sigmoid, bias=bias)
                                else:
                                    last_ = a.activation(HT[u][:, cc, :], hp[:, c, :], ACT.Gelu_apprx_tanh, bias=bias)
                            last_.then_inc(s(f"b{n}_{'sig' if n == 0 else 'act'}{u}"), 1)

                every_group(a, JOBS[n], act_group)

            def evac_pair(src, dst, wait, i, done, per=2):
                for half in range(2):
                    a.wait_ge(wait, per * i + half + 1)
                    a.activation(dst[:, 512 * half:512 * (half + 1)], banks[src + half][:, :], ACT.Copy)\
                        .then_inc(done, 1)

            def sequence(i):
                evac_pair(0, xnT, s("a0_t1"), i, s("a0_xT"))
                for t in tiles:
                    a.wait_ge(s("a0_qsub"), T * i + t + 1)
                    a.activation(val[:, t, 0:D], banks[2 + t % 2][:, 2 * D:3 * D], ACT.Copy).then_inc(s("a0_v"), 1)
                for half in range(2):
                    a.wait_ge(s("a0_qsub"), T * i + 4 * half + 4)
                    a.activation(qk[:, 4 * half:4 * half + 4, :], qk[:, 4 * half:4 * half + 4, :], ACT.Exp)\
                        .then_inc(s("a0_exp"), 1)
                evac_pair(0, qT, s("a0_t2"), i, s("a0_qT"))
                evac_pair(0, qT, s("a0_t3"), i, s("a0_yT"))
                evac_pair(0, xnT, s("a0_t4"), i, s("a0_x2T"))
                a.wait_ge(s("a0_dmax"), i + 1)
                a.activation(lg[:, 0], lg[:, 4], ACT.Exp).then_inc(s("a0_p"), 1)
            each_sequence(a, sequence)
            experts(0)
            def copy(dst, src):
                return a.activation(dst, src, ACT.Copy)

            def body(i):
                def step(r, stage):
                    def root1(i, t):
                        need(a, s("a1_mv"), i, t + 1)
                        a.activation(std1[:, t % 4:t % 4 + 1], mv1[:, t % 4, 1:2], ACT.Sqrt, bias=eps1[:, :])\
                            .then_inc(s("a1_std"), 1)

                    def root_heads(i, t):
                        need(a, s("a1_hsum"), i, t + 1)
                        a.activation(hstd[:, t % 4, :], hsum[:, t % 4, :], ACT.Sqrt, bias=eps_head[:, :],
                                     scale=1.0 / DH).then_inc(s("a1_hstd"), 1)

                    def high(i, t):
                        need(a, s("a1_rope"), i, t + 1)
                        for side in range(2):
                            parts = split[:, side, :, 0:3:2, :] if side == 0 else split[:, side, :, 0:2, :]
                            x = qk[:, t, D * side:D * side + D].rearrange("p (h d) -> p h d", d=DH)
                            last = copy(parts, x.unsqueeze(2).broadcast_to([P, H, 2, DH]))
                        last.then_inc(s("a1_high"), 1)

                    def squares(i, t):
                        need(a, s("a1_qk"), i, t + 1)
                        for hh in range(4):
                            last = a.activation(score[:, t % 2, hh, :, :].rearrange("p g c -> p (g c)"),
                                                banks[hh][:, :], ACT.Square, scale=1.0 / DH)
                        last.then_inc(s("a1_sqr"), 1)

                    def copy_z(i, t):
                        need(a, s("a1_z"), i, t + 1)
                        copy(zT[:, :], banks[6][:, 0:P]).then_inc(s("a1_zT"), 1)

                    def root2(i, t):
                        need(a, s("a1_var2"), i, t + 1)
                        a.activation(std2[:, t % 2:t % 2 + 1], mv2[:, t % 2, 1:2], ACT.Sqrt, bias=eps1[:, :])\
                            .then_inc(s("a1_std2"), 1)

                    def copy_qkv(i, t):
                        need(a, s("a1_qkv"), i, t + 1)
                        copy(qk[:, t, :], banks[4][:, 0:2 * D])
                        copy(val[:, t, 0:D], banks[4][:, 2 * D:3 * D])
                        a.activation(sq[:, t % 2, :], banks[4][:, 0:2 * D], ACT.Square).then_inc(s("a1_qv"), 1)

                    def features(i, t):
                        need(a, s("a1_ph"), i, t + 1)
                        a.activation(feats[:, t % 4, 1:NDIFF, :].rearrange("p a b -> p (a b)"), banks[5][:, :],
                                     ACT.Square).then_inc(s("a1_feat"), 1)

                    def copy_x1(i, t):
                        need(a, s("a1_t1"), i, t + 1)
                        copy(x1T[:, t % 2, :], banks[2][:, 0:P]).then_inc(s("a1_xT"), 1)

                    def copy_q(i, t):
                        need(a, s("a1_plain"), i, t + 1)
                        copy(qT1[:, t % 2, :], banks[3][:, 0:P])
                        a.activation(feats[:, t % 4, 0, :], banks[3][:, 0:P], ACT.Square).then_inc(s("a1_qT"), 1)

                    def copy_split(i, t):
                        for side in range(2):
                            need(a, s("a1_splitT_ps"), i, t, 2, side + 1)
                            copy(splitT[:, t % 2, 4 * side:4 * side + 4, :].rearrange("p a b -> p (a b)"),
                                 banks[4 + side][:, :]).then_inc(s("a1_splitT"), 1)

                    stage(6, root1)
                    stage(4, root_heads)
                    stage(3, high)
                    stage(2, squares)
                    stage(1, copy_z)
                    stage(5, copy_qkv)
                    stage(0, root2)
                    stage(2, features)
                    if r > 0:
                        stage(-1, copy_x2)
                    stage(6, copy_x1)
                    stage(3, copy_q)
                    if r > 0:
                        stage(-1, copy_logits)
                    stage(3, copy_split)

                def copy_x2(i, t):
                    need(a, s("a1_t4"), i, t + 1)
                    copy(x2T[:, :], banks[0][:, 0:P]).then_inc(s("a1_x2T"), 1)

                def copy_logits(i, t):
                    need(a, s("a1_gate"), i, t + 1)
                    copy(lg[:, 5, t, :], banks[1][:, 0:E]).then_inc(s("a1_gcopy"), 1)

                stream(i, step)
                if not isinstance(i, int) or i >= 0:
                    copy_x2(i, T - 1)
                    copy_logits(i, T - 1)
                    a.wait_ge(s("a1_dmax"), i + 1)
                    a.activation(lg[:, 0], lg[:, 4], ACT.Exp).then_inc(s("a1_p"), 1)
            each_body(a, body)
            experts(1)

        @block_.vector
        def _(v):
            v.wait_ge(s("bias_in"), 16)
            raw = qk[0:1, 0:4, :].rearrange("p a d -> p (a d)")[:, 0:NR_COLS]
            parts = got[0:1, :, :, :].rearrange("p a c d -> p (a c d)").bitcast(bf16)
            rest = qk[0:1, 4:8, :].rearrange("p a d -> p (a d)")[:, 0:NR_COLS]
            for r in range(3):
                part = parts[:, r * NR_COLS:(r + 1) * NR_COLS]
                last = v.tensor_copy(part, raw if r == 0 else rest)
                if r < 2:
                    v.drain()
                    v.tensor_tensor(rest, raw if r == 0 else rest, part, ALU.subtract)
                    v.drain()
            last.then_inc(s("bias_split"), 1)
            v.memset(ones3[:, :], 1.0)
            v.memset(words[0][:, :], 0.0)
            v.memset(eps1[:, :], EPS)
            v.memset(eps_head[:, :], 2.0 ** -23)
            v.memset(ones16[:, :], 1.0)
            v.memset(val[:, :, D:D + 1], 1.0)
            v.memset(ones8[:, :], 1.0)
            v.wait_ge(s("const_in"), 16)
            for n in range(2):
                v.tensor_copy(carry[n][:, :], K[:, C_BASE:C_BASE + E])
            v.tensor_copy(prefix16[:, :], K[:, C_PREFIX:C_PREFIX + P]).then_inc(s("setup_done"), 1)
            v.wait_ge(s("rope_in"), 16)
            v.wait_ge(s("w_in"), 16 * 6)
            v.tensor_tensor(ropeC[:, :, :], K[:, C_COS:C_COS + T * DH].rearrange("p (t d) -> p t d", d=DH),
                            wn[:, :].unsqueeze(1).broadcast_to([P, T, DH]), ALU.mult)
            sin = K[:, C_SIN:C_SIN + T * DH].rearrange("p (t j c) -> p t j c", j=4, c=2)
            ws = wn[:, :].rearrange("p (j c) -> p j c", c=2)
            rS = ropeS[:, :, :].rearrange("p t (j c) -> p t j c", c=2)
            for c in range(2):
                v.tensor_tensor(rS[:, :, :, c], sin[:, :, :, c],
                                ws[:, :, 1 - c].unsqueeze(1).broadcast_to([P, T, 4]), ALU.mult)
            v.wait_ge(s("bias_rows"), 48)
            v.wait_ge(s("zeroed"), 1)
            heads = "p (h d) -> p h d"
            def sequence(i):
                wait_apart(v, s("a0_x"), 16 * i + 16)
                layernorm(v, T * i, xn, s("a0_ln1"))
                for t in tiles:
                    v.wait_ge(s("a0_qkv"), T * i + t + 1)
                    src = banks[2 + t % 2][:, 0:2 * D].rearrange(heads, d=DH)
                    v.tensor_reduce(mx[:, :], src, AX.X, ALU.max)
                    v.drain()
                    v.tensor_tensor(qk[:, t, :].rearrange(heads, d=DH), src,
                                    mx[:, :].unsqueeze(2).broadcast_to([P, 2 * H, DH]), ALU.subtract)\
                        .then_inc(s("a0_qsub"), 1)
                    v.drain()
                v.wait_ge(s("a0_kv"), i + 1)
                v.tensor_tensor(kvm[:, 0:D], banks[4][:, 0:D], block, ALU.mult)
                v.tensor_scalar(kvm[:, D:D + H], K[:, C_HEAD:C_HEAD + H], banks[4][:, D:D + 1], None, ALU.mult)\
                    .then_inc(s("a0_kvm"), 1)
                for t2_ in range(T // 2):
                    v.wait_ge(s("a0_num"), (T // 2) * i + t2_ + 1)
                    yb = banks[5 + t2_ % 2][:, :].rearrange("p (a c) -> p a c", a=2)
                    v.tensor_scalar(den[:, :, :], yb[:, :, D:D + H], 1e-6, None, ALU.add)
                    v.drain()
                    v.reciprocal(den[:, :, :], den[:, :, :])
                    v.drain()
                    v.tensor_tensor(y[:, 2 * t2_:2 * t2_ + 2, :].rearrange("p a (h d) -> p a h d", d=DH),
                                    yb[:, :, 0:D].rearrange("p a (h d) -> p a h d", d=DH),
                                    den[:, :, :].unsqueeze(3).broadcast_to([P, 2, H, DH]), ALU.mult)\
                        .then_inc(s("a0_y"), 1)
                    v.drain()
                for half in range(2):
                    v.wait_ge(s("a0_o"), 2 * i + half + 1)
                    rows = X[:, at(T * i + 4 * half, 4), :]
                    last = v.tensor_tensor(rows, rows, banks[2 + half][:, :].rearrange("p (a d) -> p a d", a=4),
                                           ALU.add)
                last.then_inc(s("a0_x1"), 1)
                v.drain()
                if not isinstance(i, int) or i > 0:
                    wait_apart(v, s("a0_scat"), 16 * 2 * T * i)
                layernorm(v, T * i, xn2, s("a0_ln2"))
                routing(v, 0, i, banks[7][:, 0:T * E].rearrange("p (t e) -> p t e", e=E),
                        ("gcopy", "dmax", "p", "mask", "pre", "idx"))
                v.drain()
            each_sequence(v, sequence)

            def combine(i, ready, done=None):
                v.wait_ge(ready, 16 * 2 * T * (i + 1))
                for c in range(2):
                    for t in tiles:
                        row = X[:, at(T * i + t, 1), :].rearrange("p a d -> p (a d)")
                        last = v.scalar_tensor_tensor(row, got[:, t, c, :], gcur[:, t, c:c + 1], row,
                                                      ALU.mult, ALU.add)
                    if c == 0:
                        v.drain()
                if done is not None:
                    last.then_inc(done, 1)
                v.drain()

            def fetch_places(i, ready):
                v.tensor_copy(idx[:, :, :], places[:, at(T * i, T), :]).then_inc(ready, 1)
                v.tensor_copy(gcur[:, :, :], gains[:, at(T * i, T), :])
                v.drain()

            def experts(n):
                def finish(i, m):
                    k, u = use(i, m), m % 2
                    v.wait_ge(s(f"b{n}_y{u}"), k + 1)
                    wait_earlier(v, s(f"b{n}_st{u}"), 16 * k)
                    bt = BT[0] if n == 0 else BT[m]
                    v.tensor_tensor(YT[u][:, :, :], banks[6 + u][:, 0:ROWS].rearrange("p (a d) -> p a d", d=D),
                                    bt[:, :].unsqueeze(1).broadcast_to([P, ROWS // P, D]), ALU.add)\
                        .then_inc(s(f"b{n}_ysb{u}"), 1)

                def gate(i, m):
                    k, u = use(i, m), m % 2
                    v.wait_ge(s(f"b{n}_sig{u}"), k + 1)
                    wait_earlier(v, s(f"b{n}_y{u}"), k)
                    hp = banks[2 + 2 * u][:, :].rearrange("p (c r) -> p c r", r=ROWS)
                    for c in range(2):
                        last = v.scalar_tensor_tensor(HT[u][:, c, :], hp[:, c, :], WT[m][:, FF + c:FF + c + 1],
                                                      SG[u][:, c, :], ALU.add, ALU.mult)
                    last.then_inc(s(f"b{n}_act{u}"), 1)

                def dve_group(i, first, last):
                    for m in range(UNROLL):
                        if n == 0:
                            gate(i, m)
                        if not (first and m == 0):
                            finish(*before(i, m))
                    if last:
                        finish(i, UNROLL - 1)

                every_group(v, JOBS[n], dve_group)

            v.wait_ge(s("a0_scat"), 16 * 2 * T * SEQS)
            make_table(v, 0)
            experts(0)
            v.drain()
            def body(i):
                def step(r, stage):
                    def row(i, t):
                        return flat(X[:, at(T * i + t, 1), :])

                    def heads_of(a_):
                        return a_.rearrange("p (h d) -> p h d", d=DH)

                    def fetch(i, t):
                        v.tensor_copy(gcur[:, t, :], gains[:, at(T * i + t, 1), :].rearrange("p a c -> p (a c)"))
                        v.tensor_copy(place[:, t % 4, :], places[:, at(T * i + t, 1), :]
                                      .rearrange("p a c -> p (a c)")).then_inc(s("a1_place"), 1)

                    def add_expert(c):
                        def work(i, t):
                            if c == 0:
                                wait_earlier(v, s(f"a1_got{t % 2}"), 32 * (T // 2 * i + t // 2 + 1))
                            v.scalar_tensor_tensor(row(i, t), got[:, t, c, :], gcur[:, t, c:c + 1], row(i, t),
                                                   ALU.mult, ALU.add)
                        return work

                    def stats1(i, t):
                        v.bn_stats(bn1[:, t % 2, :], row(i, t))

                    def moments1(i, t):
                        v.bn_aggr(mv1[:, t % 4, :], bn1[:, t % 2, :]).then_inc(s("a1_mv"), 1)

                    def inverse1(i, t):
                        need(v, s("a1_std"), i, t + 1)
                        v.reciprocal(rstd1[:, t % 4:t % 4 + 1], std1[:, t % 4:t % 4 + 1])

                    def normalise1(i, t):
                        v.tensor_scalar(xn[:, t, :], row(i, t), mv1[:, t % 4, 0:1], rstd1[:, t % 4:t % 4 + 1],
                                        ALU.subtract, ALU.mult).then_inc(s("a1_ln1"), 1)

                    def skip(i, t):
                        v.tensor_tensor(row(i, t), row(i, t), xn[:, t, :], ALU.add)

                    def sum_squares(i, t):
                        need(v, s("a1_qv"), i, t + 1)
                        v.tensor_reduce(hsum[:, t % 4, :], heads_of(sq[:, t % 2, :]), AX.X, ALU.add)\
                            .then_inc(s("a1_hsum"), 1)

                    def inverse_heads(i, t):
                        need(v, s("a1_hstd"), i, t + 1)
                        v.reciprocal(hrec[:, t % 2, :], hstd[:, t % 4, :])

                    def scale_heads(i, t):
                        v.tensor_tensor(heads_of(qk[:, t, :]), heads_of(qk[:, t, :]),
                                        hrec[:, t % 2, :].unsqueeze(2).broadcast_to([P, 2 * H, DH]), ALU.mult)

                    def turn(i, t):
                        qh = qk[:, t, :].rearrange("p (h j c) -> p h j c", j=4, c=2)
                        th = turned[:, t % 2, :].rearrange("p (h j c) -> p h j c", j=4, c=2)
                        for c in range(2):
                            v.tensor_tensor(th[:, :, :, c], qh[:, :, :, 1 - c],
                                            ropeS[:, t, :].rearrange("p (j c) -> p j c", c=2)[:, :, c]
                                            .unsqueeze(1).broadcast_to([P, 2 * H, 4]), ALU.mult)
                        v.tensor_tensor(heads_of(scaled[:, t % 2, :]), heads_of(qk[:, t, :]),
                                        ropeC[:, t, :].unsqueeze(1).broadcast_to([P, 2 * H, DH]), ALU.mult)

                    def add_turned(i, t):
                        v.tensor_tensor(qk[:, t, :], scaled[:, t % 2, :], turned[:, t % 2, :], ALU.add)\
                            .then_inc(s("a1_rope"), 1)

                    def sum_k(i, t):
                        v.tensor_reduce(ksum[:, t % 2, :], heads_of(qk[:, t, D:2 * D]), AX.X, ALU.add)

                    def products(i, t):
                        k_ = heads_of(qk[:, t, D:2 * D])
                        for d in range(1, NDIFF):
                            pd = heads_of(prods[:, t % 4, d, :])
                            v.tensor_tensor(pd[:, :, 0:DH - d], k_[:, :, 0:DH - d], k_[:, :, d:DH], ALU.mult)
                            v.tensor_tensor(pd[:, :, DH - d:DH], k_[:, :, DH - d:DH], k_[:, :, 0:d], ALU.mult)

                    def product0a(i, t):
                        v.scalar_tensor_tensor(heads_of(prods[:, t % 4, 0, :]), heads_of(qk[:, t, D:2 * D]), 2.0,
                                               ksum[:, t % 2, :].unsqueeze(2).broadcast_to([P, H, DH]),
                                               ALU.mult, ALU.subtract)

                    def product0b(i, t):
                        p0 = prods[:, t % 4, 0, :]
                        v.tensor_tensor(p0, p0, qk[:, t, D:2 * D], ALU.mult).then_inc(s("a1_prod"), 1)

                    def low(i, t):
                        need(v, s("a1_high"), i, t + 1)
                        for side in range(2):
                            if side == 0:
                                dst, hi = split[:, 0, :, 1:4:2, :], split[:, 0, :, 0:3:2, :]
                            else:
                                dst, hi = split[:, 1, :, 2:4, :], split[:, 1, :, 0:2, :]
                            x = heads_of(qk[:, t, D * side:D * side + D]).unsqueeze(2).broadcast_to([P, H, 2, DH])
                            last = v.tensor_tensor(dst, x, hi, ALU.subtract)
                        last.then_inc(s("a1_split"), 1)

                    def pad_values(i, t):
                        need(v, s("a1_z"), i, t - 1)
                        for hh in range(4):
                            last = v.tensor_copy(vpad[:, t % 2, :, :].rearrange("p (g h) e -> p g h e", h=4)
                                                 [:, :, hh, DH * hh:DH * (hh + 1)],
                                                 val[:, t, 0:D].rearrange("p (g h e) -> p g h e", g=4, h=4)
                                                 [:, :, hh, :])
                        last.then_inc(s("a1_vpad"), 1)

                    def new_state(i, t):
                        if t < T - 1:
                            wait_earlier(v, s("a1_st"), (T - 1) * i + t + 1)
                            need(v, s("a1_z"), i, t + 1)
                            v.tensor_tensor(state[:, :, :].rearrange("p d (g c) -> p d g c", c=32),
                                            banks[7][:, 0:NDIFF * 32].rearrange("p (d c) -> p d c", c=32)
                                            .unsqueeze(2).broadcast_to([P, NDIFF, 4, 32]),
                                            K[:, C_STATE:C_STATE + NDIFF * P]
                                            .rearrange("p (d g c) -> p d g c", g=4, c=32), ALU.mult)\
                                .then_inc(s("a1_state"), 1)

                    def add_attention(i, t):
                        need(v, s("a1_o"), i, t + 1)
                        v.tensor_tensor(row(i, t), row(i, t), banks[6][:, P:2 * P], ALU.add)\
                            .then_inc(s("a1_x1"), 1)

                    def stats2(i, t):
                        v.bn_stats(bn2[:, t % 2, :], row(i, t))

                    def moments2(i, t):
                        v.bn_aggr(mv2[:, t % 2, :], bn2[:, t % 2, :]).then_inc(s("a1_var2"), 1)

                    def inverse2(i, t):
                        need(v, s("a1_std2"), i, t + 1)
                        v.reciprocal(rstd2[:, t % 2:t % 2 + 1], std2[:, t % 2:t % 2 + 1])

                    def normalise2(i, t):
                        wait_earlier(v, s(f"a1_nat{t % 4}"), 16 * (2 * i + t // 4))
                        wait_earlier(v, s(f"a1_scat{t % 4}"), 32 * (2 * i - 2 + t // 4 + 1))
                        v.tensor_scalar(xn2[:, t, :], row(i, t), mv2[:, t % 2, 0:1], rstd2[:, t % 2:t % 2 + 1],
                                        ALU.subtract, ALU.mult).then_inc(s("a1_ln2"), 1)

                    stage(8, fetch)
                    stage(7, add_expert(0))
                    stage(0, stats2)
                    stage(3, sum_k)
                    stage(3, products)
                    stage(2, pad_values)
                    v.drain()
                    stage(7, add_expert(1))
                    stage(0, moments2)
                    stage(6, inverse1)
                    stage(4, inverse_heads)
                    stage(3, product0a)
                    v.drain()
                    stage(7, stats1)
                    stage(6, normalise1)
                    stage(4, scale_heads)
                    stage(3, product0b)
                    stage(3, low)
                    v.drain()
                    stage(7, moments1)
                    stage(6, skip)
                    stage(4, turn)
                    stage(1, new_state)
                    stage(5, sum_squares)
                    stage(0, inverse2)
                    v.drain()
                    stage(0, normalise2)
                    stage(4, add_turned)
                    stage(1, add_attention)
                    v.drain()

                stream(i, step)
                if not isinstance(i, int) or i >= 0:
                    routing(v, 1, i, lg[:, 5], ("gcopy", "dmax", "p", "mask2", "pre", "idx2"))
                    v.drain()
            each_body(v, body)
            for signal, count in scattered(1):
                v.wait_ge(signal, count * SEQS)
            make_table(v, 1)
            experts(1)
            v.drain()
            def sequence(i):
                wait_earlier(v, s("c_got"), 16 * 2 * T * i)
                fetch_places(i, s("c_idx"))
                v.wait_ge(s("c_sh"), 16 * (i + 1))
                rows = X[:, at(T * i, T), :]
                v.tensor_tensor(rows, rows, y[:, :, :], ALU.add)
                v.drain()
                combine(i, s("c_got"), s("c_out"))

            each_sequence(v, sequence)
        @block_.tensor
        def _(pe):
            def transposes(src, bank0, i, ready, done):
                pe.wait_ge(ready, i + 1)
                for half in range(2):
                    for t in range(4):
                        last = pe.transpose(banks[bank0 + half][:, P * t:P * (t + 1)], src(4 * half + t), ident)
                    last.then_inc(done, 1)

            def biased(dst, lhsT, rhs, col, n):
                pe.matmul(dst, ones3[:, :], brow[:, col:col + n], start=True, stop=False)
                return pe.matmul(dst, lhsT, rhs, start=False, stop=True)

            def routing_sums(n, i, mask, pre, bank):
                pe.wait_ge(mask, i + 1)
                pos = banks[bank][:, 256:256 + T * E].rearrange("p (t e) -> p t e", e=E)
                for t in tiles:
                    pe.matmul(pos[:, t, :], prefix16[:, :], mask16[:, t, :], start=(t == 0), stop=False,
                              skip_group_check=True)
                for t in range(T - 1):
                    pe.matmul(pos[:, t + 1:T, :], ones16[:, :],
                              mask16[:, t, :].unsqueeze(1).broadcast_to([P, T - 1 - t, E]),
                              start=False, stop=(t == T - 2), skip_group_check=True)
                for t in tiles:
                    last = pe.matmul(banks[bank][:, 320:320 + E], ones16[:, :], mask16[:, t, :],
                                     start=(t == 0), stop=(t == T - 1), skip_group_check=True)
                last.then_inc(pre, 1)

            def experts(n):
                def flip(i, m):
                    k, u = use(i, m), m % 2
                    pe.wait_ge(s(f"b{n}_x{u}"), 16 * (k + 1))
                    wait_earlier(pe, s(f"b{n}_xT{u}"), k)
                    for a_ in range(ROWS // P):
                        last = pe.transpose(banks[u][:, P * a_:P * (a_ + 1)], XT[u][:, a_, :], ident)
                    last.then_inc(s(f"b{n}_xt{u}"), 1)

                def up(i, m):
                    k, u = use(i, m), m % 2
                    pe.wait_ge(s(f"b{n}_xT{u}"), k + 1)
                    pe.wait_ge(s(f"b{n}_w{m}"), 16 * (1 + n) * (i + 1))
                    wait_earlier(pe, s(f"b{n}_act{u}"), k * (1 + n))
                    for half in range(2):
                        hp = banks[2 + 2 * u + half][:, :].rearrange("p (c r) -> p c r", r=ROWS)
                        for c in range(2):
                            cc = 2 * half + c
                            last = pe.matmul(hp[:, c, :], WT[m][:, P * cc:P * (cc + 1)], XTT[u][:, :],
                                             start=True, stop=True)
                        last.then_inc(s(f"b{n}_h{u}"), 1)

                def down(i, m):
                    k, u = use(i, m), m % 2
                    pe.wait_ge(s(f"b{n}_act{u}"), (k + 1) * (1 + n))
                    wait_earlier(pe, s(f"b{n}_ysb{u}"), k)
                    chunks = (2, 4)[n]
                    for a_ in range(ROWS // P):
                        for c in range(chunks):
                            rhs = WA2[:, c, :] if n == 0 else WT[m][:, FF + 4 + P * c:FF + 4 + P * (c + 1)]
                            last = pe.matmul(banks[6 + u][:, D * a_:D * (a_ + 1)],
                                             HT[u][:, c, P * a_:P * (a_ + 1)], rhs,
                                             start=(c == 0), stop=(c == chunks - 1))
                    last.then_inc(s(f"b{n}_y{u}"), 1)

                def pe_group(i, first, last):
                    if first:
                        flip(0, 0)
                    for m in range(UNROLL):
                        if not (last and m == UNROLL - 1):
                            flip(*after(i, m))
                        up(i, m)
                        if not (first and m == 0):
                            down(*before(i, m))
                    if last:
                        down(i, UNROLL - 1)

                every_group(pe, JOBS[n], pe_group)

            pe.wait_ge(s("const_in"), 16)
            pe.wait_ge(s("w_in"), 16 * 6)
            pe.wait_ge(s("bias_rows"), 48)
            pe.wait_ge(s("setup_done"), 1)
            def sequence(i):
                wait_earlier(pe, s("a0_qT"), 2 * i)
                wait_earlier(pe, s("a0_x2T"), 2 * i)
                transposes(lambda t: xn[:, t, :], 0, i, s("a0_ln1"), s("a0_t1"))
                pe.wait_ge(s("a0_xT"), 2 * i + 2)
                wait_earlier(pe, s("a0_x1"), i)
                for t in tiles:
                    if t >= 2:
                        pe.wait_ge(s("a0_qsub"), T * i + t - 1)
                        pe.wait_ge(s("a0_v"), T * i + t - 1)
                    biased(banks[2 + t % 2][:, 0:3 * D], xnT[:, P * t:P * (t + 1)], WA[0][:, 0:3 * D],
                           R_QKV0, 3 * D).then_inc(s("a0_qkv"), 1)
                pe.wait_ge(s("a0_exp"), 2 * i + 2)
                pe.wait_ge(s("a0_v"), T * i + T)
                for t in tiles:
                    last = pe.matmul(banks[4][:, 0:D + 1], qk[:, t, D:2 * D], val[:, t, :],
                                     start=(t == 0), stop=(t == T - 1))
                last.then_inc(s("a0_kv"), 1)
                transposes(lambda t: qk[:, t, 0:D], 0, 2 * i + 1, s("a0_exp"), s("a0_t2"))
                pe.wait_ge(s("a0_kvm"), i + 1)
                pe.wait_ge(s("a0_qT"), 2 * i + 2)
                for c in range(T // 2):
                    if c >= 2:
                        pe.wait_ge(s("a0_y"), (T // 2) * i + c - 1)
                    for t in range(2):
                        last = pe.matmul(banks[5 + c % 2][:, 256 * t:256 * t + D + H],
                                         qT[:, P * (2 * c + t):P * (2 * c + t + 1)], kvm[:, :], start=True, stop=True)
                    last.then_inc(s("a0_num"), 1)
                transposes(lambda t: y[:, t, :], 0, (T // 2) * i + T // 2 - 1, s("a0_y"), s("a0_t3"))
                pe.wait_ge(s("a0_yT"), 2 * i + 2)
                for half in range(2):
                    for t in range(4):
                        k = 4 * half + t
                        last = biased(banks[2 + half][:, D * t:D * (t + 1)], qT[:, P * k:P * (k + 1)],
                                      WA[0][:, 3 * D:4 * D], R_O0, D)
                    last.then_inc(s("a0_o"), 1)
                transposes(lambda t: xn2[:, t, :], 0, i, s("a0_ln2"), s("a0_t4"))
                pe.wait_ge(s("a0_x2T"), 2 * i + 2)
                for t in tiles:
                    last = pe.matmul(banks[7][:, E * t:E * (t + 1)], xnT[:, P * t:P * (t + 1)], WG[0][:, :],
                                     start=True, stop=True)
                last.then_inc(s("a0_gate"), 1)
                routing_sums(0, i, s("a0_mask"), s("a0_pre"), 7)
            each_sequence(pe, sequence)
            experts(0)
            def body(i):
                def step(r, stage):
                    def scores(i, t):
                        need(pe, s("a1_splitT"), i, t + 1, 2)
                        need(pe, s("a1_sqr"), i, t)
                        need(pe, s("a1_xT"), i, t + 4)
                        need(pe, s("a1_qT"), i, t + 1)
                        need(pe, s("a1_gcopy"), i, t - 3 + (t == 2))
                        for g in range(4):
                            for hh in range(4):
                                last = pe.matmul(banks[hh][:, P * g:P * (g + 1)],
                                                 splitT[32 * hh:32 * hh + 32, t % 2, 4 + g, :],
                                                 splitT[32 * hh:32 * hh + 32, t % 2, g, :], start=True, stop=True)
                        last.then_inc(s("a1_qk"), 1)

                    def mix(i, t):
                        need(pe, s("a1_feat"), i, t + 1)
                        need(pe, s("a1_x1"), i, t)
                        if t > 0:
                            wait_earlier(pe, s("a1_state"), (T - 1) * i + t)
                            for d in range(NDIFF):
                                pe.matmul(banks[6][:, 0:P], state[:, d, :], feats[:, t % 4, d, :],
                                          start=(d == 0), stop=False, skip_group_check=True)
                        need(pe, s("a1_mask"), i, t + 1)
                        need(pe, s("a1_vpad"), i, t + 1)
                        for hh in range(4):
                            for g in range(4):
                                last = pe.matmul(banks[6][32 * g:32 * g + 32, 0:P], vpad[:, t % 2, 4 * g + hh, :],
                                                 score[:, t % 2, hh, g, :], start=(t == 0 and hh == 0),
                                                 stop=(hh == 3), skip_group_check=True)
                        last.then_inc(s("a1_z"), 1)

                    def add_state(i, t):
                        if t == T - 1:
                            return
                        need(pe, s("a1_prod"), i, t + 1)
                        wait_earlier(pe, s("a1_state"), (T - 1) * i + t)
                        for d in range(NDIFF):
                            for g in range(4):
                                last = pe.matmul(banks[7][32 * g:32 * g + 32, 32 * d:32 * d + 32],
                                                 prods[:, t % 4, d, 32 * g:32 * g + 32],
                                                 val[:, t, 32 * g:32 * g + 32],
                                                 start=(t == 0 and d == 0), stop=True, skip_group_check=True)
                        last.then_inc(s("a1_st"), 1)

                    def qkv(i, t):
                        need(pe, s("a1_xT"), i, t + 1)
                        need(pe, s("a1_splitT"), i, t - 3, 2, 1)
                        biased(banks[4][:, 0:3 * D], x1T[:, t % 2, :], WA[1][:, 0:3 * D], R_QKV1, 3 * D)\
                            .then_inc(s("a1_qkv"), 1)

                    def shifts(i, t):
                        need(pe, s("a1_qT"), i, t + 1)
                        need(pe, s("a1_splitT"), i, t + 1, 2)
                        if t == 2:
                            wait_earlier(pe, s("a1_idx2"), i)
                        for d in range(1, NDIFF):
                            last = pe.matmul(banks[5][:, P * (d - 1):P * d],
                                             K[:, C_SHIFT + P * (d - 1):C_SHIFT + P * d], qT1[:, t % 2, :],
                                             start=True, stop=True)
                        last.then_inc(s("a1_ph"), 1)

                    def project(i, t):
                        need(pe, s("a1_zT"), i, t + 1)
                        pe.matmul(banks[6][:, P:2 * P], zT[:, :], WA[1][:, 3 * D:4 * D], start=True, stop=True)\
                            .then_inc(s("a1_o"), 1)

                    def flip_x1(i, t):
                        need(pe, s("a1_ln1"), i, t + 1)
                        need(pe, s("a1_sqr"), i, t - 3)
                        pe.transpose(banks[2][:, 0:P], xn[:, t, :], ident).then_inc(s("a1_t1"), 1)

                    def flip_q(i, t):
                        need(pe, s("a1_rope"), i, t + 1)
                        need(pe, s("a1_sqr"), i, t)
                        pe.transpose(banks[3][:, 0:P], qk[:, t, 0:D], ident).then_inc(s("a1_plain"), 1)

                    def flip_split(i, t):
                        need(pe, s("a1_split"), i, t + 1)
                        for side in range(2):
                            if side == 0:
                                need(pe, s("a1_qv"), i, t + 3)
                            else:
                                need(pe, s("a1_feat"), i, t)
                            for g in range(4):
                                last = pe.transpose(banks[4 + side][:, P * g:P * (g + 1)],
                                                    split[:, side, 4 * g:4 * g + 4, :, :]
                                                    .rearrange("p h c d -> p (h c d)").bitcast(fp32), ident)
                            last.then_inc(s("a1_splitT_ps"), 1)

                    stage(2, scores)
                    stage(1, mix)
                    stage(1, add_state)
                    stage(5, qkv)
                    stage(2, shifts)
                    if r > 0:
                        stage(-1, flip_x2)
                    stage(1, project)
                    stage(6, flip_x1)
                    stage(3, flip_q)
                    if r > 0:
                        stage(-1, gates)
                    stage(3, flip_split)

                def flip_x2(i, t):
                    need(pe, s("a1_ln2"), i, t + 1)
                    need(pe, s("a1_sqr"), i, t + 3 + (t < T - 1))
                    pe.transpose(banks[0][:, 0:P], xn2[:, t, :], ident).then_inc(s("a1_t4"), 1)

                def gates(i, t):
                    need(pe, s("a1_x2T"), i, t + 1)
                    biased(banks[1][:, 0:E], x2T[:, :], WG[1][:, :], R_GATE, E).then_inc(s("a1_gate"), 1)

                stream(i, step)
                if not isinstance(i, int) or i >= 0:
                    flip_x2(i, T - 1)
                    gates(i, T - 1)
                    need(pe, s("a1_splitT"), i, T + 3, 2)
                    routing_sums(1, i, s("a1_mask2"), s("a1_pre"), 5)
            each_body(pe, body)
            experts(1)


def constants():
    import numpy as np
    f = np.float32
    p = np.arange(P)
    same = (p[:, None] // DH == p[None, :] // DH).astype(f)
    eye = np.eye(P, dtype=f)
    state = [same / DH ** 2] * (NDIFF - 1) + [same / (2 * DH ** 2)]
    head = p // DH * DH
    shift = [eye + (p[:, None] == (head + (p + d) % DH)[None, :]) for d in range(1, NDIFF)]
    inv = f(1.0) / f(10000.0) ** (np.arange(0, DH, 2, dtype=f) / f(DH))
    angle = np.outer(np.arange(SEQ, dtype=f), inv).astype(f)
    angle = np.concatenate([angle, angle], -1).reshape(T, P, DH).transpose(1, 0, 2)
    sign = np.where(np.arange(DH) % 2 == 0, -1.0, 1.0).astype(f)

    def rows(a):
        return np.broadcast_to(np.asarray(a, f), (P, len(a)))

    parts = [eye, same, (p[:, None] < p[None, :]).astype(f), *state, *shift,
             (p[:, None] // DH == np.arange(H)[None, :]).astype(f),
             rows(E - np.arange(E)), rows(np.arange(E) * REGION),
             np.cos(angle).reshape(P, T * DH), (np.sin(angle) * sign).reshape(P, T * DH),
             rows(np.arange(ROUTED))]
    return np.ascontiguousarray(np.concatenate(parts, 1), dtype=f)


def kernel(**inputs):
    import numpy as np
    import concourse.bacc as bacc
    from concourse.bass_utils import run_bass_kernel_spmd

    w = {k: np.asarray(v) for k, v in inputs.items()}
    cat = np.concatenate

    def attn(layer):
        return cat([w[f"L{layer}_attn_W{m}"].T for m in "qkvo"], 1)

    def columns(b):
        return b.reshape(-1, FF // P, P).transpose(0, 2, 1)

    w1 = cat([w["L1_ffn_spec_w1"], w["L1_ffn_shared_w1"][None]])
    b1 = cat([w["L1_ffn_spec_b1"], w["L1_ffn_shared_b1"][None]])
    w2 = cat([w["L1_ffn_spec_w2"], w["L1_ffn_shared_w2"][None]])
    laid = {
        "x_in": w["L0_attn_x"].reshape(TOKENS, D),
        "consts": constants(),
        "bias_row": cat([w["L0_attn_bq"], w["L0_attn_bk"], w["L0_attn_bv"], w["L0_attn_bo"],
                         w["L1_attn_bq"], w["L1_attn_bk"], w["L1_attn_bv"], w["L1_ffn_router_b"]])[None],
        "w_attn0": attn(0),
        "w_attn1": attn(1),
        "w_gate": np.stack([w["L0_ffn_Wg"].T, w["L1_ffn_router_w"].T]),
        "w_out0": w["L0_ffn_Wo"].T,
        "w_exp0": cat([w["L0_ffn_W1"].transpose(0, 2, 1), columns(w["L0_ffn_b1"])], 2),
        "w_exp1": cat([w1.transpose(0, 2, 1), columns(b1),
                       w2.reshape(E + 1, D, FF // P, P).transpose(0, 3, 2, 1).reshape(E + 1, P, FF)], 2),
        "b_out0": w["L0_ffn_bo"],
        "b_out1": cat([w["L1_ffn_spec_b2"], w["L1_ffn_shared_b2"][None]]),
        "norm_w": w["L1_attn_norm_w"],
    }
    nc = bacc.Bacc("TRN2", target_bir_lowering=False, num_devices=1)
    arrays, args = {}, []
    for name, a in laid.items():
        arrays[name] = np.ascontiguousarray(a)
        args.append(nc.dram_tensor(name, a.shape, mybir.dt.from_np(a.dtype), kind="ExternalInput").ap())
    fp32 = mybir.dt.float32
    out = nc.dram_tensor("out", (TOKENS, D), fp32, kind="ExternalOutput").ap()
    xs = [nc.dram_tensor(f"xs{n}", (DUMMY + ROWS + n * TOKENS, D), fp32, kind="Internal").ap() for n in range(2)]
    ys = [nc.dram_tensor(f"ys{n}", (Y_SHARED + n * TOKENS, D), fp32, kind="Internal").ap() for n in range(2)]
    program(nc, *args, out, xs, ys)
    r = run_bass_kernel_spmd(nc, [arrays], core_ids=[0])
    return r.results[0]["out"].reshape(SEQS, SEQ, D)
```

```python
import itertools
from contextlib import ExitStack

import concourse.bass as bass
from concourse import mybir
from concourse.alu_op_type import AluOpType as ALU

P = 128
D = 128
SEQS, SEQ = 8, 1024
TOKENS = SEQS * SEQ
T = SEQ // P
H, DH = 16, 8
E = 8
FF = 512
ROWS = 256
UNROLL = 4
REGION = TOKENS + ROWS
ROUTED = 2 * TOKENS // ROWS + E
SHARED = TOKENS // ROWS
DUMMY = E * REGION
X1_SHARED = DUMMY + ROWS
FIRST = (0, SHARED)
PACK = (E, E + 1)
NDIFF = 5

C_IDENT, C_BLOCK, C_PREFIX, C_STATE = 0, 128, 256, 384
C_SHIFT = C_STATE + NDIFF * 32
C_HEAD = C_SHIFT + 4 * 128
C_RANK = C_HEAD + H
C_BASE = C_RANK + E
C_EXPERT = C_BASE + E
C_COS = C_EXPERT + E
C_SIN = C_COS + T * DH
C_JOB = C_SIN + T * DH
JOBS = (ROUTED, ROUTED + SHARED)
NC_COLS = C_JOB + ROUTED

R_QKV0, R_O0, R_QKV1, R_GATE = 0, 384, 512, 896
NR_COLS = R_GATE + E
EPS = 1e-5


def program(nc, x_in, consts, bias_row, w_attn0, w_attn1, w_gate, w_out0, w_exp0, w_exp1, b_out0, b_out1,
            norm_w, out, xs, ys):
    fp32, bf16, i32 = mybir.dt.float32, mybir.dt.bfloat16, mybir.dt.int32
    f32r = mybir.dt.float32r
    ACT, AX = mybir.ActivationFunctionType, mybir.AxisListType

    def flat(a):
        return a.rearrange("p a d -> p (a d)")

    def at(i, n):
        return slice(i, i + n) if isinstance(i, int) else bass.DynSlice(i, n)

    with ExitStack() as ctx:
        def sb(name, shape, dt=fp32):
            return ctx.enter_context(nc.sbuf_tensor(name, shape, dt))

        def sem(name):
            return ctx.enter_context(nc.semaphore(name))

        X = sb("X", [P, SEQS * T, D])
        K = sb("K", [P, NC_COLS])
        WA = [sb(f"WA{n}", [P, 4 * D]) for n in range(2)]
        WG = [sb(f"WG{n}", [P, E]) for n in range(2)]
        brow = sb("brow", [3, NR_COLS], bf16)
        ones3 = sb("ones3", [3, P], bf16)
        prefix16 = sb("prefix16", [P, P], bf16)
        ones16 = sb("ones16", [P, P], bf16)
        gains = sb("gains", [P, T * SEQS, 2])
        places = sb("places", [P, T * SEQS, 2])
        carry = [sb(f"carry{n}", [P, E]) for n in range(2)]
        table = [sb(f"table{n}", [1, JOBS[n]], i32) for n in range(2)]
        padrow = [sb(f"padrow{n}", [1, E], i32) for n in range(2)]
        zeros = sb("zeros", [P, ROWS // P, D])
        ropeC = sb("ropeC", [P, T, DH])
        ropeS = sb("ropeS", [P, T, DH])
        wn = sb("wn", [P, DH])
        ident = K[:, C_IDENT:C_IDENT + P]
        block = K[:, C_BLOCK:C_BLOCK + P]

        xn = sb("xn", [P, T, D])
        xnT = sb("xnT", [P, T * P])
        qk = sb("qk", [P, T, 2 * D])
        val = sb("val", [P, T, D + 1])
        qT = sb("qT", [P, T * P])
        y = sb("y", [P, T, D])
        xn2 = sb("xn2", [P, T, D])
        kvm = sb("kvm", [P, D + H])
        stats = sb("stats", [P, 2 * T, 6])
        mv = sb("mv", [P, 2 * T, 2])
        rs = sb("rs", [P, 3, 2 * T])
        mx = sb("mx", [P, 2, 2 * H])
        den = sb("den", [P, T, H])
        lg = sb("lg", [P, 6, T, E])
        lr = sb("lr", [P, 8, T])
        mask16 = sb("mask16", [P, T, E], bf16)
        idx = sb("idx", [P, T, 2], i32)
        idx2 = sb("idx2", [P, T, 2], i32)
        place = sb("place", [P, 4, 2], i32)
        gcur = sb("gcur", [P, T, 2])
        got = sb("got", [P, T, 2, D])
        moments = sb("moments", [P, 2, 2, 2])
        stds = sb("stds", [P, 2, 2])
        bn1 = sb("bn1", [P, 2, 6])
        bn2 = sb("bn2", [P, 2, 6])
        eps1 = sb("eps1", [P, 1])
        eps_head = sb("eps_head", [P, 1])
        x1T = xnT[:, :].rearrange("p (t c) -> p t c", t=T)
        x2T = sb("x2T", [P, P])
        sq = sb("sq", [P, 2, 2 * D])
        hsum = sb("hsum", [P, 4, 2 * H])
        hstd = sb("hstd", [P, 4, 2 * H])
        hrec = sb("hrec", [P, 3, 2 * H])
        recs = sb("recs", [P, 3, 2])
        turned = sb("turned", [P, 2, 2 * D])
        scaled = sb("scaled", [P, 2, 2 * D])
        ksum = sb("ksum", [P, 2, H])
        cyclic = sb("cyclic", [P, 2, H, DH + NDIFF - 1])
        split = sb("split", [P, 2, H, 4, DH], f32r)
        keysT = sb("keysT", [P, 4, P], f32r)
        queriesT = sb("queriesT", [P, 4, 4, P], f32r)
        qT1 = sb("qT1", [P, 2, P])
        state = sb("state", [P, NDIFF, 32])
        score = sb("score", [P, 2, 4, 4, P])
        vpad = sb("vpad", [P, T, 4, 160])
        zT = sb("zT", [P, P])
        logits = sb("logits", [P, 2, E])
        best = sb("best", [P, 2, 8])
        best_at = sb("best_at", [P, 2, 8], mybir.dt.uint32)
        chosen = sb("chosen", [P, 2, 2])
        hot = sb("hot", [P, 4, 2, E])
        sums_sb = sb("sums_sb", [P, 2, 2 * E])
        ahead = sb("ahead", [P, E])
        picked = sb("picked", [P, 2, E])
        rows1 = sb("rows1", [P, 2])
        behind = sb("behind", [P, TOKENS // P])
        WT = [sb(f"WT{m}", [P, 2 * FF + 4]) for m in range(UNROLL)]
        BT = [sb(f"BT{m}", [P, D]) for m in range(UNROLL)]
        XT = [sb(f"XT{u}", [P, ROWS // P, D]) for u in range(2)]
        HT = [sb(f"HT{u}", [P, 4, ROWS]) for u in range(2)]
        SG = [sb(f"SG{u}", [P, 2, ROWS]) for u in range(2)]
        YT = [sb(f"YT{u}", [P, ROWS // P, D]) for u in range(2)]

        banks = [ctx.enter_context(nc.psum_tensor(f"bank{n}", [P, 512], fp32)) for n in range(8)]

        prods = [WT[m][:, 0:NDIFF * D].rearrange("p (d c) -> p d c", d=NDIFF) for m in range(4)]
        feats = [a[:, 0:NDIFF * P].rearrange("p (d c) -> p d c", d=NDIFF)
                 for a in (flat(HT[0][:, :, :]), flat(HT[1][:, :, :]), flat(y[:, :, :]), qT[:, :])]

        gots = (got, qk[:, :, :].rearrange("p t (c d) -> p t c d", c=2))
        shared = (y[:, :, :], xn[:, :, :])
        own_gains = (gcur, stats[:, 0:T, 0:2])
        at_rows = (idx, idx2)

        columns_ = split[:, :, :, :, :].rearrange("p a h k d -> p (a h k d)").bitcast(fp32)
        XC = [columns_[:, ROWS * u:ROWS * (u + 1)] for u in range(2)]

        S = {}

        def s(name):
            if name not in S:
                S[name] = sem(name)
            return S[name]

        for name in ("const_in rope_in w_in bias_in bias_split bias_rows setup_done zeroed "
                     "a0_x a0_ln1 a0_t1 a0_xT a0_qkv a0_qsub a0_v a0_exp a0_t2 a0_qT a0_kv a0_kvm "
                     "a0_num a0_y a0_t3 a0_yT a0_o a0_x1 a0_ln2 a0_t4 a0_x2T a0_gate a0_dmax "
                     "a0_p a0_mask a0_pre a0_idx a0_scat "
                     "a1_place a1_got0 a1_got1 a1_mv a1_std a1_ln1 a1_t1 a1_xT a1_qkv a1_qv a1_hsum a1_hstd a1_rope a1_high a1_plain "
                     "a1_qT a1_ph a1_feat a1_split a1_splitT_ps a1_splitT a1_prod a1_qk a1_sqr a1_mask a1_z "
                     "a1_zT a1_st a1_state a1_o a1_x1 a1_var2 a1_ln2 a1_t4 a1_x2T a1_gate a1_gcopy a1_gap "
                     "a1_p a1_mask2 a1_sums a1_scopy a1_idx2 "
                     "a1_scat0 a1_scat1 a1_scat2 a1_scat3 a1_scat4 a1_scat5 a1_scat6 a1_scat7 "
                     "a1_nat0 a1_nat1 a1_nat2 a1_nat3 "
                     "c_idx0 c_idx1 c_got0 c_got1 c_sh0 c_sh1 c_out0 c_out1 c_store").split():
            s(name)
        for n in range(2):
            for name in "table pads".split():
                s(f"{name}{n}")
            for name in "x xt cols h sig act y ysb st".split():
                for u in range(2):
                    s(f"b{n}_{name}{u}")
            for m in range(UNROLL):
                s(f"b{n}_w{m}")
        words = [sb(f"word{n}", [1, 128]) for n in range(2)]
        spots = itertools.count(1)
        block_ = ctx.enter_context(nc.Block())

        def rsqrt(v, work):
            r, a, t = work[:, 0], work[:, 1], work[:, 2]
            v.tensor_scalar(r.bitcast(i32), a.bitcast(i32), 1, None, ALU.logical_shift_right)
            v.drain()
            v.tensor_scalar(r.bitcast(i32), r.bitcast(i32), -1.0, float(0x5F3759DF), ALU.mult, ALU.add)
            for _ in range(3):
                v.drain()
                v.scalar_tensor_tensor(t, r, -0.5, r, ALU.mult, ALU.mult)
                v.drain()
                v.tensor_tensor(t, t, a, ALU.mult)
                v.drain()
                v.scalar_tensor_tensor(r, t, 1.5, r, ALU.add, ALU.mult)
            v.drain()

        def wait_apart(eng, signal, value, settle=True):
            if settle:
                eng.drain()
            word, n = words[eng is not nc.vector], next(spots)
            eng.wait_ge(signal, value)
            eng.tensor_tensor(word[:, n:n + 1], word[:, 0:1], word[:, 0:1], ALU.add)

        def every_group(eng, jobs, run):
            run(0, True, False)
            with eng.Fori(1, jobs // UNROLL - 1) as i:
                run(i, False, False)
            run(jobs // UNROLL - 1, False, True)

        def each_sequence(eng, run):
            run(0)
            with eng.Fori(1, SEQS) as i:
                run(i)

        def by_pairs(eng, pair):
            with eng.Fori(0, SEQS // 2 - 1) as j:
                pair(j, False)
            pair(SEQS // 2 - 1, True)

        def use(i, m):
            return 2 * i + m // 2

        def after(i, m):
            return (i, m + 1) if m + 1 < UNROLL else (i + 1, 0)

        def before(i, m):
            return (i, m - 1) if m > 0 else (i - 1, UNROLL - 1)

        def wait_earlier(eng, signal, value):
            if not isinstance(value, int) or value > 0:
                eng.wait_ge(signal, value)

        def stream(i, run):
            for r in range(T):
                def stage(lead, work, r=r):
                    seq, t = i + (r + lead) // T, (r + lead) % T
                    if not isinstance(seq, int) or 0 <= seq < SEQS:
                        work(seq, t)
                run(r, stage)

        def each_body(eng, body):
            body(-1)
            body(0)
            with eng.Fori(1, SEQS - 1) as i:
                body(i)
            body(SEQS - 1)
            body(SEQS)

        def need(eng, signal, i, n, each=1, more=0):
            value = each * (T * i + n) + more
            wait_earlier(eng, signal, min(value, each * TOKENS // P) if isinstance(value, int) else value)

        def need_apart(eng, signal, i, n, each=1):
            value = each * (T * i + n)
            if not isinstance(value, int):
                wait_apart(eng, signal, value, settle=False)
            elif value > 0:
                eng.wait_ge(signal, value)

        def values_of(t):
            return vpad[:, t, :, :].rearrange("p g (h c) -> p g h c", c=40)[:, :, :, 0:DH]

        def scattered(n):
            return [(s("a0_scat"), 32 * T)] if n == 0 else [(s(f"a1_scat{t}"), 32) for t in tiles]

        def each_pair(eng, body):
            body(-1, False, True)
            body(0, True, True)
            with eng.Fori(1, SEQS - 1) as i:
                body(i, True, True)
            body(SEQS - 1, True, False)

        def spread(a):
            return a.unsqueeze(2).broadcast_to([P, T, E])

        rank = K[:, C_RANK:C_RANK + E].unsqueeze(1).broadcast_to([P, T, E])

        def routing(v, i, gates, beside):
            dmax, p_ready, mask, pre, idx_ready = (s(f"a0_{k}") for k in ("dmax", "p", "mask", "pre", "idx"))
            prob, hot1, hot2, pos, tmp = (lg[:, k] for k in range(5))
            v.wait_ge(s("a0_gate"), i + 1)
            v.tensor_reduce(lr[:, 0, :], gates, AX.X, ALU.max)
            v.drain()
            v.tensor_tensor(tmp, gates, spread(lr[:, 0, :]), ALU.subtract).then_inc(dmax, 1)
            beside(0)
            v.wait_ge(p_ready, i + 1)
            v.tensor_reduce(lr[:, 1, :], prob, AX.X, ALU.add)
            v.scalar_tensor_tensor(tmp, prob, 1.0, rank, ALU.is_equal, ALU.mult)
            v.drain()
            v.tensor_reduce(lr[:, 3, :], tmp, AX.X, ALU.max)
            beside(1)
            v.drain()
            v.tensor_tensor(hot1, rank, spread(lr[:, 3, :]), ALU.is_equal)
            beside(2)
            v.drain()
            v.scalar_tensor_tensor(pos, hot1, -2.0, prob, ALU.mult, ALU.add)
            beside(3)
            v.drain()
            v.tensor_reduce(lr[:, 2, :], pos, AX.X, ALU.max)
            beside(4)
            v.drain()
            v.tensor_tensor(tmp, pos, spread(lr[:, 2, :]), ALU.is_equal)
            v.tensor_scalar(lr[:, 4, :], lr[:, 2, :], 1.0, None, ALU.add)
            beside(5)
            v.drain()
            v.tensor_tensor(tmp, tmp, rank, ALU.mult)
            v.scalar_tensor_tensor(lr[:, 5, :], lr[:, 1, :], 1e-9, lr[:, 4, :], ALU.mult, ALU.add)
            beside(6)
            v.drain()
            v.tensor_reduce(lr[:, 3, :], tmp, AX.X, ALU.max)
            v.reciprocal(lr[:, 6, :], lr[:, 5, :])
            beside(7)
            v.drain()
            v.tensor_tensor(hot2, rank, spread(lr[:, 3, :]), ALU.is_equal)
            v.tensor_copy(gains[:, at(T * i, T), 0], lr[:, 6, :])
            v.tensor_tensor(gains[:, at(T * i, T), 1], lr[:, 6, :], lr[:, 2, :], ALU.mult)
            beside(8)
            v.drain()
            v.tensor_tensor(mask16[:, :, :], hot1, hot2, ALU.add).then_inc(mask, 1)
            beside(9)
            v.drain()
            beside(10)
            v.drain()
            beside(11)
            v.wait_ge(pre, i + 1)
            v.tensor_tensor(pos, banks[7][:, 256:256 + T * E].rearrange("p (t e) -> p t e", e=E),
                            carry[0][:, :].unsqueeze(1).broadcast_to([P, T, E]), ALU.add)
            v.drain()
            v.tensor_tensor(carry[0][:, :], carry[0][:, :], banks[7][:, 320:320 + E], ALU.add)
            v.tensor_tensor(hot1, hot1, pos, ALU.mult)
            v.tensor_tensor(hot2, hot2, pos, ALU.mult)
            beside(12)
            v.drain()
            v.tensor_reduce(lr[:, 4, :], hot1, AX.X, ALU.add)
            v.tensor_reduce(lr[:, 5, :], hot2, AX.X, ALU.add)
            beside(13)
            v.drain()
            for signal, count in scattered(0):
                wait_earlier(v, signal, count * i)
            v.tensor_copy(idx[:, :, 0], lr[:, 4, :])
            v.tensor_copy(idx[:, :, 1], lr[:, 5, :])
            beside(14)
            v.drain()
            v.tensor_copy(places[:, at(T * i, T), :], idx[:, :, :]).then_inc(idx_ready, 1)
            beside(15)

        def make_table(v, n):
            cnt, til, cum, gap = (lr[:, k, :] for k in range(4))
            whole = lr[:, 4, :].bitcast(i32)
            jobs = K[0:1, C_JOB:C_JOB + ROUTED]
            v.drain()
            v.tensor_tensor(cnt, carry[n][:, :], K[:, C_BASE:C_BASE + E], ALU.subtract)
            v.drain()
            v.tensor_scalar(whole, cnt, ROWS - 1.0, None, ALU.add)
            v.drain()
            v.tensor_scalar(whole, whole, ROWS.bit_length() - 1, None, ALU.logical_shift_right)
            v.drain()
            v.tensor_copy(til, whole)
            v.drain()
            v.tensor_tensor_scan(cum, ones8[:, :], til, 0.0, ALU.mult, ALU.add)
            v.tensor_scalar(gap, til, -float(ROWS), float(REGION), ALU.mult, ALU.add)
            v.tensor_copy(padrow[n][:, :], carry[n][0:1, :])
            v.drain()
            v.tensor_tensor(lg2[:, :, :], jobs.unsqueeze(2).broadcast_to([1, ROUTED, E]),
                            cum[0:1, :].unsqueeze(1).broadcast_to([1, ROUTED, E]), ALU.is_ge)
            v.drain()
            v.tensor_reduce(jw[:, 0, :], lg2[:, :, :], AX.X, ALU.add)
            v.drain()
            v.tensor_tensor(lg2[:, :, :], lg2[:, :, :], gap[0:1, :].unsqueeze(1).broadcast_to([1, ROUTED, E]),
                            ALU.mult)
            v.drain()
            v.tensor_reduce(jw[:, 1, :], lg2[:, :, :], AX.X, ALU.add)
            v.drain()
            v.scalar_tensor_tensor(jw[:, 2, :], jobs, float(ROWS), jw[:, 1, :], ALU.mult, ALU.add)
            v.drain()
            v.tensor_scalar(jw[:, 2, :], jw[:, 2, :], float(DUMMY), PACK[n] / ROWS, ALU.min, ALU.mult)
            v.tensor_scalar(jw[:, 0, :], jw[:, 0, :], float(E - 1), None, ALU.min)
            v.drain()
            last = v.tensor_tensor(table[n][:, FIRST[n]:], jw[:, 2, :], jw[:, 0, :], ALU.add)
            last.then_inc(s(f"table{n}"), 1)
            flat_places = places[:, :, :].rearrange("p t c -> p (t c)")
            shifts = got[:, 0:E, 0, :]
            for e in range(1, E):
                v.tensor_scalar(shifts[:, e, :], flat_places, float(e * REGION), gap[:, e - 1:e], ALU.is_ge,
                                ALU.mult)
            for e in range(1, E):
                v.drain()
                if e == 1:
                    v.scalar_tensor_tensor(flat_places, flat_places, float(FIRST[n] * ROWS), shifts[:, 1, :],
                                           ALU.add, ALU.subtract)
                else:
                    v.tensor_tensor(flat_places, flat_places, shifts[:, e, :], ALU.subtract)
            v.drain()

        WA2 = sb("WA2", [P, 2, D])

        lg2 = sb("lg2", [1, ROUTED, E])
        jw = sb("jw", [1, 3, ROUTED])
        ones8 = sb("ones8", [P, E])
        tiles = range(T)

        @block_.sync
        def _(sp):
            def load_x(b):
                sp.dma_start(X[:, T * b:T * (b + 1), :], x_in[b * SEQ:(b + 1) * SEQ, :]
                             .rearrange("(t p) d -> p t d", p=P)).then_inc(s("a0_x"), 16)

            sp.dma_start(qk[0:1, 0:4, :].rearrange("p a d -> p (a d)")[:, 0:NR_COLS], bias_row)\
                .then_inc(s("bias_in"), 16)
            load_x(0)
            sp.dma_start(K[:, :], consts).then_inc(s("const_in"), 16)
            sp.dma_start(WA[0][:, :], w_attn0).then_inc(s("w_in"), 16)
            sp.dma_start(WA[1][:, :], w_attn1).then_inc(s("w_in"), 16)
            for n in range(2):
                sp.dma_start(WG[n][:, :], w_gate[n]).then_inc(s("w_in"), 16)
            sp.dma_start(WA2[:, :, :], w_out0.rearrange("(c p) d -> p c d", p=P)).then_inc(s("w_in"), 16)
            sp.dma_start(BT[0][:, :], b_out0.partition_broadcast(P)).then_inc(s("w_in"), 16)
            sp.dma_start(wn[:, :], norm_w.partition_broadcast(P)).then_inc(s("rope_in"), 16)
            sp.wait_ge(s("bias_split"), 1)
            parts = got[0:1, :, :, :].rearrange("p a c d -> p (a c d)").bitcast(bf16)
            for r in range(3):
                sp.dma_start(brow[r:r + 1, :], parts[:, r * NR_COLS:(r + 1) * NR_COLS])\
                    .then_inc(s("bias_rows"), 16)
            for b in range(1, SEQS):
                sp.wait_ge(s("a0_x"), 16 * b)
                load_x(b)
            for n in range(2):
                if n == 1:
                    def body(i):
                        def step(r, stage):
                            def store(i, t):
                                need(sp, s("a1_ln2"), i, t + 1)
                                sp.dma_start(xs[1][at(X1_SHARED + SEQ * i + P * t, P), :], xn2[:, t, :])\
                                    .then_inc(s(f"a1_nat{t % 4}"), 16)
                            stage(-3, store)
                        stream(i, step)
                    each_body(sp, body)
                def pad_routed():
                    sp.wait_ge(s(f"table{n}"), 1)
                    sp.wait_ge(s("zeroed"), 1)
                    for e in range(E):
                        row = sp.value_load(padrow[n][0:1, e:e + 1], min_val=0, max_val=DUMMY - ROWS)
                        sp.dma_start(xs[n][at(row, ROWS), :].rearrange("(a p) d -> p a d", p=P), zeros[:, :, :])\
                            .then_inc(s(f"pads{n}"), 16)
                    sp.dma_start(xs[n][DUMMY:DUMMY + ROWS, :].rearrange("(a p) d -> p a d", p=P), zeros[:, :, :])\
                        .then_inc(s(f"pads{n}"), 16)

                def routed_in_place():
                    sp.wait_ge(s(f"pads{n}"), 16 * (E + 1))
                    for signal, count in scattered(n):
                        sp.wait_ge(signal, count * SEQS)

                width = (FF + 4, 2 * FF + 4)[n]

                def load(i, m):
                    k, u = use(i, m), m % 2
                    entry = sp.value_load(table[n][0:1, at(UNROLL * i + m, 1)], min_val=0,
                                          max_val=(DUMMY, X1_SHARED + TOKENS - ROWS)[n] // ROWS * PACK[n] + E - 1 + n)
                    e = entry % PACK[n]
                    row = entry // PACK[n] * ROWS
                    wait_earlier(sp, s(f"b{n}_xt{u}"), k)
                    sp.dma_start(XT[u][:, :, :], xs[n][at(row, ROWS), :].rearrange("(a p) d -> p a d", p=P))\
                        .then_inc(s(f"b{n}_x{u}"), 16)
                    wait_earlier(sp, s(f"b{n}_ysb{u}"), k - 1)
                    sp.dma_start(WT[m][:, 0:width], (w_exp0, w_exp1)[n][at(e, 1), :, :].rearrange("a p f -> p (a f)"))\
                        .then_inc(s(f"b{n}_w{m}"), 16)
                    if n == 1:
                        sp.dma_start(BT[m][:, :], b_out1[at(e, 1), :].rearrange("a d -> (a d)").partition_broadcast(P))\
                            .then_inc(s(f"b{n}_w{m}"), 16)

                def load_group(i, first, last):
                    for m in range(UNROLL):
                        load(i, m)

                if n == 0:
                    pad_routed()
                    routed_in_place()
                    every_group(sp, JOBS[0], load_group)
                else:
                    sp.wait_ge(s("setup_done"), 1)
                    for m in range(4):
                        sp.wait_ge(s(f"a1_nat{m}"), 16 * SEQS * T // 4)
                    load_group(0, True, False)
                    with sp.Fori(1, SHARED // UNROLL // 2) as i:
                        load_group(i, False, False)
                    pad_routed()
                    with sp.Fori(SHARED // UNROLL // 2, SHARED // UNROLL) as i:
                        load_group(i, False, False)
                    routed_in_place()
                    with sp.Fori(SHARED // UNROLL, JOBS[1] // UNROLL) as i:
                        load_group(i, False, False)
            for u in range(2):
                sp.wait_ge(s(f"b1_st{u}"), 16 * (JOBS[1] // 2))
            def load_shared(j, u):
                sp.dma_start(shared[u], ys[1][at(SEQ * (2 * j + u), SEQ), :]
                             .rearrange("(t p) d -> p t d", p=P)).then_inc(s(f"c_sh{u}"), 16)

            def pair(j, last):
                for u in range(2):
                    sp.wait_ge(s(f"c_out{u}"), j + 1)
                    sp.dma_start(out[at(SEQ * (2 * j + u), SEQ), :].rearrange("(t p) d -> p t d", p=P),
                                 X[:, at(T * (2 * j + u), T), :]).then_inc(s("c_store"), 16)
                    if not last:
                        load_shared(j + 1, u)

            for u in range(2):
                load_shared(0, u)
            by_pairs(sp, pair)
            sp.wait_ge(s("c_store"), 16 * SEQS)

        @block_.gpsimd
        def _(g):
            g.memset(vpad[:, :, :, :].rearrange("p t g c -> p (t g c)"), 0.0)
            g.memset(words[1][:, :], 0.0)
            g.memset(zeros[:, :, :], 0.0).then_inc(s("zeroed"), 1)
            g.drain()

            def scatter(n, i, ready):
                wait_apart(g, ready, i + 1)
                for t in tiles:
                    for c in range(2):
                        g.indirect_dma_start(xs[n], bass.IndirectOffsetOnAxis(idx[:, t, c:c + 1], 0),
                                             xn2[:, t, :], None).then_inc(s(f"a{n}_scat"), 16)

            def store_all(n):
                def store_group(i, first, last):
                    for m in range(UNROLL):
                        k, u = use(i, m), m % 2
                        g.wait_ge(s(f"b{n}_ysb{u}"), k + 1)
                        g.dma_start(ys[n][at(ROWS * (UNROLL * i + m), ROWS), :].rearrange("(a p) d -> p a d", p=P), YT[u][:, :, :])\
                            .then_inc(s(f"b{n}_st{u}"), 16)

                every_group(g, JOBS[n], store_group)
                for u in range(2):
                    g.wait_ge(s(f"b{n}_st{u}"), 16 * (JOBS[n] // 2))

            def sequence(i):
                scatter(0, i, s("a0_idx"))
            each_sequence(g, sequence)
            g.memset(queriesT[:, :, :, :].rearrange("p g h c -> p (g h c)").bitcast(fp32), 0.0)\
                .then_inc(s("zeroed"), 1)
            store_all(0)
            def body(i):
                def step(r, stage):
                    def gather_tile(i, t):
                        need_apart(g, s("a1_place"), i, t + 1)
                        for c in range(2):
                            g.indirect_dma_start(got[:, t, c, :], None, ys[0],
                                                 bass.IndirectOffsetOnAxis(place[:, t % 4, c:c + 1], 0))\
                                .then_inc(s(f"a1_got{t % 2}"), 16)

                    def causal(i, t):
                        need_apart(g, s("a1_sqr"), i, t + 1)
                        all_scores = score[:, t % 2, :, :, :].rearrange("p a b c -> p (a b) c")
                        g.affine_select(out=all_scores, in_=all_scores, compare_op=ALU.is_ge, fill=0.0, base=0,
                                        pattern=[[0, H], [1, P]], channel_multiplier=-1)\
                            .then_inc(s("a1_mask"), 1)

                    def scatter_tile(i, t):
                        need_apart(g, s("a1_idx2"), i, t + 1)
                        for c in range(2):
                            g.indirect_dma_start(xs[1], bass.IndirectOffsetOnAxis(idx[:, t, c:c + 1], 0),
                                                 xn2[:, t, :], None).then_inc(s(f"a1_scat{t}"), 16)

                    stage(0, causal)
                    stage(8, gather_tile)
                    stage(-8, scatter_tile)
                stream(i, step)
            each_body(g, body)
            store_all(1)
            def pair(j, last):
                for u in range(2):
                    wait_apart(g, s(f"c_idx{u}"), j + 1, settle=(u == 0))
                    for t in tiles:
                        for c in range(2):
                            g.indirect_dma_start(gots[u][:, t, c, :], None, ys[1],
                                                 bass.IndirectOffsetOnAxis(at_rows[u][:, t, c:c + 1], 0))\
                                .then_inc(s(f"c_got{u}"), 16)
            by_pairs(g, pair)

        @block_.scalar
        def _(a):
            def experts(n):
                def act_group(i, first, last):
                    for m in range(UNROLL):
                        k, u = use(i, m), m % 2
                        for half in range(2):
                            hp = banks[2 + 2 * u + half][:, :].rearrange("p (c r) -> p c r", r=ROWS)
                            if n == 0 and half == 0:
                                continue
                            a.wait_ge(s(f"b{n}_h{u}"), 2 * k + half + 1)
                            if n == 0:
                                wait_earlier(a, s(f"b{n}_act{u}"), k)
                            elif half == 0:
                                wait_earlier(a, s(f"b{n}_y{u}"), k)
                            for c in range(2):
                                cc = 2 * half + c
                                bias = WT[m][:, FF + cc:FF + cc + 1]
                                if n == 0:
                                    last_ = a.activation(SG[u][:, c, :], hp[:, c, :], ACT.Sigmoid, bias=bias)
                                else:
                                    last_ = a.activation(HT[u][:, cc, :], hp[:, c, :], ACT.Gelu_apprx_tanh, bias=bias)
                            last_.then_inc(s(f"b{n}_{'sig' if n == 0 else 'act'}{u}"), 1)

                every_group(a, JOBS[n], act_group)

            def evac_pair(src, dst, wait, i, done, per=2):
                for half in range(2):
                    a.wait_ge(wait, per * i + half + 1)
                    a.activation(dst[:, 512 * half:512 * (half + 1)], banks[src + half][:, :], ACT.Copy)\
                        .then_inc(done, 1)

            def body(i, back, front):
                if back:
                    evac_pair(0, qT, s("a0_t3"), i, s("a0_yT"))
                    evac_pair(0, qT, s("a0_t4"), i, s("a0_x2T"))
                if front:
                    evac_pair(5, xnT, s("a0_t1"), i + 1, s("a0_xT"))
                if back:
                    a.wait_ge(s("a0_dmax"), i + 1)
                    a.activation(lg[:, 0], lg[:, 4], ACT.Exp).then_inc(s("a0_p"), 1)
                if front:
                    f = i + 1
                    for t in tiles:
                        a.wait_ge(s("a0_qsub"), T * f + t + 1)
                        a.activation(val[:, t, 0:D], banks[2 + t % 2][:, 2 * D:3 * D], ACT.Copy)\
                            .then_inc(s("a0_v"), 1)
                        if t % 4 == 3:
                            a.activation(qk[:, t - 3:t + 1, :], qk[:, t - 3:t + 1, :], ACT.Exp)\
                                .then_inc(s("a0_exp"), 1)
                    evac_pair(0, qT, s("a0_t2"), f, s("a0_qT"))
            each_pair(a, body)
            experts(0)
            a.wait_ge(s("zeroed"), 2)
            def copy(dst, src):
                return a.activation(dst, src, ACT.Copy)

            def body(i):
                def step(r, stage):
                    def roots():
                        if not isinstance(i, int) or 0 <= T * i + r + 7 < TOKENS // P + 9:
                            need(a, s("a1_mv"), i, r + 8)
                            need(a, s("a1_var2"), i, r - 1)
                            a.activation(stds[:, (r + 1) % 2, :], moments[:, (r + 1) % 2, :, 1], ACT.Sqrt,
                                         bias=eps1[:, :]).then_inc(s("a1_std"), 1)

                    def root_heads(i, t):
                        need(a, s("a1_hsum"), i, t + 1)
                        a.activation(hstd[:, t % 4, :], hsum[:, t % 4, :], ACT.Sqrt, bias=eps_head[:, :],
                                     scale=1.0 / DH).then_inc(s("a1_hstd"), 1)

                    def high(i, t):
                        need(a, s("a1_rope"), i, t + 1)
                        need(a, s("a1_prod"), i, t - 1)
                        k_ = qk[:, t, D:2 * D].rearrange("p (h d) -> p h d", d=DH)
                        copy(cyclic[:, t % 2, :, 0:DH], k_)
                        copy(cyclic[:, t % 2, :, DH:DH + NDIFF - 1], k_[:, :, 0:NDIFF - 1])
                        for side in range(2):
                            parts = split[:, side, :, 0:3:2, :] if side == 0 else split[:, side, :, 0:2, :]
                            x = qk[:, t, D * side:D * side + D].rearrange("p (h d) -> p h d", d=DH)
                            last = copy(parts, x.unsqueeze(2).broadcast_to([P, H, 2, DH]))
                        last.then_inc(s("a1_high"), 1)

                    def squares(i, t):
                        need(a, s("a1_qk"), i, t + 1)
                        for g in range(4):
                            last = a.activation(score[:, t % 2, g, :, :].rearrange("p h c -> p (h c)"),
                                                banks[g][:, :], ACT.Square, scale=1.0 / DH)
                        last.then_inc(s("a1_sqr"), 1)

                    def copy_z(i, t):
                        need(a, s("a1_z"), i, t + 1)
                        copy(zT[:, :], banks[6][:, 0:P]).then_inc(s("a1_zT"), 1)

                    def copy_qkv(i, t):
                        need(a, s("a1_qkv"), i, t + 1)
                        copy(qk[:, t, :], banks[4][:, 0:2 * D])
                        copy(values_of(t), banks[4][:, 2 * D:3 * D].rearrange("p (g h e) -> p g h e", g=4, h=4))
                        a.activation(sq[:, t % 2, :], banks[4][:, 0:2 * D], ACT.Square).then_inc(s("a1_qv"), 1)

                    def features(i, t):
                        need(a, s("a1_ph"), i, t + 1)
                        a.activation(feats[t % 4][:, 1:NDIFF, :].rearrange("p a b -> p (a b)"), banks[5][:, :],
                                     ACT.Square).then_inc(s("a1_feat"), 1)

                    def copy_x1(i, t):
                        need(a, s("a1_t1"), i, t + 1)
                        copy(x1T[:, t, :], banks[2][:, 0:P]).then_inc(s("a1_xT"), 1)

                    def copy_q(i, t):
                        need(a, s("a1_plain"), i, t + 1)
                        copy(qT1[:, t % 2, :], banks[3][:, 0:P])
                        a.activation(feats[t % 4][:, 0, :], banks[3][:, 0:P], ACT.Square).then_inc(s("a1_qT"), 1)

                    def copy_split(side):
                        def work(i, t):
                            need(a, s("a1_splitT_ps"), i, t, 2, side + 1)
                            for hh in range(4 if side == 0 else 0):
                                rows = slice(32 * hh, 32 * hh + 32)
                                last = copy(queriesT[rows, :, hh, :],
                                            banks[4][rows, :].rearrange("p (g c) -> p g c", g=4))
                            if side == 1:
                                last = copy(keysT[:, :, :].rearrange("p a b -> p (a b)"), banks[5][:, :])
                            last.then_inc(s("a1_splitT"), 1)
                        return work

                    stage(0, squares)
                    stage(4, root_heads)
                    stage(1, copy_split(0))
                    stage(1, copy_q)
                    stage(5, copy_x1)
                    stage(-4, copy_x2)
                    stage(-6, copy_sums)
                    stage(1, copy_split(1))
                    stage(-1, copy_z)
                    stage(2, high)
                    stage(5, copy_qkv)
                    stage(1, features)
                    stage(-4, copy_logits)
                    roots()

                def copy_sums(i, t):
                    need(a, s("a1_sums"), i, t + 1)
                    copy(sums_sb[:, t % 2, :], banks[1][:, 0:2 * E]).then_inc(s("a1_scopy"), 1)

                def copy_x2(i, t):
                    need(a, s("a1_t4"), i, t + 1)
                    copy(x2T[:, :], banks[0][:, 0:P]).then_inc(s("a1_x2T"), 1)

                def copy_logits(i, t):
                    need(a, s("a1_gate"), i, t + 1)
                    copy(logits[:, t % 2, :], banks[6][:, 2 * P:2 * P + E]).then_inc(s("a1_gcopy"), 1)

                stream(i, step)
            each_body(a, body)
            a.wait_ge(s("a1_gap"), 1)
            a.activation(gains[:, :, 1], behind[:, :], ACT.Exp).then_inc(s("a1_p"), 1)
            experts(1)

        @block_.vector
        def _(v):
            v.wait_ge(s("bias_in"), 16)
            raw = qk[0:1, 0:4, :].rearrange("p a d -> p (a d)")[:, 0:NR_COLS]
            parts = got[0:1, :, :, :].rearrange("p a c d -> p (a c d)").bitcast(bf16)
            rest = qk[0:1, 4:8, :].rearrange("p a d -> p (a d)")[:, 0:NR_COLS]
            for r in range(3):
                part = parts[:, r * NR_COLS:(r + 1) * NR_COLS]
                last = v.tensor_copy(part, raw if r == 0 else rest)
                if r < 2:
                    v.drain()
                    v.tensor_tensor(rest, raw if r == 0 else rest, part, ALU.subtract)
                    v.drain()
            last.then_inc(s("bias_split"), 1)
            v.memset(ones3[:, :], 1.0)
            v.memset(words[0][:, :], 0.0)
            v.memset(eps1[:, :], EPS)
            v.memset(moments[:, :, :, :], 1.0)
            v.memset(eps_head[:, :], 2.0 ** -23)
            v.memset(ones16[:, :], 1.0)
            v.memset(val[:, :, D:D + 1], 1.0)
            v.memset(ones8[:, :], 1.0)
            v.wait_ge(s("const_in"), 16)
            for n in range(2):
                v.tensor_copy(carry[n][:, :], K[:, C_BASE:C_BASE + E])
            v.tensor_scalar(table[1][:, 0:SHARED], K[0:1, C_JOB:C_JOB + SHARED], float(PACK[1]),
                            float(X1_SHARED // ROWS * PACK[1] + E), ALU.mult, ALU.add)
            v.tensor_copy(prefix16[:, :], K[:, C_PREFIX:C_PREFIX + P]).then_inc(s("setup_done"), 1)
            v.wait_ge(s("rope_in"), 16)
            v.wait_ge(s("w_in"), 16 * 6)
            v.tensor_tensor(ropeC[:, :, :], K[:, C_COS:C_COS + T * DH].rearrange("p (t d) -> p t d", d=DH),
                            wn[:, :].unsqueeze(1).broadcast_to([P, T, DH]), ALU.mult)
            sin = K[:, C_SIN:C_SIN + T * DH].rearrange("p (t j c) -> p t j c", j=4, c=2)
            ws = wn[:, :].rearrange("p (j c) -> p j c", c=2)
            rS = ropeS[:, :, :].rearrange("p t (j c) -> p t j c", c=2)
            for c in range(2):
                v.tensor_tensor(rS[:, :, :, c], sin[:, :, :, c],
                                ws[:, :, 1 - c].unsqueeze(1).broadcast_to([P, T, 4]), ALU.mult)
            v.wait_ge(s("bias_rows"), 48)
            v.wait_ge(s("zeroed"), 1)
            v.drain()
            heads = "p (h d) -> p h d"
            def body(i, back, front):
                f = i + 1
                if back:
                    nums = [banks[b][:, :].rearrange("p (a c) -> p a c", a=2) for b in (5, 6, 2, 3)]
                    for half in range(2):
                        pairs = (2 * half, 2 * half + 1)
                        for c in pairs:
                            v.wait_ge(s("a0_num"), (T // 2) * i + c + 1)
                            v.tensor_scalar(den[:, 2 * c:2 * c + 2, :], nums[c][:, :, D:D + H], 1e-6, None, ALU.add)
                        v.drain()
                        own = slice(4 * half, 4 * half + 4)
                        v.reciprocal(den[:, own, :], den[:, own, :])
                        v.drain()
                        for c in pairs:
                            v.tensor_tensor(y[:, 2 * c:2 * c + 2, :].rearrange("p a (h d) -> p a h d", d=DH),
                                            nums[c][:, :, 0:D].rearrange("p a (h d) -> p a h d", d=DH),
                                            den[:, 2 * c:2 * c + 2, :].unsqueeze(3).broadcast_to([P, 2, H, DH]),
                                            ALU.mult).then_inc(s("a0_y"), 1)
                if front:
                    wait_apart(v, s("a0_x"), 16 * f + 16)
                    for t in tiles:
                        v.bn_stats(stats[:, t, :], flat(X[:, at(T * f + t, 1), :]))
                    v.drain()
                    for t in tiles:
                        v.bn_aggr(mv[:, t, :], stats[:, t, :])
                if back:
                    for half in range(2):
                        v.wait_ge(s("a0_o"), 2 * i + half + 1)
                        rows = X[:, at(T * i + 4 * half, 4), :]
                        last = v.tensor_tensor(rows, rows,
                                               banks[2 + half][:, :].rearrange("p (a d) -> p a d", a=4), ALU.add)
                        if half == 1:
                            last.then_inc(s("a0_x1"), 1)
                        v.drain()
                        for t in range(4 * half, 4 * half + 4):
                            v.bn_stats(stats[:, T + t, :], flat(X[:, at(T * i + t, 1), :]))
                    v.drain()
                    for t in range(T, 2 * T):
                        v.bn_aggr(mv[:, t, :], stats[:, t, :])
                v.drain()
                own = slice(0 if front else T, 2 * T if back else T)
                v.tensor_scalar(rs[:, 1, own], mv[:, own, 1], EPS, None, ALU.add)
                v.drain()
                rsqrt(v, rs[:, :, own])
                if back:
                    if not isinstance(i, int) or i > 0:
                        wait_apart(v, s("a0_scat"), 16 * 2 * T * i)
                    for t in tiles:
                        last = v.tensor_scalar(xn2[:, t, :], flat(X[:, at(T * i + t, 1), :]), mv[:, T + t, 0:1],
                                               rs[:, 0, T + t:T + t + 1], ALU.subtract, ALU.mult)
                        if t % 4 == 3:
                            last.then_inc(s("a0_ln2"), 1)
                if front:
                    for t in tiles:
                        last = v.tensor_scalar(xn[:, t, :], flat(X[:, at(T * f + t, 1), :]), mv[:, t, 0:1],
                                               rs[:, 0, t:t + 1], ALU.subtract, ALU.mult)
                        if t % 4 == 3:
                            last.then_inc(s("a0_ln1"), 1)

                def less_maximum(k):
                    t = k // 2
                    if not front:
                        return
                    src = banks[2 + t % 2][:, 0:2 * D].rearrange(heads, d=DH)
                    if k % 2 == 0:
                        v.wait_ge(s("a0_qkv"), T * f + t + 1)
                        v.tensor_reduce(mx[:, t % 2, :], src, AX.X, ALU.max)
                    else:
                        v.tensor_tensor(qk[:, t, :].rearrange(heads, d=DH), src,
                                        mx[:, t % 2, :].unsqueeze(2).broadcast_to([P, 2 * H, DH]), ALU.subtract)\
                            .then_inc(s("a0_qsub"), 1)

                if back:
                    routing(v, i, banks[7][:, 0:T * E].rearrange("p (t e) -> p t e", e=E), less_maximum)
                else:
                    for k in range(2 * T):
                        less_maximum(k)
                        v.drain()
                if front:
                    v.wait_ge(s("a0_kv"), f + 1)
                    v.tensor_tensor(kvm[:, 0:D], banks[4][:, 0:D], block, ALU.mult)
                    v.tensor_scalar(kvm[:, D:D + H], K[:, C_HEAD:C_HEAD + H], banks[4][:, D:D + 1], None, ALU.mult)\
                        .then_inc(s("a0_kvm"), 1)
                v.drain()
            each_pair(v, body)

            def experts(n):
                def finish(i, m):
                    k, u = use(i, m), m % 2
                    v.wait_ge(s(f"b{n}_y{u}"), k + 1)
                    wait_earlier(v, s(f"b{n}_st{u}"), 16 * k)
                    bt = BT[0] if n == 0 else BT[m]
                    v.tensor_tensor(YT[u][:, :, :], banks[6 + u][:, 0:ROWS].rearrange("p (a d) -> p a d", d=D),
                                    bt[:, :].unsqueeze(1).broadcast_to([P, ROWS // P, D]), ALU.add)\
                        .then_inc(s(f"b{n}_ysb{u}"), 1)

                def gate(i, m):
                    k, u = use(i, m), m % 2
                    v.wait_ge(s(f"b{n}_sig{u}"), k + 1)
                    wait_earlier(v, s(f"b{n}_y{u}"), k)
                    hp = banks[2 + 2 * u][:, :].rearrange("p (c r) -> p c r", r=ROWS)
                    for c in range(2):
                        last = v.scalar_tensor_tensor(HT[u][:, c, :], hp[:, c, :], WT[m][:, FF + c:FF + c + 1],
                                                      SG[u][:, c, :], ALU.add, ALU.mult)
                    last.then_inc(s(f"b{n}_act{u}"), 1)

                def columns(i, m):
                    k, u = use(i, m), m % 2
                    v.wait_ge(s(f"b{n}_xt{u}"), k + 1)
                    wait_earlier(v, s(f"b{n}_h{u}"), 2 * k)
                    v.tensor_copy(XC[u], banks[u][:, 0:ROWS]).then_inc(s(f"b{n}_cols{u}"), 1)

                def dve_group(i, first, last):
                    if first:
                        columns(0, 0)
                    for m in range(UNROLL):
                        if not (last and m == UNROLL - 1):
                            columns(*after(i, m))
                        if n == 0:
                            gate(i, m)
                        if not (first and m == 0):
                            finish(*before(i, m))
                    if last:
                        finish(i, UNROLL - 1)

                every_group(v, JOBS[n], dve_group)

            make_table(v, 0)
            experts(0)
            v.drain()
            def newton(work, a_, eps, scale, k):
                r, e1, e2 = work[:, 0], work[:, 1], work[:, 2]
                if k == 0:
                    v.scalar_tensor_tensor(e1, a_, eps, r, ALU.add, ALU.mult)
                elif k == 1:
                    v.scalar_tensor_tensor(e2, e1, -0.5 / scale, r, ALU.mult, ALU.mult)
                else:
                    v.scalar_tensor_tensor(r, e2, 1.5, r, ALU.add, ALU.mult)

            def body(i):
                def step(r, stage):
                    layernorms = not isinstance(i, int) or 0 <= T * i + r + 6 < TOKENS // P + 9

                    def row(i, t):
                        return flat(X[:, at(T * i + t, 1), :])

                    def heads_of(a_):
                        return a_.rearrange("p (h d) -> p h d", d=DH)

                    def fetch(i, t):
                        v.tensor_copy(gcur[:, t, :], gains[:, at(T * i + t, 1), :].rearrange("p a c -> p (a c)"))
                        v.tensor_copy(place[:, t % 4, :], places[:, at(T * i + t, 1), :]
                                      .rearrange("p a c -> p (a c)")).then_inc(s("a1_place"), 1)

                    def add_expert(c):
                        def work(i, t):
                            if c == 0:
                                wait_earlier(v, s(f"a1_got{t % 2}"), 32 * (T // 2 * i + t // 2 + 1))
                            v.scalar_tensor_tensor(row(i, t), got[:, t, c, :], gcur[:, t, c:c + 1], row(i, t),
                                                   ALU.mult, ALU.add)
                        return work

                    def stats1(i, t):
                        v.bn_stats(bn1[:, t % 2, :], row(i, t))

                    def moments1(i, t):
                        v.bn_aggr(moments[:, t % 2, 0, :], bn1[:, t % 2, :]).then_inc(s("a1_mv"), 1)

                    def inverse():
                        if layernorms:
                            wait_earlier(v, s("a1_std"), T * i + r + 7)
                            v.reciprocal(recs[:, 0, :], stds[:, r % 2, :])

                    def newton_both(k):
                        if layernorms:
                            newton(recs, moments[:, r % 2, :, 1], EPS, 1, k)

                    def normalise1(i, t):
                        v.tensor_scalar(xn[:, t, :], row(i, t), moments[:, t % 2, 0, 0:1], recs[:, 0, 0:1],
                                        ALU.subtract, ALU.mult).then_inc(s("a1_ln1"), 1)

                    def sum_squares(i, t):
                        need(v, s("a1_qv"), i, t + 1)
                        v.tensor_reduce(hsum[:, t % 4, :], heads_of(sq[:, t % 2, :]), AX.X, ALU.add)\
                            .then_inc(s("a1_hsum"), 1)

                    def inverse_heads(i, t):
                        need(v, s("a1_hstd"), i, t + 1)
                        v.reciprocal(hrec[:, 0, :], hstd[:, t % 4, :])

                    def newton_heads(k):
                        return lambda i, t: newton(hrec, hsum[:, t % 4, :], DH * 2.0 ** -23, DH, k)

                    def scale_heads(i, t):
                        v.tensor_tensor(heads_of(qk[:, t, :]), heads_of(qk[:, t, :]),
                                        hrec[:, 0, :].unsqueeze(2).broadcast_to([P, 2 * H, DH]), ALU.mult)

                    def turn(i, t):
                        qh = qk[:, t, :].rearrange("p (h j c) -> p h j c", j=4, c=2)
                        th = turned[:, t % 2, :].rearrange("p (h j c) -> p h j c", j=4, c=2)
                        for c in range(2):
                            v.tensor_tensor(th[:, :, :, c], qh[:, :, :, 1 - c],
                                            ropeS[:, t, :].rearrange("p (j c) -> p j c", c=2)[:, :, c]
                                            .unsqueeze(1).broadcast_to([P, 2 * H, 4]), ALU.mult)
                        v.tensor_tensor(heads_of(scaled[:, t % 2, :]), heads_of(qk[:, t, :]),
                                        ropeC[:, t, :].unsqueeze(1).broadcast_to([P, 2 * H, DH]), ALU.mult)

                    def add_turned(i, t):
                        v.tensor_tensor(qk[:, t, :], scaled[:, t % 2, :], turned[:, t % 2, :], ALU.add)\
                            .then_inc(s("a1_rope"), 1)

                    def sum_k(i, t):
                        v.tensor_reduce(ksum[:, t % 2, :], heads_of(qk[:, t, D:2 * D]), AX.X, ALU.add)

                    def products(i, t):
                        need(v, s("a1_high"), i, t + 1)
                        window = cyclic[:, t % 2, :, 1:1 + DH].unsqueeze(1).broadcast_to([P, NDIFF - 1, H, DH])
                        steps = [list(step) for step in window.ap]
                        steps[1][0] = steps[3][0]
                        windows = bass.AP(window.tensor, window.offset, steps)
                        v.tensor_tensor(prods[t % 4][:, 1:NDIFF, :].rearrange("p d (h j) -> p d h j", j=DH),
                                        heads_of(qk[:, t, D:2 * D]).unsqueeze(1).broadcast_to([P, NDIFF - 1, H, DH]),
                                        windows, ALU.mult).then_inc(s("a1_prod"), 1)

                    def product0a(i, t):
                        v.scalar_tensor_tensor(heads_of(prods[t % 4][:, 0, :]), heads_of(qk[:, t, D:2 * D]), 2.0,
                                               ksum[:, t % 2, :].unsqueeze(2).broadcast_to([P, H, DH]),
                                               ALU.mult, ALU.subtract)

                    def product0b(i, t):
                        p0 = prods[t % 4][:, 0, :]
                        v.tensor_tensor(p0, p0, qk[:, t, D:2 * D], ALU.mult)

                    def low(i, t):
                        need(v, s("a1_high"), i, t + 1)
                        for side in range(2):
                            if side == 0:
                                dst, hi = split[:, 0, :, 1:4:2, :], split[:, 0, :, 0:3:2, :]
                            else:
                                dst, hi = split[:, 1, :, 2:4, :], split[:, 1, :, 0:2, :]
                            x = heads_of(qk[:, t, D * side:D * side + D]).unsqueeze(2).broadcast_to([P, H, 2, DH])
                            last = v.tensor_tensor(dst, x, hi, ALU.subtract)
                        last.then_inc(s("a1_split"), 1)

                    def new_state(i, t):
                        if t < T - 1:
                            wait_earlier(v, s("a1_st"), (T - 1) * i + t + 1)
                            need(v, s("a1_z"), i, t + 1)
                            v.tensor_tensor(state[:, :, :].rearrange("p d c -> p (d c)"),
                                            banks[7][:, 0:NDIFF * 32], K[:, C_STATE:C_STATE + NDIFF * 32],
                                            ALU.mult)\
                                .then_inc(s("a1_state"), 1)

                    def add_attention(i, t):
                        need(v, s("a1_o"), i, t + 1)
                        v.tensor_tensor(row(i, t), row(i, t), banks[6][:, P:2 * P], ALU.add)\
                            .then_inc(s("a1_x1"), 1)

                    def stats2(i, t):
                        v.bn_stats(bn2[:, t % 2, :], row(i, t))

                    def moments2(i, t):
                        v.bn_aggr(moments[:, (t + 1) % 2, 1, :], bn2[:, t % 2, :]).then_inc(s("a1_var2"), 1)

                    stage(8, fetch)
                    stage(-5, rank_experts)
                    stage(3, newton_heads(2))
                    stage(2, sum_k)
                    stage(4, sum_squares)
                    inverse()
                    stage(-2, add_attention)
                    stage(7, add_expert(0))
                    v.drain()
                    stage(7, add_expert(1))
                    newton_both(0)
                    stage(-2, stats2)
                    stage(-5, find_experts)
                    stage(-7, place_rows)
                    stage(2, product0a)
                    stage(3, scale_heads)
                    v.drain()
                    stage(7, stats1)
                    newton_both(1)
                    stage(-2, moments2)
                    stage(-5, experts_as_floats)
                    stage(-7, pick_rows)
                    stage(2, product0b)
                    stage(4, inverse_heads)
                    stage(3, turn)
                    v.drain()
                    stage(7, moments1)
                    newton_both(2)
                    stage(-5, flag_experts)
                    stage(-7, add_rows)
                    stage(3, add_turned)
                    stage(4, newton_heads(0))
                    v.drain()
                    stage(4, newton_heads(1))
                    stage(-1, new_state)
                    stage(6, normalise1)
                    stage(-5, add_flags)
                    stage(-7, keep_rows)
                    stage(-3, normalise2)
                    stage(2, products)
                    stage(2, low)
                    v.drain()

                def normalise2(i, t):
                    wait_earlier(v, s(f"a1_nat{t % 4}"), 16 * (2 * i + t // 4))
                    wait_earlier(v, s(f"a1_scat{t}"), 32 * i)
                    v.tensor_scalar(xn2[:, t, :], flat(X[:, at(T * i + t, 1), :]), moments[:, (t + 1) % 2, 1, 0:1],
                                    recs[:, 0, 1:2],
                                    ALU.subtract, ALU.mult).then_inc(s("a1_ln2"), 1)

                def rank_experts(i, t):
                    need_apart(v, s("a1_gcopy"), i, t + 1)
                    v.max(best[:, t % 2, :], logits[:, t % 2, :])

                def find_experts(i, t):
                    v.max_index(best_at[:, t % 2, :], best[:, t % 2, :], logits[:, t % 2, :])
                    v.tensor_tensor(behind[:, at(T * i + t, 1)], best[:, t % 2, 1:2], best[:, t % 2, 0:1], ALU.subtract)

                def experts_as_floats(i, t):
                    v.tensor_copy(chosen[:, t % 2, :], best_at[:, t % 2, 0:2])

                def flag_experts(i, t):
                    v.tensor_tensor(hot[:, t % 4, :, :],
                                    K[:, C_EXPERT:C_EXPERT + E].unsqueeze(1).broadcast_to([P, 2, E]),
                                    chosen[:, t % 2, :].unsqueeze(2).broadcast_to([P, 2, E]), ALU.is_equal)

                def add_flags(i, t):
                    v.tensor_tensor(mask16[:, t, :], hot[:, t % 4, 0, :], hot[:, t % 4, 1, :], ALU.add)\
                        .then_inc(s("a1_mask2"), 1)

                def place_rows(i, t):
                    need(v, s("a1_scopy"), i, t + 1)
                    v.tensor_tensor(ahead[:, :], sums_sb[:, t % 2, 0:E], carry[1][:, :], ALU.add)
                    v.tensor_tensor(carry[1][:, :], sums_sb[:, t % 2, E:2 * E], carry[1][:, :], ALU.add)

                def pick_rows(i, t):
                    v.tensor_tensor(picked[:, :, :], hot[:, t % 4, :, :],
                                    ahead[:, :].unsqueeze(1).broadcast_to([P, 2, E]), ALU.mult)

                def add_rows(i, t):
                    v.tensor_reduce(rows1[:, :], picked[:, :, :], AX.X, ALU.add)

                def keep_rows(i, t):
                    wait_earlier(v, s(f"a1_scat{t}"), 32 * i)
                    v.tensor_copy(places[:, at(T * i + t, 1), :].rearrange("p a c -> p (a c)"), rows1[:, :])
                    v.tensor_copy(idx[:, t, :], rows1[:, :]).then_inc(s("a1_idx2"), 1)

                stream(i, step)
            each_body(v, body)
            v.tensor_copy(behind[:, :], behind[:, :]).then_inc(s("a1_gap"), 1)
            v.wait_ge(s("a1_p"), 1)
            odds, first = gains[:, :, 1], gains[:, :, 0]
            v.tensor_scalar(first, odds, 1.0, None, ALU.add)
            v.drain()
            v.reciprocal(first, first)
            v.drain()
            v.tensor_tensor(odds, odds, first, ALU.mult)
            make_table(v, 1)
            experts(1)
            v.drain()
            def fetch_places(j, u):
                v.tensor_copy(at_rows[u][:, :, :], places[:, at(T * (2 * j + u), T), :]).then_inc(s(f"c_idx{u}"), 1)
                v.tensor_copy(own_gains[u][:, :, :], gains[:, at(T * (2 * j + u), T), :])

            def pair(j, last):
                for u in range(2):
                    rows = X[:, at(T * (2 * j + u), T), :]
                    v.wait_ge(s(f"c_sh{u}"), 16 * (j + 1))
                    v.tensor_tensor(rows, rows, shared[u], ALU.add)
                    v.drain()
                    v.wait_ge(s(f"c_got{u}"), 16 * 2 * T * (j + 1))
                    for c in range(2):
                        for t in tiles:
                            row = flat(X[:, at(T * (2 * j + u) + t, 1), :])
                            done = v.scalar_tensor_tensor(row, gots[u][:, t, c, :], own_gains[u][:, t, c:c + 1], row,
                                                          ALU.mult, ALU.add)
                        if c == 0:
                            v.drain()
                    done.then_inc(s(f"c_out{u}"), 1)
                    if not last:
                        v.drain()
                        fetch_places(j + 1, u)

            for u in range(2):
                fetch_places(0, u)
            v.drain()
            by_pairs(v, pair)
        @block_.tensor
        def _(pe):
            def transposes(src, bank0, i, per, ready, done, halves=range(2)):
                for half in halves:
                    pe.wait_ge(ready, per * i + per * (half + 1) // 2)
                    for t in range(4):
                        last = pe.transpose(banks[bank0 + half][:, P * t:P * (t + 1)], src(4 * half + t), ident)
                    last.then_inc(done, 1)

            def biased(dst, lhsT, rhs, col, n):
                pe.matmul(dst, ones3[:, :], brow[:, col:col + n], start=True, stop=False)
                return pe.matmul(dst, lhsT, rhs, start=False, stop=True)

            def routing_sums(i):
                pe.wait_ge(s("a0_mask"), i + 1)
                pos = banks[7][:, 256:256 + T * E].rearrange("p (t e) -> p t e", e=E)
                for t in tiles:
                    pe.matmul(pos[:, t, :], prefix16[:, :], mask16[:, t, :], start=(t == 0), stop=False,
                              skip_group_check=True)
                for t in range(T - 1):
                    pe.matmul(pos[:, t + 1:T, :], ones16[:, :],
                              mask16[:, t, :].unsqueeze(1).broadcast_to([P, T - 1 - t, E]),
                              start=False, stop=(t == T - 2), skip_group_check=True)
                for t in tiles:
                    last = pe.matmul(banks[7][:, 320:320 + E], ones16[:, :], mask16[:, t, :],
                                     start=(t == 0), stop=(t == T - 1), skip_group_check=True)
                last.then_inc(s("a0_pre"), 1)

            def experts(n):
                def flip(i, m):
                    k, u = use(i, m), m % 2
                    pe.wait_ge(s(f"b{n}_x{u}"), 16 * (k + 1))
                    wait_earlier(pe, s(f"b{n}_cols{u}"), k)
                    for a_ in range(ROWS // P):
                        last = pe.transpose(banks[u][:, P * a_:P * (a_ + 1)], XT[u][:, a_, :], ident)
                    last.then_inc(s(f"b{n}_xt{u}"), 1)

                def up(i, m):
                    k, u = use(i, m), m % 2
                    pe.wait_ge(s(f"b{n}_cols{u}"), k + 1)
                    pe.wait_ge(s(f"b{n}_w{m}"), 16 * (1 + n) * (i + 1))
                    wait_earlier(pe, s(f"b{n}_act{u}"), k * (1 + n))
                    for half in range(2):
                        hp = banks[2 + 2 * u + half][:, :].rearrange("p (c r) -> p c r", r=ROWS)
                        for c in range(2):
                            cc = 2 * half + c
                            last = pe.matmul(hp[:, c, :], WT[m][:, P * cc:P * (cc + 1)], XC[u], start=True, stop=True)
                        last.then_inc(s(f"b{n}_h{u}"), 1)

                def down(i, m):
                    k, u = use(i, m), m % 2
                    pe.wait_ge(s(f"b{n}_act{u}"), (k + 1) * (1 + n))
                    wait_earlier(pe, s(f"b{n}_ysb{u}"), k)
                    chunks = (2, 4)[n]
                    for a_ in range(ROWS // P):
                        for c in range(chunks):
                            rhs = WA2[:, c, :] if n == 0 else WT[m][:, FF + 4 + P * c:FF + 4 + P * (c + 1)]
                            last = pe.matmul(banks[6 + u][:, D * a_:D * (a_ + 1)],
                                             HT[u][:, c, P * a_:P * (a_ + 1)], rhs,
                                             start=(c == 0), stop=(c == chunks - 1))
                    last.then_inc(s(f"b{n}_y{u}"), 1)

                def pe_group(i, first, last):
                    if first:
                        flip(0, 0)
                    for m in range(UNROLL):
                        if not (last and m == UNROLL - 1):
                            flip(*after(i, m))
                        up(i, m)
                        if not (first and m == 0):
                            down(*before(i, m))
                    if last:
                        down(i, UNROLL - 1)

                every_group(pe, JOBS[n], pe_group)

            pe.wait_ge(s("const_in"), 16)
            pe.wait_ge(s("w_in"), 16 * 6)
            pe.wait_ge(s("bias_rows"), 48)
            pe.wait_ge(s("setup_done"), 1)
            def body(i, back, front):
                f = i + 1
                if back:
                    pe.wait_ge(s("a0_kvm"), i + 1)
                    for c, b in enumerate((5, 6, 2, 3)):
                        if c % 2 == 0:
                            pe.wait_ge(s("a0_qT"), 2 * i + c // 2 + 1)
                        for t in range(2):
                            last = pe.matmul(banks[b][:, 256 * t:256 * t + D + H],
                                             qT[:, P * (2 * c + t):P * (2 * c + t + 1)], kvm[:, :],
                                             start=True, stop=True)
                        last.then_inc(s("a0_num"), 1)
                    transposes(lambda t: y[:, t, :], 0, i, T // 2, s("a0_y"), s("a0_t3"))
                    for half in range(2):
                        pe.wait_ge(s("a0_yT"), 2 * i + half + 1)
                        for t in range(4):
                            k = 4 * half + t
                            last = biased(banks[2 + half][:, D * t:D * (t + 1)], qT[:, P * k:P * (k + 1)],
                                          WA[0][:, 3 * D:4 * D], R_O0, D)
                        last.then_inc(s("a0_o"), 1)
                    transposes(lambda t: xn2[:, t, :], 0, i, 2, s("a0_ln2"), s("a0_t4"))
                if front:
                    transposes(lambda t: xn[:, t, :], 5, f, 2, s("a0_ln1"), s("a0_t1"))
                if back:
                    for t in tiles:
                        if t % 4 == 0:
                            pe.wait_ge(s("a0_x2T"), 2 * i + t // 4 + 1)
                        last = pe.matmul(banks[7][:, E * t:E * (t + 1)], qT[:, P * t:P * (t + 1)], WG[0][:, :],
                                         start=True, stop=True)
                    last.then_inc(s("a0_gate"), 1)
                if not front:
                    routing_sums(i)
                    return
                pe.wait_ge(s("a0_xT"), 2 * f + 2)
                for t in tiles:
                    if t >= 2:
                        pe.wait_ge(s("a0_qsub"), T * f + t - 1)
                        pe.wait_ge(s("a0_v"), T * f + t - 1)
                    biased(banks[2 + t % 2][:, 0:3 * D], xnT[:, P * t:P * (t + 1)], WA[0][:, 0:3 * D],
                           R_QKV0, 3 * D).then_inc(s("a0_qkv"), 1)
                    if back and t == 5:
                        routing_sums(i)
                for half in range(2):
                    pe.wait_ge(s("a0_exp"), 2 * f + half + 1)
                    pe.wait_ge(s("a0_v"), T * f + 4 * half + 4)
                    for t in range(4 * half, 4 * half + 4):
                        last = pe.matmul(banks[4][:, 0:D + 1], qk[:, t, D:2 * D], val[:, t, :],
                                         start=(t == 0), stop=(t == T - 1))
                    if half == 1:
                        last.then_inc(s("a0_kv"), 1)
                    transposes(lambda t: qk[:, t, 0:D], 0, f, 2, s("a0_exp"), s("a0_t2"), [half])
            each_pair(pe, body)
            experts(0)
            def body(i):
                def step(r, stage):
                    def scores(i, t):
                        need(pe, s("a1_splitT"), i, t + 1, 2)
                        need(pe, s("a1_sqr"), i, t)
                        need(pe, s("a1_xT"), i, t + 5)
                        need(pe, s("a1_qT"), i, t + 1)
                        need(pe, s("a1_x2T"), i, t - 4)
                        need(pe, s("a1_scopy"), i, t - 6)
                        for g in range(4):
                            last = pe.matmul(banks[g][:, :], keysT[:, g, :],
                                             queriesT[:, g, :, :].rearrange("p h c -> p (h c)"),
                                             start=True, stop=True)
                        last.then_inc(s("a1_qk"), 1)

                    def mix(i, t):
                        need(pe, s("a1_x1"), i, t)
                        need(pe, s("a1_mask"), i, t + 1)
                        need(pe, s("a1_feat"), i, t + 1)
                        if t > 0:
                            wait_earlier(pe, s("a1_state"), (T - 1) * i + t)
                        for hh in range(4):
                            for g in range(4):
                                last = pe.matmul(banks[6][32 * g:32 * g + 32, 0:P], vpad[:, t, g, 32 * hh:32 * hh + 32],
                                                 score[:, t % 2, g, hh, :], start=(hh == 0),
                                                 stop=(t == 0 and hh == 3), skip_group_check=True)
                        for d in range(NDIFF if t > 0 else 0):
                            for g in range(4):
                                own = slice(32 * g, 32 * g + 32)
                                last = pe.matmul(banks[6][own, 0:P], state[own, d, :], feats[t % 4][own, d, :],
                                                 start=False, stop=(d == NDIFF - 1), skip_group_check=True)
                        last.then_inc(s("a1_z"), 1)

                    def add_state(i, t):
                        if t == T - 1:
                            return
                        need(pe, s("a1_prod"), i, t + 1)
                        wait_earlier(pe, s("a1_state"), (T - 1) * i + t)
                        for d in range(NDIFF):
                            for g in range(4):
                                last = pe.matmul(banks[7][32 * g:32 * g + 32, 32 * d:32 * d + 32],
                                                 prods[t % 4][:, d, 32 * g:32 * g + 32],
                                                 values_of(t)[:, g, :, :],
                                                 start=(t == 0 and d == 0), stop=True, skip_group_check=True)
                        last.then_inc(s("a1_st"), 1)

                    def qkv(i, t):
                        need(pe, s("a1_xT"), i, t + 1)
                        need(pe, s("a1_splitT"), i, t - 4, 2, 1)
                        biased(banks[4][:, 0:3 * D], x1T[:, t, :], WA[1][:, 0:3 * D], R_QKV1, 3 * D)\
                            .then_inc(s("a1_qkv"), 1)

                    def shifts(i, t):
                        need(pe, s("a1_qT"), i, t + 1)
                        need(pe, s("a1_splitT"), i, t + 1, 2)
                        for d in range(1, NDIFF):
                            last = pe.matmul(banks[5][:, P * (d - 1):P * d],
                                             K[:, C_SHIFT + P * (d - 1):C_SHIFT + P * d], qT1[:, t % 2, :],
                                             start=True, stop=True)
                        last.then_inc(s("a1_ph"), 1)

                    def project(i, t):
                        need(pe, s("a1_zT"), i, t + 1)
                        need(pe, s("a1_gcopy"), i, t - 2)
                        pe.matmul(banks[6][:, P:2 * P], x1T[:, t, :], ident, start=True, stop=False)
                        pe.matmul(banks[6][:, P:2 * P], zT[:, :], WA[1][:, 3 * D:4 * D], start=False, stop=True)\
                            .then_inc(s("a1_o"), 1)

                    def flip_x1(i, t):
                        need(pe, s("a1_ln1"), i, t + 1)
                        need(pe, s("a1_sqr"), i, t - 4)
                        pe.transpose(banks[2][:, 0:P], xn[:, t, :], ident).then_inc(s("a1_t1"), 1)

                    def flip_q(i, t):
                        need(pe, s("a1_rope"), i, t + 1)
                        need(pe, s("a1_sqr"), i, t)
                        pe.transpose(banks[3][:, 0:P], qk[:, t, 0:D], ident).then_inc(s("a1_plain"), 1)

                    def flip_split(i, t):
                        need(pe, s("a1_split"), i, t + 1)
                        for side in range(2):
                            if side == 0:
                                need(pe, s("a1_qv"), i, t + 4)
                            else:
                                need(pe, s("a1_feat"), i, t)
                            for g in range(4):
                                last = pe.transpose(banks[4 + side][:, P * g:P * (g + 1)],
                                                    split[:, side, 4 * g:4 * g + 4, :, :]
                                                    .rearrange("p h c d -> p (h c d)").bitcast(fp32), ident)
                            last.then_inc(s("a1_splitT_ps"), 1)

                    stage(-2, project)
                    stage(1, flip_split)
                    stage(5, flip_x1)
                    stage(1, flip_q)
                    stage(-4, flip_x2)
                    stage(-6, sums)
                    stage(-1, add_state)
                    stage(-1, mix)
                    stage(5, qkv)
                    stage(-4, gates)
                    stage(1, shifts)
                    stage(1, scores)

                def sums(i, t):
                    need(pe, s("a1_mask2"), i, t + 1)
                    need(pe, s("a1_scopy"), i, t)
                    need(pe, s("a1_sqr"), i, t + 7)
                    pe.matmul(banks[1][:, 0:E], prefix16[:, :], mask16[:, t, :], start=True, stop=True)
                    pe.matmul(banks[1][:, E:2 * E], ones16[:, :], mask16[:, t, :], start=True, stop=True)\
                        .then_inc(s("a1_sums"), 1)

                def flip_x2(i, t):
                    need(pe, s("a1_ln2"), i, t + 1)
                    need(pe, s("a1_sqr"), i, t + 5)
                    pe.transpose(banks[0][:, 0:P], xn2[:, t, :], ident).then_inc(s("a1_t4"), 1)

                def gates(i, t):
                    need(pe, s("a1_x2T"), i, t + 1)
                    need(pe, s("a1_zT"), i, t + 4)
                    need(pe, s("a1_x1"), i, t + 3)
                    biased(banks[6][:, 2 * P:2 * P + E], x2T[:, :], WG[1][:, :], R_GATE, E).then_inc(s("a1_gate"), 1)

                stream(i, step)
            each_body(pe, body)
            pe.wait_ge(s("a1_scopy"), TOKENS // P)
            experts(1)


def constants():
    import numpy as np
    f = np.float32
    p = np.arange(P)
    same = (p[:, None] // DH == p[None, :] // DH).astype(f)
    eye = np.eye(P, dtype=f)
    same32 = (p[:, None] % 32 // DH == np.arange(32)[None, :] // DH).astype(f)
    state = [same32 / DH ** 2] * (NDIFF - 1) + [same32 / (2 * DH ** 2)]
    head = p // DH * DH
    shift = [eye + (p[:, None] == (head + (p + d) % DH)[None, :]) for d in range(1, NDIFF)]
    inv = f(1.0) / f(10000.0) ** (np.arange(0, DH, 2, dtype=f) / f(DH))
    angle = np.outer(np.arange(SEQ, dtype=f), inv).astype(f)
    angle = np.concatenate([angle, angle], -1).reshape(T, P, DH).transpose(1, 0, 2)
    sign = np.where(np.arange(DH) % 2 == 0, -1.0, 1.0).astype(f)

    def rows(a):
        return np.broadcast_to(np.asarray(a, f), (P, len(a)))

    parts = [eye, same, (p[:, None] < p[None, :]).astype(f), *state, *shift,
             (p[:, None] // DH == np.arange(H)[None, :]).astype(f),
             rows(E - np.arange(E)), rows(np.arange(E) * REGION),
             rows(np.arange(E)),
             np.cos(angle).reshape(P, T * DH), (np.sin(angle) * sign).reshape(P, T * DH),
             rows(np.arange(ROUTED))]
    return np.ascontiguousarray(np.concatenate(parts, 1), dtype=f)


def kernel(**inputs):
    import numpy as np
    import concourse.bacc as bacc
    from concourse.bass_utils import run_bass_kernel_spmd

    w = {k: np.asarray(v) for k, v in inputs.items()}
    cat = np.concatenate

    def attn(layer):
        return cat([w[f"L{layer}_attn_W{m}"].T for m in "qkvo"], 1)

    def columns(b):
        return b.reshape(-1, FF // P, P).transpose(0, 2, 1)

    w1 = cat([w["L1_ffn_spec_w1"], w["L1_ffn_shared_w1"][None]])
    b1 = cat([w["L1_ffn_spec_b1"], w["L1_ffn_shared_b1"][None]])
    w2 = cat([w["L1_ffn_spec_w2"], w["L1_ffn_shared_w2"][None]])
    laid = {
        "x_in": w["L0_attn_x"].reshape(TOKENS, D),
        "consts": constants(),
        "bias_row": cat([w["L0_attn_bq"], w["L0_attn_bk"], w["L0_attn_bv"], w["L0_attn_bo"],
                         w["L1_attn_bq"], w["L1_attn_bk"], w["L1_attn_bv"], w["L1_ffn_router_b"]])[None],
        "w_attn0": attn(0),
        "w_attn1": attn(1),
        "w_gate": np.stack([w["L0_ffn_Wg"].T, w["L1_ffn_router_w"].T]),
        "w_out0": w["L0_ffn_Wo"].T,
        "w_exp0": cat([w["L0_ffn_W1"].transpose(0, 2, 1), columns(w["L0_ffn_b1"])], 2),
        "w_exp1": cat([w1.transpose(0, 2, 1), columns(b1),
                       w2.reshape(E + 1, D, FF // P, P).transpose(0, 3, 2, 1).reshape(E + 1, P, FF)], 2),
        "b_out0": w["L0_ffn_bo"],
        "b_out1": cat([w["L1_ffn_spec_b2"], w["L1_ffn_shared_b2"][None]]),
        "norm_w": w["L1_attn_norm_w"],
    }
    nc = bacc.Bacc("TRN2", target_bir_lowering=False, num_devices=1)
    arrays, args = {}, []
    for name, a in laid.items():
        arrays[name] = np.ascontiguousarray(a)
        args.append(nc.dram_tensor(name, a.shape, mybir.dt.from_np(a.dtype), kind="ExternalInput").ap())
    fp32 = mybir.dt.float32
    out = nc.dram_tensor("out", (TOKENS, D), fp32, kind="ExternalOutput").ap()
    xs = [nc.dram_tensor(f"xs{n}", (DUMMY + ROWS + n * TOKENS, D), fp32, kind="Internal").ap() for n in range(2)]
    ys = [nc.dram_tensor(f"ys{n}", ((ROUTED + n * SHARED) * ROWS, D), fp32, kind="Internal").ap() for n in range(2)]
    program(nc, *args, out, xs, ys)
    r = run_bass_kernel_spmd(nc, [arrays], core_ids=[0])
    return r.results[0]["out"].reshape(SEQS, SEQ, D)
```
